# Optimizing a Trainium2 kernel written in Bass

```python
import numpy as np
import jax
import jax.numpy as jnp

def _softmax(x, axis=-1):
    return jax.nn.softmax(x, axis=axis)

def _gelu(x):
    return jax.nn.gelu(x, approximate=True)

def _silu(x):
    return jax.nn.silu(x)

def _sigmoid(x):
    return jax.nn.sigmoid(x)

def _layernorm(x, axis=-1, eps=1e-05):
    m = jnp.mean(x, axis=axis, keepdims=True)
    v = jnp.var(x, axis=axis, keepdims=True)
    return (x - m) / jnp.sqrt(v + eps)

def _scatter_add(tgt, idx, src, axis=0):
    return tgt.at[idx].add(src)

def _segment_sum(src, seg, n):
    return jax.ops.segment_sum(src, seg, n)
kernel_name = 'mk_recurrent_d2_jaxref_r8_2d42fd'

def setup_inputs(seed: int=0):
    np.random.seed(seed)
    _w = jnp.asarray

    def _L0_attn_setup():
        import jax, jax.numpy as jnp
        import numpy as np
        D_ATT_IN = 128
        NUM_HEADS = 16
        D_Q = 64
        D_V = 64
        D_MODEL = 128

        def _trunc_normal(key, shape, std):
            return jax.random.truncated_normal(key, -3.0, 3.0, shape, dtype=jnp.float32) * std
        key = jax.random.key(seed)
        k_x, k_q, k_k, k_v, k_o = jax.random.split(key, 5)

        def init_w(k, out_f, in_f):
            s = np.sqrt(2.0 / (in_f + out_f))
            return _trunc_normal(k, (out_f, in_f), s)
        return {'in_features': jax.random.normal(k_x, (4, 256, D_ATT_IN), dtype=jnp.float32), 'w_q': init_w(k_q, NUM_HEADS * D_Q, D_ATT_IN), 'w_k': init_w(k_k, NUM_HEADS * D_Q, D_ATT_IN), 'w_v': init_w(k_v, NUM_HEADS * D_V, D_ATT_IN), 'w_o': init_w(k_o, D_MODEL, NUM_HEADS * D_V)}
    _L0_attn_in = _L0_attn_setup()

    def _L0_ffn_setup():
        import jax, jax.numpy as jnp
        import numpy as np
        B, S, D_MODEL, D_FF, E, R, TOP_K = (4, 256, 128, 512, 8, 16, 2)
        key = jax.random.key(seed)
        ks = jax.random.split(key, 9)
        sd = 1.0 / np.sqrt(D_MODEL)
        return {'hidden_states': jax.random.normal(ks[0], (B, S, D_MODEL), jnp.float32), 'wi': jax.random.normal(ks[1], (D_FF, D_MODEL), jnp.float32) * sd, 'bi': jax.random.normal(ks[2], (D_FF,), jnp.float32) * 0.01, 'wo': jax.random.normal(ks[3], (D_MODEL, D_FF), jnp.float32) * (1.0 / np.sqrt(D_FF)), 'bo': jax.random.normal(ks[4], (D_MODEL,), jnp.float32) * 0.01, 'lora_A': jax.random.normal(ks[5], (E, R, D_MODEL), jnp.float32) * sd, 'lora_B': jax.random.normal(ks[6], (E, D_FF, R), jnp.float32) * 0.02, 'gate_w': jax.random.normal(ks[7], (E, D_MODEL), jnp.float32) * sd, 'gate_b': jax.random.normal(ks[8], (E,), jnp.float32) * 0.01}
    _L0_ffn_in = _L0_ffn_setup()

    def _L1_attn_setup():
        import jax, jax.numpy as jnp
        import numpy as np
        D_MODEL = 128
        NUM_HEADS = 16
        D_HEAD = D_MODEL // NUM_HEADS
        LAMBDA_INIT = 0.8
        EPS = 1e-05
        B, N = (4, 128)
        key = jax.random.key(seed)
        ks = jax.random.split(key, 10)
        w_scale = 1.0 / np.sqrt(D_MODEL)
        d2 = 2 * D_HEAD * NUM_HEADS
        return {'X': jax.random.normal(ks[0], (B, N, D_MODEL), jnp.float32), 'Wq': jax.random.normal(ks[1], (d2, D_MODEL), jnp.float32) * w_scale, 'Wk': jax.random.normal(ks[2], (d2, D_MODEL), jnp.float32) * w_scale, 'Wv': jax.random.normal(ks[3], (d2, D_MODEL), jnp.float32) * w_scale, 'Wo': jax.random.normal(ks[4], (D_MODEL, d2), jnp.float32) * w_scale, 'lq1': jax.random.normal(ks[5], (NUM_HEADS, D_HEAD), jnp.float32), 'lk1': jax.random.normal(ks[6], (NUM_HEADS, D_HEAD), jnp.float32), 'lq2': jax.random.normal(ks[7], (NUM_HEADS, D_HEAD), jnp.float32), 'lk2': jax.random.normal(ks[8], (NUM_HEADS, D_HEAD), jnp.float32), 'rms_scale': jnp.ones((2 * D_HEAD,), jnp.float32)}
    _L1_attn_in = _L1_attn_setup()

    def _L1_ffn_setup():
        import jax, jax.numpy as jnp
        import numpy as np
        H, I, E, K = (128, 64, 32, 8)
        B, S = (4, 128)

        def silu(x):
            return x * jax.nn.sigmoid(x)
        key = jax.random.key(seed)
        ks = jax.random.split(key, 14)

        def w(k, shape, fan_in):
            return jax.random.normal(k, shape, jnp.float32) / np.float32(np.sqrt(fan_in))
        return {'hidden_states': jax.random.normal(ks[0], (B, S, H), jnp.float32), 'Wr': w(ks[1], (H, E), H), 'br': jnp.zeros((E,), jnp.float32), 'Wg_s': w(ks[2], (H, I), H), 'bg_s': jnp.zeros((I,), jnp.float32), 'Wu_s': w(ks[3], (H, I), H), 'bu_s': jnp.zeros((I,), jnp.float32), 'Wd_s': w(ks[4], (I, H), I), 'bd_s': jnp.zeros((H,), jnp.float32), 'Wg': w(ks[5], (E, H, I), H), 'bg': jnp.zeros((E, I), jnp.float32), 'Wu': w(ks[6], (E, H, I), H), 'bu': jnp.zeros((E, I), jnp.float32), 'Wd': w(ks[7], (E, I, H), I), 'bd': jnp.zeros((E, H), jnp.float32)}
    _L1_ffn_in = _L1_ffn_setup()
    _d = {'L0_attn_in_features': _L0_attn_in['in_features'], 'L0_attn_w_q': _L0_attn_in['w_q'], 'L0_attn_w_k': _L0_attn_in['w_k'], 'L0_attn_w_v': _L0_attn_in['w_v'], 'L0_attn_w_o': _L0_attn_in['w_o'], 'L0_ffn_wi': _L0_ffn_in['wi'], 'L0_ffn_bi': _L0_ffn_in['bi'], 'L0_ffn_wo': _L0_ffn_in['wo'], 'L0_ffn_bo': _L0_ffn_in['bo'], 'L0_ffn_lora_A': _L0_ffn_in['lora_A'], 'L0_ffn_lora_B': _L0_ffn_in['lora_B'], 'L0_ffn_gate_w': _L0_ffn_in['gate_w'], 'L0_ffn_gate_b': _L0_ffn_in['gate_b'], 'L1_attn_Wq': _L1_attn_in['Wq'], 'L1_attn_Wk': _L1_attn_in['Wk'], 'L1_attn_Wv': _L1_attn_in['Wv'], 'L1_attn_Wo': _L1_attn_in['Wo'], 'L1_attn_lq1': _L1_attn_in['lq1'], 'L1_attn_lk1': _L1_attn_in['lk1'], 'L1_attn_lq2': _L1_attn_in['lq2'], 'L1_attn_lk2': _L1_attn_in['lk2'], 'L1_attn_rms_scale': _L1_attn_in['rms_scale'], 'L1_ffn_Wr': _L1_ffn_in['Wr'], 'L1_ffn_br': _L1_ffn_in['br'], 'L1_ffn_Wg_s': _L1_ffn_in['Wg_s'], 'L1_ffn_bg_s': _L1_ffn_in['bg_s'], 'L1_ffn_Wu_s': _L1_ffn_in['Wu_s'], 'L1_ffn_bu_s': _L1_ffn_in['bu_s'], 'L1_ffn_Wd_s': _L1_ffn_in['Wd_s'], 'L1_ffn_bd_s': _L1_ffn_in['bd_s'], 'L1_ffn_Wg': _L1_ffn_in['Wg'], 'L1_ffn_bg': _L1_ffn_in['bg'], 'L1_ffn_Wu': _L1_ffn_in['Wu'], 'L1_ffn_bu': _L1_ffn_in['bu'], 'L1_ffn_Wd': _L1_ffn_in['Wd'], 'L1_ffn_bd': _L1_ffn_in['bd']}
    _x0 = _d['L0_attn_in_features']
    _d['L0_attn_in_features'] = jax.random.normal(jax.random.fold_in(jax.random.key(seed), 1), (8, 256, 128), dtype=_x0.dtype)
    del _x0
    return _d

def reference(L0_attn_in_features, L0_attn_w_q, L0_attn_w_k, L0_attn_w_v, L0_attn_w_o, L0_ffn_wi, L0_ffn_bi, L0_ffn_wo, L0_ffn_bo, L0_ffn_lora_A, L0_ffn_lora_B, L0_ffn_gate_w, L0_ffn_gate_b, L1_attn_Wq, L1_attn_Wk, L1_attn_Wv, L1_attn_Wo, L1_attn_lq1, L1_attn_lk1, L1_attn_lq2, L1_attn_lk2, L1_attn_rms_scale, L1_ffn_Wr, L1_ffn_br, L1_ffn_Wg_s, L1_ffn_bg_s, L1_ffn_Wu_s, L1_ffn_bu_s, L1_ffn_Wd_s, L1_ffn_bd_s, L1_ffn_Wg, L1_ffn_bg, L1_ffn_Wu, L1_ffn_bu, L1_ffn_Wd, L1_ffn_bd):

    def _L0_attn_ref(in_features, w_q, w_k, w_v, w_o):
        import jax, jax.numpy as jnp
        import numpy as np
        D_ATT_IN = 128
        NUM_HEADS = 16
        D_Q = 64
        D_V = 64
        D_MODEL = 128

        def _trunc_normal(key, shape, std):
            return jax.random.truncated_normal(key, -3.0, 3.0, shape, dtype=jnp.float32) * std
        q = jnp.einsum('oi,bsi->bso', w_q, in_features)
        k = jnp.einsum('oi,bsi->bso', w_k, in_features)
        v = jnp.einsum('oi,bsi->bso', w_v, in_features)
        s = in_features.shape[-2]
        scores = jnp.einsum('bqd,bkd->bqk', q, k) / jnp.sqrt(jnp.asarray(k.shape[-1], q.dtype))
        causal = jnp.tril(jnp.ones((s, s), dtype=bool))
        scores = jnp.where(causal[None, :, :], scores, -jnp.inf)
        att = jax.nn.softmax(scores, axis=-1)
        ctx = jnp.einsum('bqk,bkd->bqd', att, v)
        return jnp.einsum('oi,bsi->bso', w_o, ctx)

    def _L0_ffn_ref(hidden_states, wi, bi, wo, bo, lora_A, lora_B, gate_w, gate_b):
        import jax, jax.numpy as jnp
        import numpy as np
        B, S, D_MODEL, D_FF, E, R, TOP_K = (4, 256, 128, 512, 8, 16, 2)
        logits = jnp.einsum('bsd,ed->bse', hidden_states, gate_w) + gate_b
        scores = jax.nn.softmax(logits, axis=-1)
        top_v, top_i = jax.lax.top_k(scores, TOP_K)
        val_sum = top_v.sum(axis=-1)
        out = jnp.zeros_like(hidden_states)
        for e in range(E):
            count = (top_i == e).sum(axis=-1).astype(hidden_states.dtype)
            gate = count * val_sum
            inter = jnp.einsum('bsd,fd->bsf', hidden_states, wi) + bi + jnp.einsum('bsr,fr->bsf', jnp.einsum('bsd,rd->bsr', hidden_states, lora_A[e]), lora_B[e])
            h = jax.nn.relu(inter)
            expert_out = jnp.einsum('bsf,df->bsd', h, wo) + bo
            out = out + gate[..., None] * expert_out
        return out

    def _L1_attn_ref(X, Wq, Wk, Wv, Wo, lq1, lk1, lq2, lk2, rms_scale):
        import jax, jax.numpy as jnp
        import numpy as np
        D_MODEL = 128
        NUM_HEADS = 16
        D_HEAD = D_MODEL // NUM_HEADS
        LAMBDA_INIT = 0.8
        EPS = 1e-05
        B, N = (4, 128)
        b, n, _ = X.shape
        H, dh = (NUM_HEADS, D_HEAD)

        def proj(W):
            return (X @ W.T).reshape(b, n, H, 2 * dh).transpose(0, 2, 1, 3)
        Q, K, V = (proj(Wq), proj(Wk), proj(Wv))
        Q1, Q2 = jnp.split(Q, 2, axis=-1)
        K1, K2 = jnp.split(K, 2, axis=-1)
        lam = jnp.exp(jnp.sum(lq1 * lk1, axis=-1)) - jnp.exp(jnp.sum(lq2 * lk2, axis=-1)) + LAMBDA_INIT
        lam = lam[None, :, None, None]
        scaling = 1.0 / np.sqrt(dh)
        causal = jnp.tril(jnp.ones((n, n), bool))
        A1 = jnp.where(causal, jnp.einsum('bhnd,bhmd->bhnm', Q1, K1) * scaling, -jnp.inf)
        A2 = jnp.where(causal, jnp.einsum('bhnd,bhmd->bhnm', Q2, K2) * scaling, -jnp.inf)
        attn = jax.nn.softmax(A1, axis=-1) - lam * jax.nn.softmax(A2, axis=-1)
        O = jnp.einsum('bhnm,bhmd->bhnd', attn, V)
        rms = jnp.sqrt(jnp.mean(O * O, axis=-1, keepdims=True) + EPS)
        O = O / rms * rms_scale * (1.0 - LAMBDA_INIT)
        Oc = O.transpose(0, 2, 1, 3).reshape(b, n, H * 2 * dh)
        return Oc @ Wo.T

    def _L1_ffn_ref(hidden_states, Wr, br, Wg_s, bg_s, Wu_s, bu_s, Wd_s, bd_s, Wg, bg, Wu, bu, Wd, bd):
        import jax, jax.numpy as jnp
        import numpy as np
        H, I, E, K = (128, 64, 32, 8)
        B, S = (4, 128)

        def silu(x):
            return x * jax.nn.sigmoid(x)
        b, s, h = hidden_states.shape
        T = b * s
        x = hidden_states.reshape(T, h)
        logits = jnp.dot(x.astype(jnp.float32), Wr) + br
        aff = jax.nn.sigmoid(logits)
        top_v, top_i = jax.lax.top_k(aff, K)
        top_w = top_v / (jnp.sum(top_v, axis=-1, keepdims=True) + 1e-09)
        top_w = top_w.astype(hidden_states.dtype)
        e_total = Wr.shape[1]
        w_full = jnp.zeros((T, e_total), hidden_states.dtype)
        w_full = w_full.at[jnp.arange(T)[:, None], top_i].set(top_w)
        shared = jnp.dot(silu(jnp.dot(x, Wg_s) + bg_s) * (jnp.dot(x, Wu_s) + bu_s), Wd_s) + bd_s
        gate = silu(jnp.einsum('th,ehi->eti', x, Wg) + bg[:, None, :])
        up = jnp.einsum('th,ehi->eti', x, Wu) + bu[:, None, :]
        down = jnp.einsum('eti,eih->eth', gate * up, Wd) + bd[:, None, :]
        routed = jnp.einsum('te,eth->th', w_full, down)
        return (shared + routed).reshape(b, s, h)
    x = L0_attn_in_features
    xn = _layernorm(x, axis=-1)
    s = _L0_attn_ref(xn, L0_attn_w_q, L0_attn_w_k, L0_attn_w_v, L0_attn_w_o)
    g = _silu(_L0_ffn_ref(xn, L0_ffn_wi, L0_ffn_bi, L0_ffn_wo, L0_ffn_bo, L0_ffn_lora_A, L0_ffn_lora_B, L0_ffn_gate_w, L0_ffn_gate_b))
    x = x + s * g
    xn = _layernorm(x, axis=-1)
    s = _L1_attn_ref(xn, L1_attn_Wq, L1_attn_Wk, L1_attn_Wv, L1_attn_Wo, L1_attn_lq1, L1_attn_lk1, L1_attn_lq2, L1_attn_lk2, L1_attn_rms_scale)
    g = _silu(_L1_ffn_ref(xn, L1_ffn_Wr, L1_ffn_br, L1_ffn_Wg_s, L1_ffn_bg_s, L1_ffn_Wu_s, L1_ffn_bu_s, L1_ffn_Wd_s, L1_ffn_bd_s, L1_ffn_Wg, L1_ffn_bg, L1_ffn_Wu, L1_ffn_bu, L1_ffn_Wd, L1_ffn_bd))
    x = x + s * g
    return x

_drawn_inputs = setup_inputs


def setup_inputs(seed=0):
    import zlib

    import numpy as np

    out = dict(_drawn_inputs(seed))
    spreads = {'L1_attn_rms_scale': (1.0, 0.6),
     'L1_ffn_br': (0.0, 0.8),
     'L1_ffn_bg_s': (0.0, 0.723),
     'L1_ffn_bu_s': (0.0, 0.8),
     'L1_ffn_bd_s': (0.0, 0.518),
     'L1_ffn_bg': (0.0, 2.0),
     'L1_ffn_bu': (0.0, 2.0),
     'L1_ffn_bd': (0.0, 2.0)}
    factors = {'L0_attn_w_q': 5.29,
     'L0_attn_w_k': 5.086,
     'L0_ffn_bi': 28.92,
     'L0_ffn_bo': 8.0,
     'L0_ffn_lora_A': 8.0,
     'L0_ffn_lora_B': 8.0,
     'L0_ffn_gate_w': 4.731,
     'L0_ffn_gate_b': 8.0}
    for name, (base, spread) in spreads.items():
        noise = np.random.default_rng([zlib.crc32(name.encode()), seed]).standard_normal(out[name].shape)
        drawn = base * np.exp(spread * noise) if base else spread * noise
        out[name] = jnp.asarray(drawn.astype(out[name].dtype))
    for name, factor in factors.items():
        out[name] = (out[name] * factor).astype(out[name].dtype)
    return out
```

```python
from contextlib import ExitStack

import numpy as np

import concourse.bass as bass
from concourse import mybir

ALU = mybir.AluOpType
ACT = mybir.ActivationFunctionType
F32 = mybir.dt.float32
BF16 = mybir.dt.bfloat16
U32 = mybir.dt.uint32
AX = mybir.AxisListType.X

P = 128
D = 128
BATCHES, SEQ = 8, 256
CHUNK = 512
CB = CHUNK // SEQ
TILES = CHUNK // P
CHUNKS = BATCHES * SEQ // CHUNK
EPS = 1e-5
MASKED = -1e30

OT = 1024 // P
E0, R0 = 8, 16
FB = 512 // P
SCALE0 = 1.0 / 32.0

HEADS, DH = 16, 8
HC = 2 * HEADS
DV = 2 * DH
HR = 3
VW1 = 32
SCALE1 = 1.0 / float(np.sqrt(DH))
SLOTS = 6
NEG_ROW = 96
KROWS = NEG_ROW + 3
LAM0 = 0.8
GROUPS = 4
GH = HEADS // GROUPS
GHC = 2 * GH
E1, INNER = 32, 64
PAIRS = E1 // 2
TOPK = 8

MAX_UNITS = 3 * GROUPS


def plan_layer1():
    moe = [("moe", j) for j in range(PAIRS + 3)]
    steps = moe[:5]
    rest = moe[5:]
    attention = []
    for b in range(CB):
        attention += [("max", b, g, u) for g in range(GROUPS) for u in range(3)] + [("minus", b)]
        attention += [("attend", b, g) for g in range(GROUPS)] + [("norm", b)]
    n = len(attention)
    for k, s in enumerate(attention):
        steps.append(s)
        while rest and (len(moe) - 5 - len(rest)) * n < (k + 1) * (len(moe) - 5):
            steps.append(rest.pop(0))
    return steps + rest


PLAN = plan_layer1()
N_WEIGHTS = 20 + 4 + 2 + 4 + P // DV
N_CONSTS = 10
WB_IN = 32 * PAIRS // 4
QK_IN = 16 * 2 * SLOTS
N_SETUP_VEC = 11
SETUP_LINKS = 4
DVE_LINKS = 86


def build(nc, t):
    with ExitStack() as ctx:
        def sb(name, shape, dt=F32):
            return ctx.enter_context(nc.sbuf_tensor(name, shape, dt))

        def sem(name):
            return ctx.enter_context(nc.semaphore(name))

        pairs = [ctx.enter_context(nc.psum_tensor(f"scores{n}", [P, 2, 512], F32)) for n in range(2)]
        single = [ctx.enter_context(nc.psum_tensor(f"bank{n}", [P, 512], F32)) for n in range(4, 8)]
        bank = [pairs[0][:, 0, :], pairs[0][:, 1, :], pairs[1][:, 0, :], pairs[1][:, 1, :]] + [s[:, :] for s in single]

        ident = sb("ident", [P, P])
        identb = sb("identb", [P, P], BF16)
        mask_q = sb("mask_q", [P, 4, P], BF16)
        mask_k = sb("mask_k", [P, 4, P], BF16)
        twos_row = sb("twos_row", [1, P])
        minus_half = sb("minus_half", [P, HC])
        waited = sb("waited", [P, 2])
        iota8 = sb("iota8", [P, E0])
        mt = sb("mt", [P, P])
        vo = sb("vo", [P, P])
        wi_t = sb("wi_t", [P, 512])
        bi = sb("bi", [P, FB])
        wo_t = sb("wo_t", [P, FB, P])
        bo = sb("bo", [1, P])
        la = sb("la", [P, E0 * R0])
        lb = sb("lb", [P, 512])
        gate_w = sb("gate_w", [P, E0])
        gate_b = sb("gate_b", [P, E0])
        wq1 = sb("wq1", [P, 2 * P])
        wk1 = sb("wk1", [P, 2 * P])
        wv1 = sb("wv1", [P, 2 * P])
        wo1 = sb("wo1", [P, 2, P])
        wo1s = sb("wo1s", [P, 2, P])
        rms_col = sb("rms_col", [P, 1])
        lam_in = sb("lam_in", [P, 4, HEADS * DH])
        lam_e = sb("lam_e", [P, 2, HEADS])
        lam = sb("lam", [P, HEADS])
        wr = sb("wr", [P, E1])
        br = sb("br", [P, E1])
        wg = sb("wg", [P, E1 * INNER])
        wu = sb("wu", [P, E1 * INNER])
        wd = sb("wd", [P, PAIRS, P])
        bd = sb("bd", [E1, P])
        bg = sb("bg", [P, PAIRS + 1])
        bgh = sb("bgh", [P, PAIRS + 1])
        bu = sb("bu", [P, PAIRS + 1])
        wgs = sb("wgs", [P, INNER])
        wus = sb("wus", [P, INNER])
        wds = sb("wds", [INNER, P])
        bds = sb("bds", [P, 1])
        bdsh = sb("bdsh", [P, 1])

        x = sb("x", [P, TILES, D])
        stats = sb("stats", [P, TILES, 6])
        mv = sb("mv", [P, TILES, 2])
        vare = sb("vare", [P, TILES])
        rstd = sb("rstd", [P, TILES])
        xn = sb("xn", [P, TILES, D])
        xnt = sb("xnt", [P, CHUNK])
        yk = sb("yk", [P, CHUNK])
        vw = sb("vw", [P, TILES, D])
        nmax0 = sb("nmax0", [P, TILES])
        nbias0 = sb("nbias0", [P, TILES])
        p0 = sb("p0", [P, TILES, SEQ])
        l0 = sb("l0", [P, TILES])
        rl0 = sb("rl0", [P, TILES])
        pt0 = sb("pt0", [P, CB, 3 * P])
        logit = sb("logit", [P, TILES, E0])
        lmax = sb("lmax", [P, TILES])
        lexp = sb("lexp", [P, TILES, E0])
        lsum = sb("lsum", [P, TILES])
        top = sb("top", [P, TILES, 8])
        topi = sb("topi", [P, TILES, 8], U32)
        topf = sb("topf", [P, TILES, 2])
        pick = sb("pick", [P, 2, TILES, E0])
        hvs = sb("hvs", [P, TILES])
        um = sb("um", [P, 2, TILES, E0 * R0])
        umt = sb("umt", [P, 2, CHUNK])
        ha = sb("ha", [P, FB, CHUNK])
        hb = sb("hb", [P, 2, CHUNK])
        th0 = xn
        tmp0 = sb("tmp0", [P, TILES, D])
        gate0 = sb("gate0", [P, TILES, D])
        x1 = sb("x1", [P, TILES, D])

        xn1 = sb("xn1", [P, TILES, D])
        xnt1 = sb("xnt1", [P, CHUNK])
        rlog = sb("rlog", [P, TILES, E1])
        rexp = sb("rexp", [P, TILES, E1])
        aff = sb("aff", [P, TILES, E1])
        top1 = sb("top1", [P, TILES, 8])
        rest1 = sb("rest1", [P, TILES, E1])
        wsum = sb("wsum", [P, TILES])
        wtok = sb("wtok", [P, TILES, E1])
        wt = sb("wt", [E1, CHUNK])
        wb = sb("wb", [P, 2, 2, CHUNK])
        qkf = sb("qkf", [P, 4, CHUNK])
        parts = sb("parts", [P, 3, 4, CHUNK], BF16)
        qa = sb("qa", [KROWS, HC, SEQ], BF16)
        ka = sb("ka", [KROWS, HC, SEQ], BF16)
        v1 = sb("v1", [P, TILES, HEADS, VW1])
        nmax1 = sb("nmax1", [P, TILES, HC])
        mres = sb("mres", [P, TILES, HC])
        mparts = sb("mparts", [P, TILES, 3, HC], BF16)
        mrows = sb("mrows", [3 * HC, CHUNK], BF16)
        room = parts[:, :, :, :].rearrange("p a f t -> p (a f t)").bitcast(F32)
        pk0 = room[:, 0:GHC * SEQ].rearrange("p (h q) -> p h q", q=SEQ)
        pk1 = room[:, GHC * SEQ:GHC * (SEQ + P)].rearrange("p (h q) -> p h q", q=P)
        ot = sb("ot", [P, 2, SEQ])
        rl1 = sb("rl1", [P, 2, 2, GH])
        o12 = sb("o12", [P, 2, 2, GH, DV])
        oc = sb("oc", [P, TILES, HEADS * DV])
        osq = sb("osq", [P, 2, HEADS * DV])
        oms = sb("oms", [P, 2, HEADS])
        orms = sb("orms", [P, 2, HEADS])
        on = sb("on", [P, 2, HEADS * DV])
        oct_ = sb("oct", [P, 2, CHUNK])
        gt = sb("gt", [P, 2, CHUNK])
        gb = sb("gb", [P, 2, CHUNK])
        h1 = sb("h1", [P, HR, CHUNK])
        wstack = ha[:, :, :].rearrange("p f t -> p (f t)").rearrange("p (a c) -> p a c", a=2)
        fth = sb("fth", [P, CHUNK])
        fvh = sb("fvh", [P, CHUNK])
        fg = sb("fg", [P, CHUNK])
        out = sb("out_tok", [P, TILES, D])

        s_weights_in = sem("weights_in")
        s_consts_ready = sem("consts_ready")
        s_wstack_in = sem("wstack_in")
        s_mt_done = sem("mt_done")
        s_vo_done = sem("vo_done")
        s_mt_copied = sem("mt_copied")
        s_vo_copied = sem("vo_copied")
        s_setup_vec = sem("setup_vec")
        s_setup_act = sem("setup_act")
        s_lam_exp = sem("lam_exp")
        s_x_in = sem("x_in")
        s_var0 = sem("var0")
        s_rstd0 = sem("rstd0")
        s_xn0 = sem("xn0")
        s_xnt_ps = sem("xnt_ps")
        s_xnt_sb = sem("xnt_sb")
        s_yk_ps = sem("yk_ps")
        s_yk_sb = sem("yk_sb")
        s_vw_ps = sem("vw_ps")
        s_vw_sb = sem("vw_sb")
        s_s0_ps = sem("s0_ps")
        s_nb0 = sem("nb0")
        s_p0_done = sem("p0_done")
        s_pt_ps = sem("pt_ps")
        s_pt_sb = sem("pt_sb")
        s_att_ps = sem("att_ps")
        s_logits_ps = sem("logits_ps")
        s_u_ps = sem("u_ps")
        s_lsub = sem("lsub")
        s_lexp_done = sem("lexp_done")
        s_um_done = sem("um_done")
        s_umt_ps = sem("umt_ps")
        s_umt_sb = sem("umt_sb")
        s_inter_ps = sem("inter_ps")
        s_ha_done = sem("ha_done")
        s_hb_done = sem("hb_done")
        s_hsum_done = sem("hsum_done")
        s_z_ps = sem("z_ps")
        s_th0_done = sem("th0_done")
        s_var1 = sem("var1")
        s_rstd1 = sem("rstd1")
        s_xn1_done = sem("xn1_done")
        s_xnt1_ps = sem("xnt1_ps")
        s_xnt1_sb = sem("xnt1_sb")
        s_router_ps = sem("router_ps")
        s_rl_done = sem("rl_done")
        s_rexp_done = sem("rexp_done")
        s_w_done = sem("w_done")
        s_wt_ps = sem("wt_ps")
        s_wt_sb = sem("wt_sb")
        s_wt_stored = sem("wt_stored")
        s_wb_in0 = sem("wb_in0")
        s_wb_in1 = sem("wb_in1")
        s_qk_ps = sem("qk_ps")
        s_qkf_done = sem("qkf_done")
        s_part1 = sem("part1")
        s_part2 = sem("part2")
        s_part3 = sem("part3")
        s_parts_stored = sem("parts_stored")
        s_qk_in0 = sem("qk_in0")
        s_qk_in1 = sem("qk_in1")
        s_qk_in2 = sem("qk_in2")
        s_qk_in3 = sem("qk_in3")
        s_v_ps = sem("v_ps")
        s_v_sb = sem("v_sb")
        s_max_ps = sem("max_ps")
        s_nmax_done = sem("nmax_done")
        s_mp_done = sem("mp_done")
        s_mrow_ps = sem("mrow_ps")
        s_mrow_sb = sem("mrow_sb")
        s_mrow_in = sem("mrow_in")
        s_gate_ps = sem("gate_ps")
        s_gate_act = sem("gate_act")
        s_ga_mid = sem("ga_mid")
        s_ga_done = sem("ga_done")
        s_up_ps = sem("up_ps")
        s_h_done = sem("h_done")
        s_acc_ps = sem("acc_ps")
        s_sc_ps = sem("sc_ps")
        s_pk_done = sem("pk_done")
        s_pv_ps = sem("pv_ps")
        s_ot_sb = sem("ot_sb")
        s_ot_ps = sem("ot_ps")
        s_oc_done = sem("oc_done")
        s_ms_done = sem("ms_done")
        s_orms_done = sem("orms_done")
        s_on_done = sem("on_done")
        s_oct_ps = sem("oct_ps")
        s_oct_sb = sem("oct_sb")
        s_s1_ps = sem("s1_ps")
        s_fth_done = sem("fth_done")
        s_fg_done = sem("fg_done")
        s_fin_ps = sem("fin_ps")
        s_out_done = sem("out_done")
        s_out_stored = sem("out_stored")
        s_dve_link = sem("dve_link")
        s_qk_in = [s_qk_in0, s_qk_in1, s_qk_in2, s_qk_in3]
        s_wb_in = [s_wb_in0, s_wb_in1]

        PER = dict(x_in=16, var0=1, rstd0=1, xn0=TILES, xnt_ps=1, xnt_sb=1, yk_ps=1, yk_sb=1, vw_ps=1, vw_sb=1,
                   s0_ps=CB, nb0=1, p0_done=TILES, pt_ps=CB, pt_sb=CB, att_ps=1, logits_ps=1, u_ps=1, lsub=1,
                   lexp_done=1, um_done=2, umt_ps=2, umt_sb=2, inter_ps=2 * FB, ha_done=FB, hb_done=FB,
                   hsum_done=FB, z_ps=1, th0_done=TILES, var1=1, rstd1=1, xn1_done=TILES, xnt1_ps=1,
                   xnt1_sb=1, router_ps=1, rl_done=1, rexp_done=1, w_done=1, wt_ps=1, wt_sb=1, wt_stored=16,
                   qk_ps=4, qkf_done=4, part1=4, part2=4, part3=4, parts_stored=16 * 6,
                   v_ps=2, v_sb=2, max_ps=CB * MAX_UNITS, nmax_done=CB * MAX_UNITS,
                   mp_done=CB, mrow_ps=CB, mrow_sb=CB, mrow_in=16 * 3 * CB,
                   gate_ps=PAIRS + 1, gate_act=2 * (PAIRS + 1), ga_mid=PAIRS + 1, ga_done=PAIRS,
                   up_ps=PAIRS + 1, h_done=PAIRS + 1, acc_ps=PAIRS + 1, sc_ps=CB * GROUPS * 3, pk_done=CB * GROUPS * 3,
                   pv_ps=CB * GROUPS, ot_sb=CB * GROUPS, ot_ps=CB * GROUPS, oc_done=CB * GROUPS, ms_done=CB,
                   orms_done=CB, on_done=CB, oct_ps=CB, oct_sb=CB, s1_ps=1, fth_done=2, fg_done=1,
                   fin_ps=1, out_done=1, out_stored=16)

        def at(i, name, k):
            return i * PER[name] + k

        UNITS = [s[0] for s in PLAN for _ in range({"max": 1, "attend": 3}.get(s[0], 0))]

        def pair_free(eng, i, unit):
            if unit >= 2:
                kind = UNITS[unit - 2]
                if kind == "max":
                    eng.wait_ge(s_nmax_done, at(i, "nmax_done", UNITS[:unit - 1].count(kind)))
                else:
                    eng.wait_ge(s_pk_done, at(i, "pk_done", UNITS[:unit - 1].count(kind)))

        block = ctx.enter_context(nc.Block())

        n_weights = [0]

        @block.sync
        def _(sp):
            def load(dst, src):
                sp.dma_start(dst, src).then_inc(s_weights_in, 16)
                n_weights[0] += 1

            sp.dma_start(wstack[:, :, :], t["wkq"]).then_inc(s_wstack_in, 16)
            sp.wait_ge(s_mt_done, 1)
            sp.dma_start(wstack[:, :, :], t["wvo"]).then_inc(s_wstack_in, 16)
            for dst, name in ((wi_t, "wi_t"), (bi, "bi"), (wo_t, "wo_t"), (la, "la"), (lb, "lb"),
                              (gate_w, "gate_w"), (bo, "bo"), (wq1, "wq1"), (wk1, "wk1"), (wv1, "wv1"),
                              (wo1, "wo1"), (wr, "wr"), (wg, "wg"), (wu, "wu"), (wd, "wd"), (bd, "bd"),
                              (wgs, "wgs"), (wus, "wus"), (wds, "wds"), (bds, "bds")):
                load(dst[tuple(slice(None) for _ in dst.shape)], t[name])
            load(bg[:, 0:PAIRS], t["bg"])
            load(bu[:, 0:PAIRS], t["bu"])
            load(bg[0:INNER, PAIRS:], t["bgs"])
            load(bu[0:INNER, PAIRS:], t["bus"])
            load(gate_b[:, :], t["gate_b"].partition_broadcast(P))
            load(br[:, :], t["br"].partition_broadcast(P))
            for n, name in enumerate(("lq1", "lk1", "lq2", "lk2")):
                load(lam_in[:, n, :], t[name].partition_broadcast(P))
            for g in range(P // DV):
                load(rms_col[g * DV:(g + 1) * DV, :], t["rms"])
            assert n_weights[0] == N_WEIGHTS

            with sp.Fori(0, CHUNKS) as i:
                sp.dma_start(x[:, :, :], t["x"][bass.ds(i, 1)].rearrange("c p t d -> (c p) t d")).then_inc(s_x_in, 16)
                sp.wait_ge(s_part3, at(i, "part3", 4))
                sp.wait_ge(s_part2, at(i, "part2", 4))
                sp.wait_ge(s_part1, at(i, "part1", 4))
                for n in range(2):
                    for a in range(3):
                        sp.dma_start(t["parts_dram"][n, a].rearrange("(f p) t -> p f t", p=P),
                                     parts[:, a, 2 * n:2 * n + 2, :]).then_inc(s_parts_stored, 16)
                sp.wait_ge(s_parts_stored, at(i, "parts_stored", 96))

                def load_qk(b, g):
                    for n, (dst, order) in enumerate(((qa, (0, 0, 0, 1, 1, 2)), (ka, (0, 1, 2, 0, 1, 0)))):
                        for s, part in enumerate(order):
                            src = t["parts_dram"][n, part, g * GHC * DH:(g + 1) * GHC * DH, b * SEQ:(b + 1) * SEQ]
                            sp.dma_start(dst[DH * s:DH * s + DH, g * GHC:(g + 1) * GHC, :],
                                         src.rearrange("(h d) t -> d h t", d=DH)).then_inc(s_qk_in[g], 16)

                for g in range(GROUPS):
                    load_qk(0, g)
                sp.wait_ge(s_wt_sb, at(i, "wt_sb", 1))
                sp.dma_start(t["wt_dram"], wt[:, :]).then_inc(s_wt_stored, 16)
                sp.wait_ge(s_wt_stored, at(i, "wt_stored", 16))

                def load_wb(k):
                    src = t["wt_dram"].rearrange("(j e) t -> e j t", e=2)
                    for e in range(2):
                        sp.dma_start(wb[e * INNER:(e + 1) * INNER, k % 2, :, :],
                                     src[e, 2 * k:2 * k + 2, :].partition_broadcast(INNER)).then_inc(s_wb_in[k % 2], 16)

                load_wb(0)
                load_wb(1)
                for step in PLAN:
                    if step[0] == "moe" and step[1] % 2 == 0 and 4 <= step[1] + 2 < PAIRS:
                        sp.wait_ge(s_ga_done, at(i, "ga_done", step[1]))
                        load_wb(step[1] // 2 + 1)
                    elif step[0] == "attend" and step[1] == 0:
                        sp.wait_ge(s_sc_ps, at(i, "sc_ps", 3 * (step[2] + 1)))
                        load_qk(1, step[2])
                sp.wait_ge(s_out_done, at(i, "out_done", 1))
                sp.dma_start(t["out"][bass.ds(i, 1)].rearrange("c p t d -> (c p) t d"), out[:, :, :]).then_inc(s_out_stored, 16)
                sp.wait_ge(s_wstack_in, 32)
                sp.wait_ge(s_out_stored, at(i, "out_stored", 16))

        wall = 16 * N_WEIGHTS

        @block.tensor
        def _(pe):
            mm = nc.tensor.matmul

            for n, (b, done) in enumerate(((4, s_mt_done), (5, s_vo_done))):
                pe.wait_ge(s_wstack_in, 16 * (n + 1))
                for o in range(OT):
                    last = mm(bank[b][:, 0:P], wstack[:, 0, o * P:(o + 1) * P], wstack[:, 1, o * P:(o + 1) * P],
                              start=(o == 0), stop=(o == OT - 1))
                last.then_inc(done, 1)
            pe.wait_ge(s_weights_in, wall)
            pe.wait_ge(s_consts_ready, N_CONSTS)
            pe.wait_ge(s_setup_vec, N_SETUP_VEC)
            pe.wait_ge(s_mt_copied, 1)
            pe.wait_ge(s_vo_copied, 1)

            with pe.Fori(0, CHUNKS) as i:
                pe.wait_ge(s_xn0, at(i, "xn0", TILES))
                for c in range(TILES):
                    last = nc.tensor.transpose(bank[7][:, c * P:(c + 1) * P], xn[:, c, :], ident[:, :])
                last.then_inc(s_xnt_ps, 1)
                pe.wait_ge(s_xnt_sb, at(i, "xnt_sb", 1))
                for c in range(TILES):
                    last = mm(bank[7][:, c * E0:(c + 1) * E0], xnt[:, c * P:(c + 1) * P], gate_w[:, :], start=(c == 0), stop=True, skip_group_check=True)
                last.then_inc(s_logits_ps, 1)
                mm(bank[4][:, :], mt[:, :], xnt[:, :], start=True, stop=True).then_inc(s_yk_ps, 1)
                for c in range(TILES):
                    last = mm(bank[6][:, c * P:(c + 1) * P], xnt[:, c * P:(c + 1) * P], la[:, :], start=(c == 0), stop=True, skip_group_check=True)
                last.then_inc(s_u_ps, 1)
                for c in range(TILES):
                    last = mm(bank[5][:, c * P:(c + 1) * P], xnt[:, c * P:(c + 1) * P], vo[:, :], start=(c == 0), stop=True, skip_group_check=True)
                last.then_inc(s_vw_ps, 1)
                pe.wait_ge(s_yk_sb, at(i, "yk_sb", 1))
                for b in range(CB):
                    s = bank[b]
                    base = b * SEQ
                    mm(s[:, 0:P], identb[:, :], mask_q[:, 0, :], start=True, stop=False, skip_group_check=True)
                    mm(s[:, 2 * P:3 * P], identb[:, :], mask_q[:, 0, :], start=False, stop=False, skip_group_check=True)
                    mm(s[:, 0:P], xnt[:, base:base + P], yk[:, base:base + P], start=False, stop=True, skip_group_check=True)
                    mm(s[:, P:3 * P], xnt[:, base + P:base + SEQ], yk[:, base:base + SEQ], start=False, stop=True,
                       skip_group_check=True).then_inc(s_s0_ps, 1)
                for j in range(2):
                    pe.wait_ge(s_um_done, at(i, "um_done", j + 1))
                    for c in range(TILES):
                        last = nc.tensor.transpose(bank[2 + j][:, c * P:(c + 1) * P], um[:, j, c, :], ident[:, :])
                    last.then_inc(s_umt_ps, 1)
                for f in range(FB):
                    for j in range(2):
                        b = 4 + j if f % 2 == 0 else 6 + j
                        if f == 0:
                            pe.wait_ge(s_umt_sb, at(i, "umt_sb", j + 1))
                            if j:
                                pe.wait_ge(s_vw_sb, at(i, "vw_sb", 1))
                        elif f >= 2:
                            if j == 0:
                                pe.wait_ge(s_ha_done, at(i, "ha_done", f - 1))
                            else:
                                pe.wait_ge(s_hb_done, at(i, "hb_done", f - 1))
                        mm(bank[b], wi_t[:, f * P:(f + 1) * P], xnt[:, :], start=True, stop=False)
                        mm(bank[b], lb[:, f * P:(f + 1) * P], umt[:, j, :], start=False, stop=True).then_inc(s_inter_ps, 1)
                    if f == 0:
                        for b in range(CB):
                            pe.wait_ge(s_p0_done, at(i, "p0_done", 2 * b + 2))
                            s = bank[2 + b]
                            nc.tensor.transpose(s[:, 0:P], p0[:, 2 * b, 0:P], ident[:, :])
                            nc.tensor.transpose(s[:, P:2 * P], p0[:, 2 * b + 1, 0:P], ident[:, :])
                            nc.tensor.transpose(s[:, 2 * P:3 * P], p0[:, 2 * b + 1, P:SEQ], ident[:, :]).then_inc(s_pt_ps, 1)
                pe.wait_ge(s_vw_sb, at(i, "vw_sb", 1))
                for b in range(CB):
                    pe.wait_ge(s_pt_sb, at(i, "pt_sb", b + 1))
                    c = 2 * b
                    mm(bank[0][:, c * P:(c + 1) * P], pt0[:, b, 0:P], vw[:, c, :], start=(b == 0), stop=True, skip_group_check=True)
                    mm(bank[0][:, (c + 1) * P:(c + 2) * P], pt0[:, b, P:2 * P], vw[:, c, :], start=False, stop=False, skip_group_check=True)
                    last = mm(bank[0][:, (c + 1) * P:(c + 2) * P], pt0[:, b, 2 * P:3 * P], vw[:, c + 1, :], start=False, stop=True, skip_group_check=True)
                last.then_inc(s_att_ps, 1)
                pe.wait_ge(s_hsum_done, at(i, "hsum_done", FB))
                for c in range(TILES):
                    z = bank[1][:, c * P:(c + 1) * P]
                    mm(z, twos_row[:, :], bo[:, :], start=(c == 0), stop=False, skip_group_check=True)
                    for f in range(FB):
                        last = mm(z, ha[:, f, c * P:(c + 1) * P], wo_t[:, f, :], start=False, stop=(f == FB - 1), skip_group_check=True)
                last.then_inc(s_z_ps, 1)

                pe.wait_ge(s_xn1_done, at(i, "xn1_done", TILES))
                for c in range(TILES):
                    last = nc.tensor.transpose(bank[7][:, c * P:(c + 1) * P], xn1[:, c, :], ident[:, :])
                last.then_inc(s_xnt1_ps, 1)
                pe.wait_ge(s_xnt1_sb, at(i, "xnt1_sb", 1))
                for c in range(TILES):
                    last = mm(bank[7][:, c * E1:(c + 1) * E1], xnt1[:, c * P:(c + 1) * P], wr[:, :], start=(c == 0), stop=True, skip_group_check=True)
                last.then_inc(s_router_ps, 1)
                for n, (b, w) in enumerate(((4, wq1), (5, wq1), (6, wk1), (4, wk1))):
                    f = n % 2
                    if n == 3:
                        pe.wait_ge(s_part1, at(i, "part1", 1))
                    mm(bank[b], w[:, f * P:(f + 1) * P], xnt1[:, :], start=True, stop=True).then_inc(s_qk_ps, 1)
                for c in range(TILES):
                    last = mm(bank[c // 2][:, (c % 2) * 2 * P:(c % 2 + 1) * 2 * P], xnt1[:, c * P:(c + 1) * P], wv1[:, :],
                              start=(c % 2 == 0), stop=True, skip_group_check=True)
                    if c % 2:
                        last.then_inc(s_v_ps, 1)

                def up(j):
                    if j:
                        pe.wait_ge(s_h_done, at(i, "h_done", j))
                    else:
                        pe.wait_ge(s_part1, at(i, "part1", 3))
                    if j == PAIRS:
                        m = mm(bank[6][0:INNER, :], wus[:, :], xnt1[:, :], start=True, stop=True)
                    else:
                        m = mm(bank[6], wu[:, j * P:(j + 1) * P], xnt1[:, :], start=True, stop=True)
                    m.then_inc(s_up_ps, 1)

                def gate(j):
                    if j:
                        pe.wait_ge(s_gate_act, at(i, "gate_act", 2 * j))
                    else:
                        pe.wait_ge(s_part1, at(i, "part1", 2))
                    if j == PAIRS:
                        m = mm(bank[5][0:INNER, :], wgs[:, :], xnt1[:, :], start=True, stop=True)
                    else:
                        m = mm(bank[5], wg[:, j * P:(j + 1) * P], xnt1[:, :], start=True, stop=True)
                    m.then_inc(s_gate_ps, 1)

                def down(j):
                    pe.wait_ge(s_h_done, at(i, "h_done", j + 1))
                    if j == 0:
                        pe.wait_ge(s_wt_sb, at(i, "wt_sb", 1))
                        mm(bank[7], bd[:, :], wt[:, :], start=True, stop=False)
                    if j == PAIRS:
                        m = mm(bank[7], wds[:, :], h1[0:INNER, j % HR, :], start=False, stop=True)
                    else:
                        m = mm(bank[7], wd[:, j, :], h1[:, j % HR, :], start=False, stop=False)
                    m.then_inc(s_acc_ps, 1)

                def scores(i, pair, row, cols, stat, move, rows, hc0, tile0, width):
                    per = 512 // cols
                    mask = mask_q if stat is qa else mask_k
                    for n in range(2):
                        s = pairs[pair][:, n, :].rearrange("p (h c) -> p h c", c=cols)
                        diag = s[:, :, (cols - P if stat is qa else 0):(cols if stat is qa else P)]
                        mm(diag, identb[:, :], mask[:, 0:per, :], start=True, stop=False, skip_group_check=True)
                        for h in range(per):
                            hc = hc0 + n * per + h
                            last = mm(s[:, h, :], stat[0:rows, hc, row:row + P], move[0:rows, hc, tile0:tile0 + width],
                                      start=False, stop=True, skip_group_check=True)
                    return last

                units = 0
                for step in PLAN:
                    if step[0] == "moe":
                        j = step[1]
                        if j <= PAIRS:
                            gate(j)
                        if j == 1:
                            pe.wait_ge(s_w_done, at(i, "w_done", 1))
                            pe.wait_ge(s_part1, at(i, "part1", 4))
                            for c in range(TILES):
                                last = nc.tensor.transpose(bank[4][0:E1, c * P:(c + 1) * P], wtok[:, c, :], ident[:, :])
                            last.then_inc(s_wt_ps, 1)
                        if j >= 2:
                            down(j - 2)
                        if 1 <= j <= PAIRS + 1:
                            up(j - 1)
                    elif step[0] == "max":
                        _, b, g, u = step
                        if u == 0:
                            pe.wait_ge(s_qk_in[g], i * QK_IN * CB + QK_IN * (b + 1))
                        pair = units % 2
                        if units == 0:
                            pe.wait_ge(s_v_sb, at(i, "v_sb", 2))
                        else:
                            pair_free(pe, i, units)
                        units += 1
                        if u == 0:
                            last = scores(i, pair, 0, P, qa, ka, NEG_ROW, GHC * g, 0, P)
                        else:
                            last = scores(i, pair, P, SEQ, qa, ka, NEG_ROW, GHC * g + 4 * (u - 1), 0, SEQ)
                        last.then_inc(s_max_ps, 1)
                    elif step[0] == "minus":
                        b = step[1]
                        pe.wait_ge(s_mp_done, at(i, "mp_done", b + 1))
                        if b:
                            pe.wait_ge(s_oct_sb, at(i, "oct_sb", b))
                        else:
                            pe.wait_ge(s_wt_sb, at(i, "wt_sb", 1))
                        for c in range(2):
                            last = mm(bank[4][0:3 * HC, c * P:(c + 1) * P],
                                      mparts[:, 2 * b + c, :, :].rearrange("p a h -> p (a h)"), identb[:, :],
                                      start=(c == 0), stop=True, skip_group_check=True)
                        last.then_inc(s_mrow_ps, 1)
                    elif step[0] == "attend":
                        _, b, g = step
                        if g == 0:
                            pe.wait_ge(s_mrow_in, at(i, "mrow_in", 16 * 3 * (b + 1)))
                        for u in range(3):
                            pair = units % 2
                            pair_free(pe, i, units)
                            units += 1
                            if u < 2:
                                last = scores(i, pair, 0, SEQ, ka, qa, KROWS, g * GHC + 4 * u, 0, SEQ)
                            else:
                                last = scores(i, pair, P, P, ka, qa, KROWS, g * GHC, P, P)
                            last.then_inc(s_sc_ps, 1)
                        n = b * GROUPS + g
                        if g == 0:
                            pe.wait_ge(s_mrow_sb, at(i, "mrow_sb", b + 1))
                        else:
                            pe.wait_ge(s_oc_done, at(i, "oc_done", n))
                        pe.wait_ge(s_pk_done, at(i, "pk_done", 3 * n + 2))
                        o = bank[4].rearrange("p (c q) -> p c q", c=2)
                        for hh in range(GH):
                            head = g * GH + hh
                            mm(o[32 * hh:32 * hh + 32, :, :], v1[:, 2 * b, head, :], pk0[:, 2 * hh:2 * hh + 2, :],
                               start=True, stop=False, skip_group_check=True)
                        pe.wait_ge(s_pk_done, at(i, "pk_done", 3 * n + 3))
                        for hh in range(GH):
                            head = g * GH + hh
                            last = mm(o[32 * hh:32 * hh + 32, :, P:SEQ], v1[:, 2 * b + 1, head, :], pk1[:, 2 * hh:2 * hh + 2, :],
                                      start=False, stop=True, skip_group_check=True)
                        last.then_inc(s_pv_ps, 1)
                        pe.wait_ge(s_ot_sb, at(i, "ot_sb", n + 1))
                        for q in range(2):
                            for c in range(2):
                                k = 2 * q + c
                                last = nc.tensor.transpose(bank[4][:, k * P:(k + 1) * P], ot[:, c, q * P:(q + 1) * P], ident[:, :])
                        last.then_inc(s_ot_ps, 1)
                    elif step[0] == "norm":
                        b = step[1]
                        pe.wait_ge(s_on_done, at(i, "on_done", b + 1))
                        for c in range(2):
                            for f in range(2):
                                k = 2 * f + c
                                last = nc.tensor.transpose(bank[4][:, k * P:(k + 1) * P], on[:, c, f * P:(f + 1) * P], ident[:, :])
                        last.then_inc(s_oct_ps, 1)
                pe.wait_ge(s_oct_sb, at(i, "oct_sb", CB))
                for f in range(2):
                    last = mm(bank[4], wo1s[:, f, :], oct_[:, f, :], start=(f == 0), stop=(f == 1))
                last.then_inc(s_s1_ps, 1)
                pe.wait_ge(s_fg_done, at(i, "fg_done", 1))
                for c in range(TILES):
                    last = nc.tensor.transpose(bank[5][:, c * P:(c + 1) * P], fg[:, c * P:(c + 1) * P], ident[:, :])
                last.then_inc(s_fin_ps, 1)
                pe.wait_ge(s_out_done, at(i, "out_done", 1))

        @block.scalar
        def _(act):
            A = nc.scalar.activation

            act.wait_ge(s_mt_done, 1)
            A(mt[:, :], bank[4][:, 0:P], ACT.Copy).then_inc(s_mt_copied, 1)
            act.wait_ge(s_vo_done, 1)
            A(vo[:, :], bank[5][:, 0:P], ACT.Copy).then_inc(s_vo_copied, 1)
            act.wait_ge(s_lam_exp, 1)
            A(lam_e[:, :, :], lam_e[:, :, :], ACT.Exp).then_inc(s_setup_act, 1)

            with act.Fori(0, CHUNKS) as i:
                def free(ins, b):
                    ins

                def twice(ins, name, b):
                    ins.then_inc(S[name], 1)

                act.wait_ge(s_xnt_ps, at(i, "xnt_ps", 1))
                A(xnt[:, :], bank[7], ACT.Copy).then_inc(s_xnt_sb, 1)
                act.wait_ge(s_yk_ps, at(i, "yk_ps", 1))
                A(yk[:, :], bank[4], ACT.Copy).then_inc(s_yk_sb, 1)
                act.wait_ge(s_lsub, at(i, "lsub", 1))
                A(lexp[:, :, :], logit[:, :, :], ACT.Exp).then_inc(s_lexp_done, 1)
                act.wait_ge(s_vw_ps, at(i, "vw_ps", 1))
                A(vw[:, :, :], bank[5].rearrange("p (c d) -> p c d", d=D), ACT.Copy).then_inc(s_vw_sb, 1)
                act.wait_ge(s_nb0, at(i, "nb0", 1))
                for c in range(TILES):
                    w = P if c % 2 == 0 else SEQ
                    o = 0 if c % 2 == 0 else P
                    ins = A(p0[:, c, 0:w], bank[c // 2][:, o:o + w], ACT.Exp, bias=nbias0[:, c:c + 1], scale=SCALE0,
                            accum_out=l0[:, c:c + 1])
                    ins.then_inc(s_p0_done, 1)
                for j in range(2):
                    act.wait_ge(s_umt_ps, at(i, "umt_ps", j + 1))
                    ins = A(umt[:, j, :], bank[2 + j], ACT.Copy)
                    ins.then_inc(s_umt_sb, 1)
                for f in range(FB):
                    b = 4 if f % 2 == 0 else 6
                    act.wait_ge(s_inter_ps, at(i, "inter_ps", 2 * f + 1))
                    A(ha[:, f, :], bank[b], ACT.Relu, bias=bi[:, f:f + 1]).then_inc(s_ha_done, 1)
                    if f == 0:
                        for b in range(CB):
                            act.wait_ge(s_pt_ps, at(i, "pt_ps", b + 1))
                            ins = A(pt0[:, b, :], bank[2 + b][:, 0:3 * P], ACT.Copy)
                            ins.then_inc(s_pt_sb, 1)
                act.wait_ge(s_z_ps, at(i, "z_ps", 1))
                for c in range(TILES):
                    A(th0[:, c, :], bank[1][:, c * P:(c + 1) * P], ACT.Tanh, scale=hvs[:, c:c + 1]).then_inc(s_th0_done, 1)
                act.wait_ge(s_xnt1_ps, at(i, "xnt1_ps", 1))
                A(xnt1[:, :], bank[7], ACT.Copy).then_inc(s_xnt1_sb, 1)
                act.wait_ge(s_rl_done, at(i, "rl_done", 1))
                A(rexp[:, :, :], rlog[:, :, :], ACT.Exp, scale=-1.0).then_inc(s_rexp_done, 1)
                for n, b in enumerate((4, 5, 6, 4)):
                    act.wait_ge(s_qk_ps, at(i, "qk_ps", n + 1))
                    A(qkf[:, n, :], bank[b], ACT.Copy).then_inc(s_qkf_done, 1)
                    A(parts[:, 0, n, :], bank[b], ACT.Copy).then_inc(s_part1, 1)
                ng = 0
                units = 0
                for step in PLAN:
                    if step[0] == "moe":
                        j = step[1]
                        if j <= PAIRS:
                            rows = INNER if j == PAIRS else P
                            act.wait_ge(s_gate_ps, at(i, "gate_ps", j + 1))
                            if j >= 2:
                                act.wait_ge(s_h_done, at(i, "h_done", j - 1))
                            A(gt[0:rows, j % 2, :], bank[5][0:rows, :], ACT.Tanh, bias=bgh[0:rows, j:j + 1], scale=0.5).then_inc(s_gate_act, 1)
                            A(gb[0:rows, j % 2, :], bank[5][0:rows, :], ACT.Identity, bias=bg[0:rows, j:j + 1]).then_inc(s_gate_act, 1)
                        if j == 1:
                            act.wait_ge(s_wt_ps, at(i, "wt_ps", 1))
                            A(wt[:, :], bank[4][0:E1, :], ACT.Copy).then_inc(s_wt_sb, 1)
                    elif step[0] == "max":
                        units += 1
                    elif step[0] == "minus":
                        b = step[1]
                        act.wait_ge(s_mrow_ps, at(i, "mrow_ps", b + 1))
                        A(mrows[:, b * SEQ:(b + 1) * SEQ], bank[4][0:3 * HC, 0:SEQ], ACT.Copy).then_inc(s_mrow_sb, 1)
                        act.wait_ge(s_mrow_sb, at(i, "mrow_sb", b + 1))
                        for a in range(3):
                            act.dma_start(qa[NEG_ROW + a:NEG_ROW + a + 1, :, :],
                                          mrows[a * HC:(a + 1) * HC, b * SEQ:(b + 1) * SEQ]).then_inc(s_mrow_in, 16)
                    elif step[0] == "attend":
                        _, b, g = step
                        n = b * GROUPS + g
                        for u in range(3):
                            pair = units % 2
                            units += 1
                            act.wait_ge(s_sc_ps, at(i, "sc_ps", 3 * n + u + 1))
                            if u == 0 and n:
                                act.wait_ge(s_pv_ps, at(i, "pv_ps", n))
                            src = pairs[pair][:, :, :]
                            if u < 2:
                                dst = pk0[:, 4 * u:4 * u + 4, :]
                                src = src.rearrange("p n (h c) -> p (n h) c", c=SEQ)
                            else:
                                dst = pk1[:, :, :]
                                src = src.rearrange("p n (h c) -> p (n h) c", c=P)
                            A(dst, src, ACT.Exp, scale=SCALE1).then_inc(s_pk_done, 1)
                        act.wait_ge(s_pv_ps, at(i, "pv_ps", n + 1))
                        if n:
                            act.wait_ge(s_ot_ps, at(i, "ot_ps", n))
                        A(ot[:, :, :], bank[4].rearrange("p (c q) -> p c q", c=2), ACT.Copy).then_inc(s_ot_sb, 1)
                    elif step[0] == "norm":
                        b = step[1]
                        act.wait_ge(s_oct_ps, at(i, "oct_ps", b + 1))
                        A(oct_[:, :, b * SEQ:(b + 1) * SEQ], bank[4].rearrange("p (f q) -> p f q", f=2), ACT.Copy).then_inc(s_oct_sb, 1)
                act.wait_ge(s_acc_ps, at(i, "acc_ps", PAIRS + 1))
                A(fth[:, :], bank[7], ACT.Tanh, bias=bdsh[:, :], scale=0.5).then_inc(s_fth_done, 1)
                A(fvh[:, :], bank[7], ACT.Identity, bias=bdsh[:, :], scale=0.5).then_inc(s_fth_done, 1)
                act.wait_ge(s_out_done, at(i, "out_done", 1))

        @block.gpsimd
        def _(pool):
            def const(ins):
                ins.then_inc(s_consts_ready, 1)

            const(pool.memset(ident[:, :], 0.0))
            const(pool.memset(identb[:, :], 0.0))
            const(pool.memset(mask_q[:, :, :], 0.0))
            const(pool.memset(mask_k[:, :, :], 0.0))
            const(pool.memset(minus_half[:, :], -0.5))
            const(pool.iota(iota8[:, :], pattern=[[1, E0]], base=0, channel_multiplier=0, allow_small_or_imprecise_dtypes=True))
            pool.wait_ge(s_consts_ready, 6)
            for m in (ident, identb):
                const(pool.affine_select(out=m[:, :], in_=m[:, :], compare_op=ALU.not_equal, fill=1.0, base=0,
                                         pattern=[[-1, P]], channel_multiplier=1))
            const(pool.affine_select(out=mask_q[:, :, :], in_=mask_q[:, :, :], compare_op=ALU.is_ge, fill=MASKED, base=0,
                                     pattern=[[0, 4], [-1, P]], channel_multiplier=1))
            const(pool.affine_select(out=mask_k[:, :, :], in_=mask_k[:, :, :], compare_op=ALU.is_ge, fill=MASKED, base=0,
                                     pattern=[[0, 4], [1, P]], channel_multiplier=-1))
            pool.wait_ge(s_consts_ready, N_CONSTS)

            pw = nc.gpsimd.tensor_tensor
            with pool.Fori(0, CHUNKS) as i:
                pool.wait_ge(s_var0, at(i, "var0", 1))
                pw(rstd[:, :], vare[:, :], minus_half[:, 0:TILES], ALU.pow).then_inc(s_rstd0, 1)
                for f in range(FB):
                    pool.wait_ge(s_ha_done, at(i, "ha_done", f + 1))
                    pool.wait_ge(s_hb_done, at(i, "hb_done", f + 1))
                    pw(ha[:, f, :], ha[:, f, :], hb[:, f % 2, :], ALU.add).then_inc(s_hsum_done, 1)
                pool.wait_ge(s_var1, at(i, "var1", 1))
                pw(rstd[:, :], vare[:, :], minus_half[:, 0:TILES], ALU.pow).then_inc(s_rstd1, 1)
                for n in range(4):
                    pool.wait_ge(s_part2, at(i, "part2", n + 1))
                    pw(parts[:, 2, n, :], qkf[:, n, :], parts[:, 1, n, :], ALU.subtract).then_inc(s_part3, 1)
                for step in PLAN:
                    if step[0] == "moe" and step[1] <= PAIRS:
                        j = step[1]
                        pool.wait_ge(s_gate_act, at(i, "gate_act", 2 * j + 1))
                        pw(waited[:, 1:2], minus_half[:, 0:1], minus_half[:, 0:1], ALU.add)
                        rows = INNER if j == PAIRS else P
                        nc.gpsimd.tensor_scalar(gt[0:rows, j % 2, :], gt[0:rows, j % 2, :], 0.5, 0.5,
                                                ALU.mult, ALU.add).then_inc(s_ga_mid, 1)
                        if j < PAIRS:
                            k = j // 2
                            pool.wait_ge(s_ga_mid, at(i, "ga_mid", j + 1))
                            pool.wait_ge(s_wb_in[k % 2], i * WB_IN + 32 * (k // 2 + 1))
                            pw(gt[:, j % 2, :], gt[:, j % 2, :], wb[:, k % 2, j % 2, :], ALU.mult).then_inc(s_ga_done, 1)
                    elif step[0] == "norm":
                        b = step[1]
                        pool.wait_ge(s_ms_done, at(i, "ms_done", b + 1))
                        pw(orms[:, :, :], oms[:, :, :], minus_half[:, :].rearrange("p (a b) -> p a b", a=2), ALU.pow).then_inc(s_orms_done, 1)
                pool.wait_ge(s_out_done, at(i, "out_done", 1))

        @block.vector
        def _(dve):
            V = nc.vector
            count = [0]
            base_i = [None]

            def link(ins, by_copy=False):
                count[0] += 1
                ins.then_inc(s_dve_link, 1)
                if base_i[0] is None:
                    dve.wait_ge(s_dve_link, count[0])
                else:
                    dve.wait_ge(s_dve_link, base_i[0] * DVE_LINKS + count[0] + SETUP_LINKS)
                    if by_copy:
                        V.tensor_copy(waited[:, 0:1], iota8[:, 0:1])

            def setup(ins):
                ins.then_inc(s_setup_vec, 1)

            setup(V.memset(twos_row[:, :], 2.0))
            setup(V.memset(v1[:, :, :, :], 0.0))
            setup(V.memset(qa[0:NEG_ROW, :, :], 0.0))
            setup(V.memset(ka[0:NEG_ROW, :, :], 0.0))
            setup(V.memset(ka[NEG_ROW:KROWS, :, :], 1.0))
            dve.wait_ge(s_setup_vec, 2)
            setup(V.memset(v1[:, :, :, DV:DV + 1], 1.0))
            dve.wait_ge(s_weights_in, wall)
            setup(V.tensor_scalar(bgh[:, 0:PAIRS], bg[:, 0:PAIRS], 0.5, None, ALU.mult))
            setup(V.tensor_scalar(bgh[0:INNER, PAIRS:], bg[0:INNER, PAIRS:], 0.5, None, ALU.mult))
            setup(V.tensor_scalar(bdsh[:, :], bds[:, :], 0.5, None, ALU.mult))
            for f in range(2):
                setup(V.tensor_scalar(wo1s[:, f, :], wo1[:, f, :], rms_col[:, 0:1], 1.0 - LAM0, ALU.mult, ALU.mult))
            link(V.tensor_tensor(lam_in[:, 0, :], lam_in[:, 0, :], lam_in[:, 1, :], ALU.mult))
            link(V.tensor_tensor(lam_in[:, 2, :], lam_in[:, 2, :], lam_in[:, 3, :], ALU.mult))
            link(V.reduce_sum(lam_e[:, 0, :], lam_in[:, 0, :].rearrange("p (h d) -> p h d", d=DH), AX))
            V.reduce_sum(lam_e[:, 1, :], lam_in[:, 2, :].rearrange("p (h d) -> p h d", d=DH), AX).then_inc(s_lam_exp, 1)
            dve.wait_ge(s_setup_act, 1)
            link(V.scalar_tensor_tensor(out=lam[:, :], in0=lam_e[:, 0, :], scalar=LAM0, in1=lam_e[:, 1, :],
                                        op0=ALU.add, op1=ALU.subtract))
            dve.wait_ge(s_consts_ready, N_CONSTS)
            assert count[0] == SETUP_LINKS
            count[0] = 0

            def layernorm(i, src, dst, var_ready, rstd_ready, done):
                for c in range(TILES):
                    ins = V.bn_stats(stats[:, c, :], src[:, c, :])
                link(ins, True)
                for c in range(TILES):
                    ins = V.bn_aggr(mv[:, c, :], stats[:, c, :])
                link(ins)
                V.tensor_scalar(vare[:, :], mv[:, :, 1], EPS, None, ALU.add).then_inc(var_ready, 1)
                dve.wait_ge(rstd_ready, i + 1)
                for c in range(TILES):
                    V.tensor_scalar(dst[:, c, :], src[:, c, :], mv[:, c, 0:1], rstd[:, c:c + 1], ALU.subtract, ALU.mult).then_inc(done, 1)

            def wide(ap, n):
                return ap.unsqueeze(2).to_broadcast([P, ap.shape[1], n])

            with dve.Fori(0, CHUNKS) as i:
                base_i[0] = i
                dve.wait_ge(s_x_in, at(i, "x_in", 16))
                layernorm(i, x, xn, s_var0, s_rstd0, s_xn0)
                dve.wait_ge(s_logits_ps, at(i, "logits_ps", 1))
                link(V.tensor_tensor(logit[:, :, :], bank[7][:, 0:TILES * E0].rearrange("p (c e) -> p c e", e=E0),
                                     gate_b[:, :].unsqueeze(1).to_broadcast([P, TILES, E0]), ALU.add))
                link(V.reduce_max(lmax[:, :], logit[:, :, :], AX))
                V.tensor_tensor(logit[:, :, :], logit[:, :, :], wide(lmax[:, :], E0), ALU.subtract).then_inc(s_lsub, 1)
                dve.wait_ge(s_lexp_done, at(i, "lexp_done", 1))
                link(V.reduce_sum(lsum[:, :], lexp[:, :, :], AX))
                link(V.reciprocal(lsum[:, :], lsum[:, :]))
                link(V.tensor_tensor(lexp[:, :, :], lexp[:, :, :], wide(lsum[:, :], E0), ALU.mult), True)
                for c in range(TILES):
                    ins = V.max(top[:, c, :], lexp[:, c, :])
                link(ins, True)
                for c in range(TILES):
                    ins = V.max_index(topi[:, c, :], top[:, c, :], lexp[:, c, :])
                link(ins)
                link(V.tensor_copy(topf[:, :, :], topi[:, :, 0:2]))
                for j in range(2):
                    ins = V.tensor_tensor(pick[:, j, :, :], iota8[:, :].unsqueeze(1).to_broadcast([P, TILES, E0]),
                                          topf[:, :, j:j + 1].to_broadcast([P, TILES, E0]), ALU.is_equal)
                link(ins)
                link(V.tensor_tensor(hvs[:, :], top[:, :, 0], top[:, :, 1], ALU.add))
                link(V.tensor_scalar(hvs[:, :], hvs[:, :], 0.5, None, ALU.mult))
                dve.wait_ge(s_u_ps, at(i, "u_ps", 1))
                for j in range(2):
                    ins = V.tensor_tensor(um[:, j, :, :].rearrange("p c (e r) -> p (c e) r", r=R0),
                                          bank[6].rearrange("p (g r) -> p g r", r=R0),
                                          wide(pick[:, j, :, :].rearrange("p c e -> p (c e)"), R0), ALU.mult)
                    ins.then_inc(s_um_done, 1)
                for b in range(CB):
                    dve.wait_ge(s_s0_ps, at(i, "s0_ps", b + 1))
                    V.tensor_reduce(nmax0[:, 2 * b:2 * b + 1], bank[b][:, 0:P], AX, ALU.max, negate=True)
                    ins = V.tensor_reduce(nmax0[:, 2 * b + 1:2 * b + 2], bank[b][:, P:3 * P], AX, ALU.max, negate=True)
                link(ins)
                V.tensor_scalar(nbias0[:, :], nmax0[:, :], SCALE0, None, ALU.mult).then_inc(s_nb0, 1)
                for f in range(FB):
                    b = 5 if f % 2 == 0 else 7
                    dve.wait_ge(s_inter_ps, at(i, "inter_ps", 2 * f + 2))
                    if f >= 2:
                        dve.wait_ge(s_hsum_done, at(i, "hsum_done", f - 1))
                    V.tensor_scalar(hb[:, f % 2, :], bank[b], bi[:, f:f + 1], 0.0, ALU.add, ALU.max).then_inc(s_hb_done, 1)
                dve.wait_ge(s_p0_done, at(i, "p0_done", TILES))
                link(V.reciprocal(rl0[:, :], l0[:, :]))
                dve.wait_ge(s_att_ps, at(i, "att_ps", 1))
                link(V.tensor_tensor(tmp0[:, :, :], bank[0].rearrange("p (c d) -> p c d", d=D), wide(rl0[:, :], D), ALU.mult))
                dve.wait_ge(s_th0_done, at(i, "th0_done", TILES))
                link(V.tensor_tensor(gate0[:, :, :], bank[1].rearrange("p (c d) -> p c d", d=D), wide(hvs[:, :], D), ALU.mult))
                link(V.scalar_tensor_tensor(out=gate0[:, :, :], in0=th0[:, :, :], scalar=1.0, in1=gate0[:, :, :],
                                       op0=ALU.add, op1=ALU.mult))
                link(V.tensor_tensor(gate0[:, :, :], gate0[:, :, :], tmp0[:, :, :], ALU.mult))
                link(V.tensor_tensor(x1[:, :, :], x[:, :, :], gate0[:, :, :], ALU.add))
                layernorm(i, x1, xn1, s_var1, s_rstd1, s_xn1_done)
                dve.wait_ge(s_router_ps, at(i, "router_ps", 1))
                V.tensor_tensor(rlog[:, :, :], bank[7][:, 0:TILES * E1].rearrange("p (c e) -> p c e", e=E1),
                                br[:, :].unsqueeze(1).to_broadcast([P, TILES, E1]), ALU.add).then_inc(s_rl_done, 1)
                dve.wait_ge(s_rexp_done, at(i, "rexp_done", 1))
                link(V.tensor_scalar(aff[:, :, :], rexp[:, :, :], 1.0, None, ALU.add))
                link(V.reciprocal(aff[:, :, :], aff[:, :, :]), True)
                for c in range(TILES):
                    ins = V.max(top1[:, c, :], aff[:, c, :])
                link(ins, True)
                for c in range(TILES):
                    ins = V.match_replace(rest1[:, c, :], top1[:, c, :], aff[:, c, :], -1.0)
                link(ins)
                link(V.scalar_tensor_tensor(out=wtok[:, :, :], in0=rest1[:, :, :], scalar=0.0, in1=aff[:, :, :],
                                            op0=ALU.is_lt, op1=ALU.mult))
                link(V.reduce_sum(wsum[:, :], top1[:, :, :], AX))
                link(V.tensor_scalar(wsum[:, :], wsum[:, :], 1e-9, None, ALU.add))
                link(V.reciprocal(wsum[:, :], wsum[:, :]))
                V.tensor_tensor(wtok[:, :, :], wtok[:, :, :], wide(wsum[:, :], E1), ALU.mult).then_inc(s_w_done, 1)
                for n in range(4):
                    dve.wait_ge(s_qkf_done, at(i, "qkf_done", n + 1))
                    dve.wait_ge(s_part1, at(i, "part1", n + 1))
                    link(V.tensor_tensor(qkf[:, n, :], qkf[:, n, :], parts[:, 0, n, :], ALU.subtract))
                    V.tensor_copy(parts[:, 1, n, :], qkf[:, n, :]).then_inc(s_part2, 1)
                for n in range(2):
                    dve.wait_ge(s_v_ps, at(i, "v_ps", n + 1))
                    ins = V.tensor_copy(v1[:, 2 * n:2 * n + 2, :, 0:DV].rearrange("p c h d -> p (c h) d"),
                                        bank[n].rearrange("p (g d) -> p g d", d=DV))
                    ins.then_inc(s_v_sb, 1)

                def experts(j):
                    rows = INNER if j == PAIRS else P
                    dve.wait_ge(s_gate_act, at(i, "gate_act", 2 * j + 2))
                    if j == PAIRS:
                        dve.wait_ge(s_ga_mid, at(i, "ga_mid", j + 1))
                    else:
                        dve.wait_ge(s_ga_done, at(i, "ga_done", j + 1))
                    if j >= HR:
                        dve.wait_ge(s_acc_ps, at(i, "acc_ps", j - HR + 1))
                    link(V.tensor_tensor(h1[0:rows, j % HR, :], gt[0:rows, j % 2, :], gb[0:rows, j % 2, :], ALU.mult))
                    dve.wait_ge(s_up_ps, at(i, "up_ps", j + 1))
                    V.scalar_tensor_tensor(out=h1[0:rows, j % HR, :], in0=bank[6][0:rows, :], scalar=bu[0:rows, j:j + 1],
                                           in1=h1[0:rows, j % HR, :], op0=ALU.add, op1=ALU.mult).then_inc(s_h_done, 1)

                units = 0
                nmaxes = 0
                for step in PLAN:
                    if step[0] == "moe":
                        if 1 <= step[1] <= PAIRS + 1:
                            experts(step[1] - 1)
                    elif step[0] == "max":
                        _, b, g, u = step
                        pair = units % 2
                        units += 1
                        nmaxes += 1
                        dve.wait_ge(s_max_ps, at(i, "max_ps", nmaxes))
                        src = pairs[pair][:, :, :]
                        if u == 0:
                            src = src.rearrange("p n (h c) -> p (n h) c", c=P)
                            dst = nmax1[:, 2 * b, GHC * g:GHC * g + 8]
                        else:
                            src = src.rearrange("p n (h c) -> p (n h) c", c=SEQ)
                            dst = nmax1[:, 2 * b + 1, GHC * g + 4 * (u - 1):GHC * g + 4 * u]
                        V.tensor_reduce(dst, src, AX, ALU.max, negate=True).then_inc(s_nmax_done, 1)
                    elif step[0] == "minus":
                        b = step[1]
                        dve.wait_ge(s_nmax_done, at(i, "nmax_done", (b + 1) * MAX_UNITS))
                        c = slice(2 * b, 2 * b + 2)
                        link(V.tensor_copy(mparts[:, c, 0, :], nmax1[:, c, :]))
                        link(V.tensor_tensor(mres[:, c, :], nmax1[:, c, :], mparts[:, c, 0, :], ALU.subtract))
                        link(V.tensor_copy(mparts[:, c, 1, :], mres[:, c, :]))
                        V.tensor_tensor(mparts[:, c, 2, :], mres[:, c, :], mparts[:, c, 1, :], ALU.subtract).then_inc(s_mp_done, 1)
                    elif step[0] == "attend":
                        _, b, g = step
                        n = b * GROUPS + g
                        units += 3
                        dve.wait_ge(s_ot_ps, at(i, "ot_ps", n + 1))
                        o = bank[4].rearrange("p (g w) -> p g w", w=VW1)
                        rl = rl1[:, :, :, :].rearrange("p q c h -> p (q c h)")
                        link(V.reciprocal(rl, o[:, :, DV]))
                        link(V.tensor_tensor(rl1[:, :, 1, :], rl1[:, :, 1, :],
                                             lam[:, g * GH:(g + 1) * GH].unsqueeze(1).to_broadcast([P, 2, GH]), ALU.mult))
                        link(V.tensor_tensor(o12[:, :, :, :, :].rearrange("p q c h d -> p (q c h) d"), o[:, :, 0:DV],
                                        wide(rl, DV), ALU.mult))
                        V.tensor_tensor(oc[:, 2 * b:2 * b + 2, g * GH * DV:(g + 1) * GH * DV],
                                        o12[:, :, 0, :, :].rearrange("p q h d -> p q (h d)"),
                                        o12[:, :, 1, :, :].rearrange("p q h d -> p q (h d)"), ALU.subtract).then_inc(s_oc_done, 1)
                        dve.wait_ge(s_oc_done, at(i, "oc_done", n + 1))
                    elif step[0] == "norm":
                        b = step[1]
                        c = slice(2 * b, 2 * b + 2)
                        link(V.tensor_tensor(osq[:, :, :], oc[:, c, :], oc[:, c, :], ALU.mult))
                        link(V.reduce_sum(oms[:, :, :].rearrange("p q h -> p (q h)"),
                                          osq[:, :, :].rearrange("p q (h d) -> p (q h) d", d=DV), AX))
                        V.tensor_scalar(oms[:, :, :], oms[:, :, :], 1.0 / DV, EPS, ALU.mult, ALU.add).then_inc(s_ms_done, 1)
                        dve.wait_ge(s_orms_done, at(i, "orms_done", b + 1))
                        if b:
                            dve.wait_ge(s_oct_ps, at(i, "oct_ps", b))
                        V.tensor_tensor(on[:, :, :].rearrange("p q (h d) -> p (q h) d", d=DV),
                                        oc[:, c, :].rearrange("p q (h d) -> p (q h) d", d=DV),
                                        wide(orms[:, :, :].rearrange("p q h -> p (q h)"), DV), ALU.mult).then_inc(s_on_done, 1)
                dve.wait_ge(s_fth_done, at(i, "fth_done", 2))
                link(V.scalar_tensor_tensor(out=fg[:, :], in0=fth[:, :], scalar=1.0, in1=fvh[:, :], op0=ALU.add, op1=ALU.mult))
                dve.wait_ge(s_s1_ps, at(i, "s1_ps", 1))
                V.tensor_tensor(fg[:, :], bank[4], fg[:, :], ALU.mult).then_inc(s_fg_done, 1)
                dve.wait_ge(s_fin_ps, at(i, "fin_ps", 1))
                V.tensor_tensor(out[:, :, :], x1[:, :, :], bank[5].rearrange("p (c d) -> p c d", d=D), ALU.add).then_inc(s_out_done, 1)
                dve.wait_ge(s_out_stored, at(i, "out_stored", 16))
            assert count[0] == DVE_LINKS, count[0]


def l0_and_l1_kernel(nc, a, out):
    t = dict(a)
    t["out"] = out
    t["parts_dram"] = nc.dram_tensor("parts_scratch", (2, 3, 2 * P, CHUNK), BF16, kind="Internal").ap()
    t["wt_dram"] = nc.dram_tensor("wt_scratch", (E1, CHUNK), F32, kind="Internal").ap()
    build(nc, t)


def kernel(**inputs):
    import numpy as _np
    import concourse.bacc as _bacc
    from concourse import mybir as _mybir
    from concourse.bass_utils import run_bass_kernel_spmd as _run

    v = {k: _np.asarray(x) for k, x in inputs.items()}

    def rows(w, n):
        return w.reshape(n, -1, w.shape[1]).transpose(1, 0, 2)

    a = {
        "x": v["L0_attn_in_features"].reshape(CHUNKS, TILES, P, D).transpose(0, 2, 1, 3),
        "wkq": _np.stack([rows(v["L0_attn_w_k"], OT).reshape(P, -1), rows(v["L0_attn_w_q"], OT).reshape(P, -1)], 1),
        "wvo": _np.stack([rows(v["L0_attn_w_v"], OT).reshape(P, -1), rows(v["L0_attn_w_o"].T, OT).reshape(P, -1)], 1),
        "wi_t": v["L0_ffn_wi"].T,
        "bi": v["L0_ffn_bi"].reshape(FB, P).T,
        "wo_t": rows(v["L0_ffn_wo"].T, FB),
        "bo": v["L0_ffn_bo"].reshape(1, P),
        "la": v["L0_ffn_lora_A"].reshape(E0 * R0, D).T,
        "lb": v["L0_ffn_lora_B"].transpose(0, 2, 1).reshape(E0 * R0, 512),
        "gate_w": v["L0_ffn_gate_w"].T,
        "gate_b": v["L0_ffn_gate_b"],
        "wq1": v["L1_attn_Wq"].T, "wk1": v["L1_attn_Wk"].T, "wv1": v["L1_attn_Wv"].T,
        "wo1": rows(v["L1_attn_Wo"].T, 2),
        "lq1": v["L1_attn_lq1"].reshape(-1), "lk1": v["L1_attn_lk1"].reshape(-1),
        "lq2": v["L1_attn_lq2"].reshape(-1), "lk2": v["L1_attn_lk2"].reshape(-1),
        "rms": v["L1_attn_rms_scale"].reshape(DV, 1),
        "wr": v["L1_ffn_Wr"], "br": v["L1_ffn_br"],
        "wg": v["L1_ffn_Wg"].transpose(1, 0, 2).reshape(D, -1), "wu": v["L1_ffn_Wu"].transpose(1, 0, 2).reshape(D, -1),
        "wd": v["L1_ffn_Wd"].reshape(PAIRS, P, D).transpose(1, 0, 2),
        "bg": v["L1_ffn_bg"].reshape(PAIRS, P).T, "bu": v["L1_ffn_bu"].reshape(PAIRS, P).T,
        "bd": v["L1_ffn_bd"],
        "wgs": v["L1_ffn_Wg_s"], "wus": v["L1_ffn_Wu_s"], "wds": v["L1_ffn_Wd_s"],
        "bgs": v["L1_ffn_bg_s"].reshape(INNER, 1), "bus": v["L1_ffn_bu_s"].reshape(INNER, 1),
        "bds": v["L1_ffn_bd_s"].reshape(D, 1),
    }
    nc = _bacc.Bacc("TRN2", target_bir_lowering=False, num_devices=1)
    arrays, aps = {}, {}
    for name, x in a.items():
        x = _np.ascontiguousarray(x)
        arrays[f"in_{name}"] = x
        aps[name] = nc.dram_tensor(f"in_{name}", x.shape, _mybir.dt.from_np(x.dtype), kind="ExternalInput").ap()
    out = nc.dram_tensor("out", (CHUNKS, P, TILES, D), _mybir.dt.float32, kind="ExternalOutput").ap()
    l0_and_l1_kernel(nc, aps, out)
    r = _run(nc, [arrays], core_ids=[0])
    got = r.results[0]["out"]
    return got.transpose(0, 2, 1, 3).reshape(BATCHES, SEQ, D)
```

```python
from contextlib import ExitStack

import numpy as np

import concourse.bass as bass
from concourse import mybir

ALU = mybir.AluOpType
ACT = mybir.ActivationFunctionType
F32 = mybir.dt.float32
BF16 = mybir.dt.bfloat16
U32 = mybir.dt.uint32
AX = mybir.AxisListType.X

P = 128
D = 128
BATCHES, SEQ = 8, 256
CHUNK = 512
CB = CHUNK // SEQ
TILES = CHUNK // P
CHUNKS = BATCHES * SEQ // CHUNK
EPS = 1e-5
MASKED = -1e30

OT = 1024 // P
E0, R0 = 8, 16
FB = 512 // P
SCALE0 = 1.0 / 32.0

HEADS, DH = 16, 8
HC = 2 * HEADS
DV = 2 * DH
HR = 3
VW1 = 32
SCALE1 = 1.0 / float(np.sqrt(DH))
SLOTS = 6
NEG_ROW = 96
KROWS = NEG_ROW + 3
LAM0 = 0.8
GROUPS = 4
GH = HEADS // GROUPS
GHC = 2 * GH
E1, INNER = 32, 64
PAIRS = E1 // 2
TOPK = 8

FRONT = ["load", "norm0", "turn0", "keys0", "router0", "inner0", "scores0", "picks0", "probs0"]
FRONT += [f"hidden{f}" for f in range(FB)] + ["out0", "norm1", "turn1", "router1"]
FRONT_TAIL = ["queries1", "keys1", "values1", "weights1"]
MAX_UNITS = 3 * GROUPS
RING = {"turn0": 1, "keys0": 1, "inner0": 1, "scores0": 1, "picks0": 1, "probs0": 1, "out0": 1, "turn1": 1,
        "router1": 1, "queries1": 1, "keys1": 1, "values1": 1, "max": 1, "score": 3,
        **{f"hidden{f}": 1 for f in range(FB)}}
MOE_EARLY = 9


def attention_steps():
    steps = []
    maxima = [[("max", b, g, u) for g in range(GROUPS) for u in range(3)] for b in range(CB)]
    steps += maxima[0]
    for b in range(CB):
        s, v, k = ([(kind, b, g) for g in range(GROUPS)] for kind in ("score", "values", "back"))
        steps += [("minus", b), s[0], s[1], v[0], s[2], k[0], v[1], s[3], k[1], v[2]]
        late = [k[2], v[3], k[3], ("norm", b), ("turn", b)]
        ahead = maxima[b + 1] if b + 1 < CB else []
        for n, step in enumerate(late):
            steps += ahead[2 * n:2 * n + 2] + [step]
        steps += ahead[2 * len(late):]
    return steps


def spread(steps, between):
    out, n = [], 0
    for k, s in enumerate(steps):
        out.append(s)
        while n < len(between) and n * len(steps) < (k + 1) * len(between):
            out.append(between[n])
            n += 1
    return out + between[n:]


def plan(with_front):
    moe = [("moe", j) for j in range(PAIRS + 3)]
    early, late = moe[:MOE_EARLY], moe[MOE_EARLY:]
    front = [("front", f) for f in FRONT] if with_front else []
    tail = [("front", f) for f in FRONT_TAIL] if with_front else []
    return [("begin",)] + spread(attention_steps(), spread(front, early)) + spread(late, tail) + [("end",)]


def units(steps):
    out = []
    for s in steps:
        name = s[1] if s[0] == "front" else s[0]
        for n in range(RING.get(name, 0)):
            out.append((*s, n) if name == "score" else s)
    return out


OPENING = [("front", f) for f in FRONT + FRONT_TAIL]
ROUND = plan(True)
LAST = plan(False)
assert len(units(OPENING)) % 2 == 0 and len(units(ROUND)) % 2 == 0
N_WEIGHTS = 20 + 4 + 2 + 4 + P // DV
N_CONSTS = 11
WB_IN = 32 * PAIRS // 4
QK_IN = 16 * 2 * 3
N_SETUP_VEC = 11
SETUP_LINKS = 4
OPEN_LINKS = 33
ROUND_LINKS = 85


def build(nc, t):
    with ExitStack() as ctx:
        def sb(name, shape, dt=F32):
            return ctx.enter_context(nc.sbuf_tensor(name, shape, dt))

        def sem(name):
            return ctx.enter_context(nc.semaphore(name))

        pairs = [ctx.enter_context(nc.psum_tensor(f"scores{n}", [P, 2, 512], F32)) for n in range(2)]
        single = [ctx.enter_context(nc.psum_tensor(f"bank{n}", [P, 512], F32)) for n in range(4, 8)]
        bank = [pairs[0][:, 0, :], pairs[0][:, 1, :], pairs[1][:, 0, :], pairs[1][:, 1, :]] + [s[:, :] for s in single]

        ident = sb("ident", [P, P])
        identb = sb("identb", [P, P], BF16)
        mask_q = sb("mask_q", [P, 4, P], BF16)
        mask_k = sb("mask_k", [P, 4, P], BF16)
        twos_row = sb("twos_row", [1, P])
        minus_half = sb("minus_half", [P, HC])
        zero = sb("zero", [P, TILES])
        waited = sb("waited", [P, 2])
        iota8 = sb("iota8", [P, E0])
        mt = sb("mt", [P, P])
        vo = sb("vo", [P, P])
        wi_t = sb("wi_t", [P, 512])
        bi = sb("bi", [P, FB])
        wo_t = sb("wo_t", [P, FB, P])
        bo = sb("bo", [1, P])
        la = sb("la", [P, E0 * R0])
        lb = sb("lb", [P, 512])
        gate_w = sb("gate_w", [P, E0])
        gate_b = sb("gate_b", [P, E0])
        wq1 = sb("wq1", [P, 2 * P])
        wk1 = sb("wk1", [P, 2 * P])
        wv1 = sb("wv1", [P, 2 * P])
        wo1 = sb("wo1", [P, 2, P])
        wo1s = sb("wo1s", [P, 2, P])
        rms_col = sb("rms_col", [P, 1])
        lam_in = sb("lam_in", [P, 4, HEADS * DH])
        lam_e = sb("lam_e", [P, 2, HEADS])
        lam = sb("lam", [P, HEADS])
        wr = sb("wr", [P, E1])
        br = sb("br", [P, E1])
        wg = sb("wg", [P, E1 * INNER])
        wu = sb("wu", [P, E1 * INNER])
        wd = sb("wd", [P, PAIRS, P])
        bd = sb("bd", [E1, P])
        bg = sb("bg", [P, PAIRS + 1])
        bgh = sb("bgh", [P, PAIRS + 1])
        bu = sb("bu", [P, PAIRS + 1])
        wgs = sb("wgs", [P, INNER])
        wus = sb("wus", [P, INNER])
        wds = sb("wds", [INNER, P])
        bds = sb("bds", [P, 1])
        bdsh = sb("bdsh", [P, 1])

        x = sb("x", [P, TILES, D])
        stats = sb("stats", [P, TILES, 6])
        mv = sb("mv", [P, TILES, 2])
        vare = sb("vare", [P, TILES])
        rstd = sb("rstd", [P, TILES])
        xn = sb("xn", [P, TILES, D])
        xnt = sb("xnt", [P, CHUNK])
        yk = sb("yk", [P, CHUNK])
        vw = sb("vw", [P, TILES, D])
        nmax0 = sb("nmax0", [P, TILES])
        nbias0 = sb("nbias0", [P, TILES])
        l0 = sb("l0", [P, TILES])
        rl0 = sb("rl0", [P, TILES])
        pt0 = sb("pt0", [P, CB, 3 * P])
        logit = sb("logit", [P, TILES, E0])
        lmax = sb("lmax", [P, TILES])
        lexp = sb("lexp", [P, TILES, E0])
        lsum = sb("lsum", [P, TILES])
        top = sb("top", [P, TILES, 8])
        topi = sb("topi", [P, TILES, 8], U32)
        topf = sb("topf", [P, TILES, 2])
        pick = sb("pick", [P, 2, TILES, E0])
        hvs = sb("hvs", [P, TILES])
        umt = sb("umt", [P, 2, CHUNK])
        ha = sb("ha", [P, FB, CHUNK])
        hb = sb("hb", [P, 2, CHUNK])
        p0 = ha[:, 0:2, :].rearrange("p f (n q) -> p (f n) q", q=SEQ)
        um = hb[:, :, :].rearrange("p j (c e) -> p j c e", c=TILES)
        th0 = xn
        tmp0 = sb("tmp0", [P, TILES, D])
        gate0 = yk[:, :].rearrange("p (c d) -> p c d", d=D)
        x1 = sb("x1", [P, TILES, D])

        xn1 = tmp0
        xnt1n = sb("xnt1n", [P, CHUNK])
        xnt1 = sb("xnt1", [P, CHUNK])
        rlog = sb("rlog", [P, TILES, E1])
        rexp = sb("rexp", [P, TILES, E1])
        aff = sb("aff", [P, TILES, E1])
        top1 = sb("top1", [P, TILES, 8])
        rest1 = sb("rest1", [P, TILES, E1])
        wsum = sb("wsum", [P, TILES])
        wtok = sb("wtok", [P, TILES, E1])
        wt = sb("wt", [E1, CHUNK])
        wb = sb("wb", [P, 2, 2, CHUNK])
        qkf = sb("qkf", [P, 4, CHUNK])
        parts = sb("parts", [P, 3, 4, CHUNK], BF16)
        qa = sb("qa", [KROWS, HC, SEQ], BF16)
        ka = sb("ka", [KROWS, HC, SEQ], BF16)
        v1 = sb("v1", [P, TILES, HEADS, VW1])
        nmax1 = sb("nmax1", [P, TILES, HC])
        mres = sb("mres", [P, TILES, HC])
        mparts = sb("mparts", [P, TILES, 3, HC], BF16)
        mrows = sb("mrows", [3 * HC, CHUNK], BF16)
        pkb = sb("pkb", [P, GHC * (SEQ + P)])
        pk = [parts[:, :, :, :].rearrange("p a f t -> p (a f t)").bitcast(F32), pkb[:, :]]
        pk0 = [r[:, 0:GHC * SEQ].rearrange("p (h q) -> p h q", q=SEQ) for r in pk]
        pk1 = [r[:, GHC * SEQ:GHC * (SEQ + P)].rearrange("p (h q) -> p h q", q=P) for r in pk]
        ot = sb("ot", [P, 2, SEQ])
        rl1 = sb("rl1", [P, 2, 2, GH])
        o12 = sb("o12", [P, 2, 2, GH, DV])
        oc = sb("oc", [P, TILES, HEADS * DV])
        osq = sb("osq", [P, 2, HEADS * DV])
        oms = sb("oms", [P, 2, HEADS])
        orms = sb("orms", [P, 2, HEADS])
        on = sb("on", [P, 2, HEADS * DV])
        oct_ = sb("oct", [P, 2, CHUNK])
        gt = sb("gt", [P, 2, CHUNK])
        gb = sb("gb", [P, 2, CHUNK])
        h1 = sb("h1", [P, HR, CHUNK])
        wstack = ha[:, :, :].rearrange("p f t -> p (f t)").rearrange("p (a c) -> p a c", a=2)
        fth = sb("fth", [P, CHUNK])
        fvh = sb("fvh", [P, CHUNK])
        fg = fvh
        out = sb("out_tok", [P, TILES, D])

        s_weights_in = sem("weights_in")
        s_consts_ready = sem("consts_ready")
        s_wstack_in = sem("wstack_in")
        s_mt_done = sem("mt_done")
        s_vo_done = sem("vo_done")
        s_mt_copied = sem("mt_copied")
        s_vo_copied = sem("vo_copied")
        s_setup_vec = sem("setup_vec")
        s_setup_act = sem("setup_act")
        s_lam_exp = sem("lam_exp")
        s_x_in = sem("x_in")
        s_var0 = sem("var0")
        s_rstd0 = sem("rstd0")
        s_xn0 = sem("xn0")
        s_xnt_ps = sem("xnt_ps")
        s_xnt_sb = sem("xnt_sb")
        s_yk_ps = sem("yk_ps")
        s_yk_sb = sem("yk_sb")
        s_vw_ps = sem("vw_ps")
        s_vw_sb = sem("vw_sb")
        s_s0_ps = sem("s0_ps")
        s_nb0 = sem("nb0")
        s_p0_done = sem("p0_done")
        s_pt_ps = sem("pt_ps")
        s_pt_sb = sem("pt_sb")
        s_att_ps = sem("att_ps")
        s_logits_ps = sem("logits_ps")
        s_u_ps = sem("u_ps")
        s_lsub = sem("lsub")
        s_lexp_done = sem("lexp_done")
        s_um_done = sem("um_done")
        s_umt_ps = sem("umt_ps")
        s_umt_sb = sem("umt_sb")
        s_inter_ps = sem("inter_ps")
        s_ha_done = sem("ha_done")
        s_hb_done = sem("hb_done")
        s_hsum_done = sem("hsum_done")
        s_z_ps = sem("z_ps")
        s_th0_done = sem("th0_done")
        s_var1 = sem("var1")
        s_rstd1 = sem("rstd1")
        s_xn1_done = sem("xn1_done")
        s_xnt1_ps = sem("xnt1_ps")
        s_xnt1_sb = sem("xnt1_sb")
        s_router_ps = sem("router_ps")
        s_rl_done = sem("rl_done")
        s_rexp_done = sem("rexp_done")
        s_w_done = sem("w_done")
        s_wt_ps = sem("wt_ps")
        s_wt_sb = sem("wt_sb")
        s_wt_stored = sem("wt_stored")
        s_wb_in0 = sem("wb_in0")
        s_wb_in1 = sem("wb_in1")
        s_qk_ps = sem("qk_ps")
        s_qkf_done = sem("qkf_done")
        s_part1 = sem("part1")
        s_part2 = sem("part2")
        s_part3 = sem("part3")
        s_parts_stored = sem("parts_stored")
        s_qk_in0 = sem("qk_in0")
        s_qk_in1 = sem("qk_in1")
        s_qk_in2 = sem("qk_in2")
        s_qk_in3 = sem("qk_in3")
        s_v_ps = sem("v_ps")
        s_v_sb = sem("v_sb")
        s_max_ps = sem("max_ps")
        s_nmax_done = sem("nmax_done")
        s_mp_done = sem("mp_done")
        s_mrow_ps = sem("mrow_ps")
        s_mrow_sb = sem("mrow_sb")
        s_mrow_in = sem("mrow_in")
        s_gate_ps = sem("gate_ps")
        s_gate_act = sem("gate_act")
        s_ga_mid = sem("ga_mid")
        s_ga_done = sem("ga_done")
        s_up_ps = sem("up_ps")
        s_h_done = sem("h_done")
        s_acc_ps = sem("acc_ps")
        s_sc_ps = sem("sc_ps")
        s_pk_done = sem("pk_done")
        s_pv_ps = sem("pv_ps")
        s_ot_sb = sem("ot_sb")
        s_ot_ps = sem("ot_ps")
        s_oc_done = sem("oc_done")
        s_ms_done = sem("ms_done")
        s_orms_done = sem("orms_done")
        s_on_done = sem("on_done")
        s_oct_ps = sem("oct_ps")
        s_oct_sb = sem("oct_sb")
        s_s1_ps = sem("s1_ps")
        s_fth_done = sem("fth_done")
        s_fg_done = sem("fg_done")
        s_fin_ps = sem("fin_ps")
        s_keep_done = sem("keep_done")
        s_cur_done = sem("cur_done")
        s_z_read = sem("z_read")
        s_out_done = sem("out_done")
        s_out_stored = sem("out_stored")
        s_dve_link = sem("dve_link")
        s_qk_first = sem("qk_first")
        s_qk_in = [s_qk_in0, s_qk_in1, s_qk_in2, s_qk_in3]
        s_wb_in = [s_wb_in0, s_wb_in1]

        PER = dict(x_in=16, var0=1, rstd0=1, xn0=TILES, xnt_ps=1, xnt_sb=1, yk_ps=1, yk_sb=1, vw_ps=1, vw_sb=1,
                   s0_ps=CB, nb0=1, p0_done=TILES, pt_ps=CB, pt_sb=CB, att_ps=1, logits_ps=1, u_ps=1, lsub=1,
                   lexp_done=1, um_done=2, umt_ps=2, umt_sb=2, inter_ps=2 * FB, ha_done=FB, hb_done=FB,
                   hsum_done=FB, z_ps=1, th0_done=TILES, var1=1, rstd1=1, xn1_done=TILES, xnt1_ps=1,
                   xnt1_sb=1, router_ps=1, rl_done=1, rexp_done=1, w_done=1, wt_ps=1, wt_sb=1, wt_stored=16,
                   qk_ps=4, qkf_done=4, part1=4, part2=4, part3=4, parts_stored=16 * 12,
                   v_ps=2, v_sb=2, max_ps=CB * MAX_UNITS, nmax_done=CB * MAX_UNITS,
                   mp_done=CB, mrow_ps=CB, mrow_sb=CB, mrow_in=16 * 3 * CB,
                   gate_ps=PAIRS + 1, gate_act=2 * (PAIRS + 1), ga_mid=PAIRS + 1, ga_done=PAIRS,
                   up_ps=PAIRS + 1, h_done=PAIRS + 1, acc_ps=PAIRS + 1, sc_ps=CB * GROUPS * 3, pk_done=CB * GROUPS * 3,
                   pv_ps=CB * GROUPS, ot_sb=CB * GROUPS, ot_ps=CB * GROUPS, oc_done=CB * GROUPS, ms_done=CB,
                   orms_done=CB, on_done=CB, oct_ps=CB, oct_sb=CB, s1_ps=1, fth_done=2, fg_done=1,
                   fin_ps=1, out_done=1, out_stored=16, keep_done=1, cur_done=1, z_read=1)

        def at(i, name, k):
            return i * PER[name] + k

        def ring_free(pe, i, c, before):
            kind = before[1] if before[0] == "front" else before[0]
            if kind == "max":
                _, b, g, u = before
                pe.wait_ge(s_nmax_done, at(i, "nmax_done", b * MAX_UNITS + 3 * g + u + 1))
            elif kind == "score":
                _, b, g, u = before
                pe.wait_ge(s_pk_done, at(i, "pk_done", 3 * (b * GROUPS + g) + u + 1))
            elif kind == "turn0":
                pe.wait_ge(s_xnt_sb, at(c, "xnt_sb", 1))
            elif kind == "keys0":
                pe.wait_ge(s_yk_sb, at(c, "yk_sb", 1))
                pe.wait_ge(s_lsub, at(c, "lsub", 1))
            elif kind == "inner0":
                pe.wait_ge(s_vw_sb, at(c, "vw_sb", 1))
                pe.wait_ge(s_um_done, at(c, "um_done", 2))
            elif kind == "scores0":
                pe.wait_ge(s_p0_done, at(c, "p0_done", TILES))
            elif kind == "picks0":
                pe.wait_ge(s_umt_sb, at(c, "umt_sb", 2))
            elif kind == "probs0":
                pe.wait_ge(s_pt_sb, at(c, "pt_sb", CB))
            elif kind.startswith("hidden"):
                f = int(kind[6:])
                pe.wait_ge(s_ha_done, at(c, "ha_done", f + 1))
                pe.wait_ge(s_hb_done, at(c, "hb_done", f + 1))
            elif kind == "out0":
                pe.wait_ge(s_z_read, at(c, "z_read", 1))
            elif kind == "turn1":
                pe.wait_ge(s_xnt1_sb, at(c, "xnt1_sb", 1))
            elif kind == "router1":
                pe.wait_ge(s_rl_done, at(c, "rl_done", 1))
            elif kind == "queries1":
                pe.wait_ge(s_part1, at(c, "part1", 2))
            elif kind == "keys1":
                pe.wait_ge(s_part1, at(c, "part1", 4))
            elif kind == "values1":
                pe.wait_ge(s_v_sb, at(c, "v_sb", 2))

        block = ctx.enter_context(nc.Block())

        n_weights = [0]

        @block.sync
        def _(sp):
            def load(dst, src):
                sp.dma_start(dst, src).then_inc(s_weights_in, 16)
                n_weights[0] += 1

            sp.dma_start(wstack[:, :, :], t["wkq"]).then_inc(s_wstack_in, 16)
            sp.wait_ge(s_mt_done, 1)
            sp.dma_start(wstack[:, :, :], t["wvo"]).then_inc(s_wstack_in, 16)
            for dst, name in ((wi_t, "wi_t"), (bi, "bi"), (wo_t, "wo_t"), (la, "la"), (lb, "lb"),
                              (gate_w, "gate_w"), (bo, "bo"), (wq1, "wq1"), (wk1, "wk1"), (wv1, "wv1"),
                              (wo1, "wo1"), (wr, "wr"), (wg, "wg"), (wu, "wu"), (wd, "wd"), (bd, "bd"),
                              (wgs, "wgs"), (wus, "wus"), (wds, "wds"), (bds, "bds")):
                load(dst[tuple(slice(None) for _ in dst.shape)], t[name])
            load(bg[:, 0:PAIRS], t["bg"])
            load(bu[:, 0:PAIRS], t["bu"])
            load(bg[0:INNER, PAIRS:], t["bgs"])
            load(bu[0:INNER, PAIRS:], t["bus"])
            load(gate_b[:, :], t["gate_b"].partition_broadcast(P))
            load(br[:, :], t["br"].partition_broadcast(P))
            for n, name in enumerate(("lq1", "lk1", "lq2", "lk2")):
                load(lam_in[:, n, :], t[name].partition_broadcast(P))
            for g in range(P // DV):
                load(rms_col[g * DV:(g + 1) * DV, :], t["rms"])
            assert n_weights[0] == N_WEIGHTS

            def load_qk(b, g0, groups, signal):
                for n, dst in enumerate((qa, ka)):
                    row = 0
                    for width in (3, 2, 1):
                        first = 0 if n == 0 else 3 - width
                        src = t["parts_dram"][n, g0 * GHC:(g0 + groups) * GHC, first * DH:(first + width) * DH, b * SEQ:(b + 1) * SEQ]
                        sp.dma_start(dst[row:row + width * DH, g0 * GHC:(g0 + groups) * GHC, :],
                                     src.rearrange("h r t -> r h t")).then_inc(signal, 16)
                        row += width * DH

            def load_wb(k):
                src = t["wt_dram"].rearrange("(j e) t -> e j t", e=2)
                for e in range(2):
                    sp.dma_start(wb[e * INNER:(e + 1) * INNER, k % 2, :, :],
                                 src[e, 2 * k:2 * k + 2, :].partition_broadcast(INNER)).then_inc(s_wb_in[k % 2], 16)

            def steps(names, c, i):
                for step in names:
                    if step == ("front", "load"):
                        sp.dma_start(x[:, :, :], t["x"][bass.ds(c, 1)].rearrange("c p t d -> (c p) t d")).then_inc(s_x_in, 16)
                    elif step == ("front", "values1"):
                        sp.wait_ge(s_part1, at(c, "part1", 4))
                        sp.wait_ge(s_part2, at(c, "part2", 4))
                        sp.wait_ge(s_part3, at(c, "part3", 4))
                        for n in range(2):
                            for a in range(3):
                                for f in range(2):
                                    r = a if n == 0 else 2 - a
                                    dst = t["parts_dram"][n, f * 2 * GHC:(f + 1) * 2 * GHC, r * DH:(r + 1) * DH, :]
                                    sp.dma_start(dst, parts[:, a, 2 * n + f, :]).then_inc(s_parts_stored, 16)
                        sp.wait_ge(s_parts_stored, at(c, "parts_stored", 16 * 12))
                        load_qk(0, 0, GROUPS, s_qk_first)
                    elif step == ("front", "weights1"):
                        sp.wait_ge(s_wt_sb, at(c, "wt_sb", 1))
                        if i is not None:
                            sp.wait_ge(s_wb_in0, i * WB_IN + WB_IN)
                            sp.wait_ge(s_wb_in1, i * WB_IN + WB_IN)
                        sp.dma_start(t["wt_dram"], wt[:, :]).then_inc(s_wt_stored, 16)
                    elif step[0] == "begin":
                        sp.wait_ge(s_wt_stored, at(i, "wt_stored", 16))
                        load_wb(0)
                        load_wb(1)
                    elif step[0] == "moe" and step[1] % 2 == 0 and 4 <= step[1] + 2 < PAIRS:
                        sp.wait_ge(s_ga_done, at(i, "ga_done", step[1]))
                        load_wb(step[1] // 2 + 1)
                    elif step[0] == "score" and step[1] == 0:
                        g = step[2]
                        sp.wait_ge(s_sc_ps, at(i, "sc_ps", 3 * (g + 1)))
                        load_qk(1, g, 1, s_qk_in[g])
                    elif step[0] == "end":
                        sp.wait_ge(s_out_done, i + 2)
                        sp.dma_start(t["out"][bass.ds(i, 1)].rearrange("c p t d -> (c p) t d"), out[:, :, :]).then_inc(s_out_stored, 16)

            steps(OPENING, 0, None)
            with sp.Fori(0, CHUNKS - 1) as i:
                steps(ROUND, i + 1, i)
            steps(LAST, None, CHUNKS - 1)
            sp.wait_ge(s_out_stored, at(CHUNKS - 1, "out_stored", 16))

        wall = 16 * N_WEIGHTS

        @block.tensor
        def _(pe):
            mm = nc.tensor.matmul

            for n, (b, done) in enumerate(((4, s_mt_done), (5, s_vo_done))):
                pe.wait_ge(s_wstack_in, 16 * (n + 1))
                for o in range(OT):
                    last = mm(bank[b][:, 0:P], wstack[:, 0, o * P:(o + 1) * P], wstack[:, 1, o * P:(o + 1) * P],
                              start=(o == 0), stop=(o == OT - 1))
                last.then_inc(done, 1)
            pe.wait_ge(s_weights_in, wall)
            pe.wait_ge(s_consts_ready, N_CONSTS)
            pe.wait_ge(s_setup_vec, N_SETUP_VEC)
            pe.wait_ge(s_mt_copied, 1)
            pe.wait_ge(s_vo_copied, 1)

            def front(name, c, i, pair):
                one, two = pairs[pair][:, 0, :], pairs[pair][:, 1, :]
                if name == "turn0":
                    pe.wait_ge(s_xn0, at(c, "xn0", TILES))
                    for k in range(TILES):
                        last = nc.tensor.transpose(one[:, k * P:(k + 1) * P], xn[:, k, :], ident[:, :])
                    last.then_inc(s_xnt_ps, 1)
                elif name == "keys0":
                    pe.wait_ge(s_xnt_sb, at(c, "xnt_sb", 1))
                    for k in range(TILES):
                        last = mm(two[:, k * E0:(k + 1) * E0], xnt[:, k * P:(k + 1) * P], gate_w[:, :], start=(k == 0), stop=True, skip_group_check=True)
                    last.then_inc(s_logits_ps, 1)
                    mm(one, mt[:, :], xnt[:, :], start=True, stop=True).then_inc(s_yk_ps, 1)
                elif name == "inner0":
                    for k in range(TILES):
                        last = mm(one[:, k * P:(k + 1) * P], xnt[:, k * P:(k + 1) * P], la[:, :], start=(k == 0), stop=True, skip_group_check=True)
                    last.then_inc(s_u_ps, 1)
                    for k in range(TILES):
                        last = mm(two[:, k * P:(k + 1) * P], xnt[:, k * P:(k + 1) * P], vo[:, :], start=(k == 0), stop=True, skip_group_check=True)
                    last.then_inc(s_vw_ps, 1)
                elif name == "scores0":
                    pe.wait_ge(s_yk_sb, at(c, "yk_sb", 1))
                    for b in range(CB):
                        s = pairs[pair][:, b, :]
                        base = b * SEQ
                        mm(s[:, 0:P], identb[:, :], mask_q[:, 0, :], start=True, stop=False, skip_group_check=True)
                        mm(s[:, 2 * P:3 * P], identb[:, :], mask_q[:, 0, :], start=False, stop=False, skip_group_check=True)
                        mm(s[:, 0:P], xnt[:, base:base + P], yk[:, base:base + P], start=False, stop=True, skip_group_check=True)
                        mm(s[:, P:3 * P], xnt[:, base + P:base + SEQ], yk[:, base:base + SEQ], start=False, stop=True,
                           skip_group_check=True).then_inc(s_s0_ps, 1)
                elif name == "picks0":
                    for j in range(2):
                        pe.wait_ge(s_um_done, at(c, "um_done", j + 1))
                        for k in range(TILES):
                            last = nc.tensor.transpose(pairs[pair][:, j, k * P:(k + 1) * P], um[:, j, k, :], ident[:, :])
                        last.then_inc(s_umt_ps, 1)
                elif name == "probs0":
                    for b in range(CB):
                        pe.wait_ge(s_p0_done, at(c, "p0_done", 2 * b + 2))
                        s = pairs[pair][:, b, :]
                        nc.tensor.transpose(s[:, 0:P], p0[:, 2 * b, 0:P], ident[:, :])
                        nc.tensor.transpose(s[:, P:2 * P], p0[:, 2 * b + 1, 0:P], ident[:, :])
                        nc.tensor.transpose(s[:, 2 * P:3 * P], p0[:, 2 * b + 1, P:SEQ], ident[:, :]).then_inc(s_pt_ps, 1)
                elif name.startswith("hidden"):
                    f = int(name[6:])
                    for j in range(2):
                        if f == 0:
                            pe.wait_ge(s_umt_sb, at(c, "umt_sb", j + 1))
                        mm(pairs[pair][:, j, :], wi_t[:, f * P:(f + 1) * P], xnt[:, :], start=True, stop=False)
                        mm(pairs[pair][:, j, :], lb[:, f * P:(f + 1) * P], umt[:, j, :], start=False, stop=True).then_inc(s_inter_ps, 1)
                elif name == "out0":
                    pe.wait_ge(s_vw_sb, at(c, "vw_sb", 1))
                    for b in range(CB):
                        pe.wait_ge(s_pt_sb, at(c, "pt_sb", b + 1))
                        k = 2 * b
                        mm(one[:, k * P:(k + 1) * P], pt0[:, b, 0:P], vw[:, k, :], start=(b == 0), stop=True, skip_group_check=True)
                        mm(one[:, (k + 1) * P:(k + 2) * P], pt0[:, b, P:2 * P], vw[:, k, :], start=False, stop=False, skip_group_check=True)
                        last = mm(one[:, (k + 1) * P:(k + 2) * P], pt0[:, b, 2 * P:3 * P], vw[:, k + 1, :], start=False, stop=True, skip_group_check=True)
                    last.then_inc(s_att_ps, 1)
                    pe.wait_ge(s_hsum_done, at(c, "hsum_done", FB))
                    for k in range(TILES):
                        z = two[:, k * P:(k + 1) * P]
                        mm(z, twos_row[:, :], bo[:, :], start=(k == 0), stop=False, skip_group_check=True)
                        for f in range(FB):
                            last = mm(z, ha[:, f, k * P:(k + 1) * P], wo_t[:, f, :], start=False, stop=(f == FB - 1), skip_group_check=True)
                    last.then_inc(s_z_ps, 1)
                elif name == "turn1":
                    pe.wait_ge(s_xn1_done, at(c, "xn1_done", TILES))
                    for k in range(TILES):
                        last = nc.tensor.transpose(one[:, k * P:(k + 1) * P], xn1[:, k, :], ident[:, :])
                    last.then_inc(s_xnt1_ps, 1)
                elif name == "router1":
                    pe.wait_ge(s_xnt1_sb, at(c, "xnt1_sb", 1))
                    for k in range(TILES):
                        last = mm(one[:, k * E1:(k + 1) * E1], xnt1n[:, k * P:(k + 1) * P], wr[:, :], start=(k == 0), stop=True, skip_group_check=True)
                    last.then_inc(s_router_ps, 1)
                elif name in ("queries1", "keys1"):
                    w = wq1 if name == "queries1" else wk1
                    for f in range(2):
                        mm(pairs[pair][:, f, :], w[:, f * P:(f + 1) * P], xnt1n[:, :], start=True, stop=True).then_inc(s_qk_ps, 1)
                elif name == "values1":
                    for k in range(TILES):
                        last = mm(pairs[pair][:, k // 2, (k % 2) * 2 * P:(k % 2 + 1) * 2 * P], xnt1n[:, k * P:(k + 1) * P], wv1[:, :],
                                  start=(k % 2 == 0), stop=True, skip_group_check=True)
                        if k % 2:
                            last.then_inc(s_v_ps, 1)
                elif name == "weights1":
                    pe.wait_ge(s_w_done, at(c, "w_done", 1))
                    if i is not None:
                        pe.wait_ge(s_oct_sb, at(i, "oct_sb", CB))
                    for k in range(TILES):
                        last = nc.tensor.transpose(bank[4][0:E1, k * P:(k + 1) * P], wtok[:, k, :], ident[:, :])
                    last.then_inc(s_wt_ps, 1)

            def up(i, j):
                if j:
                    pe.wait_ge(s_h_done, at(i, "h_done", j))
                if j == PAIRS:
                    m = mm(bank[6][0:INNER, :], wus[:, :], xnt1[:, :], start=True, stop=True)
                else:
                    m = mm(bank[6], wu[:, j * P:(j + 1) * P], xnt1[:, :], start=True, stop=True)
                m.then_inc(s_up_ps, 1)

            def gate(i, j):
                if j:
                    pe.wait_ge(s_gate_act, at(i, "gate_act", 2 * j))
                else:
                    pe.wait_ge(s_out_done, i + 1)
                    pe.wait_ge(s_cur_done, at(i, "cur_done", 1))
                if j == PAIRS:
                    m = mm(bank[5][0:INNER, :], wgs[:, :], xnt1[:, :], start=True, stop=True)
                else:
                    m = mm(bank[5], wg[:, j * P:(j + 1) * P], xnt1[:, :], start=True, stop=True)
                m.then_inc(s_gate_ps, 1)

            def down(i, j):
                pe.wait_ge(s_h_done, at(i, "h_done", j + 1))
                if j == 0:
                    mm(bank[7], bd[:, :], wt[:, :], start=True, stop=False)
                if j == PAIRS:
                    m = mm(bank[7], wds[:, :], h1[0:INNER, j % HR, :], start=False, stop=True)
                else:
                    m = mm(bank[7], wd[:, j, :], h1[:, j % HR, :], start=False, stop=False)
                m.then_inc(s_acc_ps, 1)

            def scores(pair, row, cols, stat, move, rows, hc0, tile0, width):
                per = 512 // cols
                mask = mask_q if stat is qa else mask_k
                for n in range(2):
                    s = pairs[pair][:, n, :].rearrange("p (h c) -> p h c", c=cols)
                    diag = s[:, :, (cols - P if stat is qa else 0):(cols if stat is qa else P)]
                    mm(diag, identb[:, :], mask[:, 0:per, :], start=True, stop=False, skip_group_check=True)
                    for h in range(per):
                        hc = hc0 + n * per + h
                        last = mm(s[:, h, :], stat[0:rows, hc, row:row + P], move[0:rows, hc, tile0:tile0 + width],
                                  start=False, stop=True, skip_group_check=True)
                return last

            def steps(names, c, i, ring):
                taken = 0
                order = ring + units(names)
                first_c = c if i is None else i

                def take():
                    nonlocal taken
                    if order[taken] is not None:
                        ring_free(pe, i, first_c if taken < 2 else c, order[taken])
                    taken += 1
                    return (taken - 1) % 2

                for step in names:
                    if step[0] == "front":
                        if step[1] in ("load", "norm0", "router0", "norm1"):
                            continue
                        front(step[1], c, i, take() if step[1] in RING else 0)
                    elif step[0] == "moe":
                        j = step[1]
                        if j <= PAIRS:
                            gate(i, j)
                        if j >= 2:
                            down(i, j - 2)
                        if 1 <= j <= PAIRS + 1:
                            up(i, j - 1)
                    elif step[0] == "max":
                        _, b, g, u = step
                        if u == 0:
                            if b == 0:
                                pe.wait_ge(s_qk_first, i * QK_IN + QK_IN)
                            else:
                                pe.wait_ge(s_qk_in[g], i * QK_IN + QK_IN)
                        pair = take()
                        if u == 0:
                            last = scores(pair, 0, P, qa, ka, NEG_ROW, GHC * g, 0, P)
                        else:
                            last = scores(pair, P, SEQ, qa, ka, NEG_ROW, GHC * g + 4 * (u - 1), 0, SEQ)
                        last.then_inc(s_max_ps, 1)
                    elif step[0] == "minus":
                        b = step[1]
                        pe.wait_ge(s_mp_done, at(i, "mp_done", b + 1))
                        if b:
                            pe.wait_ge(s_oct_sb, at(i, "oct_sb", b))
                        for q in range(2):
                            last = mm(bank[4][0:3 * HC, q * P:(q + 1) * P],
                                      mparts[:, 2 * b + q, :, :].rearrange("p a h -> p (a h)"), identb[:, :],
                                      start=(q == 0), stop=True, skip_group_check=True)
                        last.then_inc(s_mrow_ps, 1)
                    elif step[0] == "score":
                        _, b, g = step
                        if g == 0:
                            pe.wait_ge(s_mrow_in, at(i, "mrow_in", 16 * 3 * (b + 1)))
                        for u in range(3):
                            pair = take()
                            if u < 2:
                                last = scores(pair, 0, SEQ, ka, qa, KROWS, g * GHC + 4 * u, 0, SEQ)
                            else:
                                last = scores(pair, P, P, ka, qa, KROWS, g * GHC, P, P)
                            last.then_inc(s_sc_ps, 1)
                    elif step[0] == "values":
                        _, b, g = step
                        n = b * GROUPS + g
                        if g == 0:
                            pe.wait_ge(s_mrow_sb, at(i, "mrow_sb", b + 1))
                        else:
                            pe.wait_ge(s_oc_done, at(i, "oc_done", n))
                        pe.wait_ge(s_pk_done, at(i, "pk_done", 3 * n + 2))
                        o = bank[4].rearrange("p (c q) -> p c q", c=2)
                        for hh in range(GH):
                            head = g * GH + hh
                            mm(o[32 * hh:32 * hh + 32, :, :], v1[:, 2 * b, head, :], pk0[g % 2][:, 2 * hh:2 * hh + 2, :],
                               start=True, stop=False, skip_group_check=True)
                        pe.wait_ge(s_pk_done, at(i, "pk_done", 3 * n + 3))
                        for hh in range(GH):
                            head = g * GH + hh
                            last = mm(o[32 * hh:32 * hh + 32, :, P:SEQ], v1[:, 2 * b + 1, head, :], pk1[g % 2][:, 2 * hh:2 * hh + 2, :],
                                      start=False, stop=True, skip_group_check=True)
                        last.then_inc(s_pv_ps, 1)
                    elif step[0] == "back":
                        _, b, g = step
                        pe.wait_ge(s_ot_sb, at(i, "ot_sb", b * GROUPS + g + 1))
                        for q in range(2):
                            for k in range(2):
                                n = 2 * q + k
                                last = nc.tensor.transpose(bank[4][:, n * P:(n + 1) * P], ot[:, k, q * P:(q + 1) * P], ident[:, :])
                        last.then_inc(s_ot_ps, 1)
                    elif step[0] == "turn":
                        b = step[1]
                        pe.wait_ge(s_on_done, at(i, "on_done", b + 1))
                        for q in range(2):
                            for f in range(2):
                                n = 2 * f + q
                                last = nc.tensor.transpose(bank[4][:, n * P:(n + 1) * P], on[:, q, f * P:(f + 1) * P], ident[:, :])
                        last.then_inc(s_oct_ps, 1)
                    elif step[0] == "end":
                        pe.wait_ge(s_oct_sb, at(i, "oct_sb", CB))
                        if c is not None:
                            pe.wait_ge(s_wt_sb, at(c, "wt_sb", 1))
                        for f in range(2):
                            last = mm(bank[4], wo1s[:, f, :], oct_[:, f, :], start=(f == 0), stop=(f == 1))
                        last.then_inc(s_s1_ps, 1)
                        pe.wait_ge(s_fg_done, at(i, "fg_done", 1))
                        for k in range(TILES):
                            last = nc.tensor.transpose(bank[5][:, k * P:(k + 1) * P], fg[:, k * P:(k + 1) * P], ident[:, :])
                        last.then_inc(s_fin_ps, 1)

            steps(OPENING, 0, None, [None, None])
            with pe.Fori(0, CHUNKS - 1) as i:
                steps(ROUND, i + 1, i, units(OPENING)[-2:])
            assert units(OPENING)[-2:] == units(ROUND)[-2:]
            steps(LAST, None, CHUNKS - 1, units(ROUND)[-2:])

        @block.scalar
        def _(act):
            A = nc.scalar.activation

            act.wait_ge(s_mt_done, 1)
            A(mt[:, :], bank[4][:, 0:P], ACT.Copy).then_inc(s_mt_copied, 1)
            act.wait_ge(s_vo_done, 1)
            A(vo[:, :], bank[5][:, 0:P], ACT.Copy).then_inc(s_vo_copied, 1)
            act.wait_ge(s_lam_exp, 1)
            A(lam_e[:, :, :], lam_e[:, :, :], ACT.Exp).then_inc(s_setup_act, 1)

            def front(name, c, i, pair):
                if name == "turn0":
                    act.wait_ge(s_xnt_ps, at(c, "xnt_ps", 1))
                    A(xnt[:, :], pairs[pair][:, 0, :], ACT.Copy).then_inc(s_xnt_sb, 1)
                elif name == "keys0":
                    act.wait_ge(s_yk_ps, at(c, "yk_ps", 1))
                    A(yk[:, :], pairs[pair][:, 0, :], ACT.Copy).then_inc(s_yk_sb, 1)
                elif name == "router0":
                    act.wait_ge(s_lsub, at(c, "lsub", 1))
                    A(lexp[:, :, :], logit[:, :, :], ACT.Exp).then_inc(s_lexp_done, 1)
                elif name == "inner0":
                    act.wait_ge(s_vw_ps, at(c, "vw_ps", 1))
                    A(vw[:, :, :], pairs[pair][:, 1, :].rearrange("p (c d) -> p c d", d=D), ACT.Copy).then_inc(s_vw_sb, 1)
                elif name == "scores0":
                    act.wait_ge(s_nb0, at(c, "nb0", 1))
                    for k in range(TILES):
                        w = P if k % 2 == 0 else SEQ
                        o = 0 if k % 2 == 0 else P
                        A(p0[:, k, 0:w], pairs[pair][:, k // 2, o:o + w], ACT.Exp, bias=nbias0[:, k:k + 1], scale=SCALE0,
                          accum_out=l0[:, k:k + 1]).then_inc(s_p0_done, 1)
                elif name == "picks0":
                    for j in range(2):
                        act.wait_ge(s_umt_ps, at(c, "umt_ps", j + 1))
                        A(umt[:, j, :], pairs[pair][:, j, :], ACT.Copy).then_inc(s_umt_sb, 1)
                elif name == "probs0":
                    for b in range(CB):
                        act.wait_ge(s_pt_ps, at(c, "pt_ps", b + 1))
                        A(pt0[:, b, :], pairs[pair][:, b, 0:3 * P], ACT.Copy).then_inc(s_pt_sb, 1)
                elif name.startswith("hidden"):
                    f = int(name[6:])
                    act.wait_ge(s_inter_ps, at(c, "inter_ps", 2 * f + 1))
                    A(ha[:, f, :], pairs[pair][:, 0, :], ACT.Relu, bias=bi[:, f:f + 1]).then_inc(s_ha_done, 1)
                elif name == "out0":
                    act.wait_ge(s_z_ps, at(c, "z_ps", 1))
                    for k in range(TILES):
                        A(th0[:, k, :], pairs[pair][:, 1, k * P:(k + 1) * P], ACT.Tanh, scale=hvs[:, k:k + 1]).then_inc(s_th0_done, 1)
                elif name == "turn1":
                    act.wait_ge(s_xnt1_ps, at(c, "xnt1_ps", 1))
                    A(xnt1n[:, :], pairs[pair][:, 0, :], ACT.Copy).then_inc(s_xnt1_sb, 1)
                elif name == "router1":
                    act.wait_ge(s_rl_done, at(c, "rl_done", 1))
                    A(rexp[:, :, :], rlog[:, :, :], ACT.Exp, scale=-1.0).then_inc(s_rexp_done, 1)
                elif name in ("queries1", "keys1"):
                    if i is not None and name == "queries1":
                        act.wait_ge(s_pv_ps, at(i, "pv_ps", CB * GROUPS))
                    for f in range(2):
                        n = f if name == "queries1" else 2 + f
                        act.wait_ge(s_qk_ps, at(c, "qk_ps", n + 1))
                        A(qkf[:, n, :], pairs[pair][:, f, :], ACT.Copy).then_inc(s_qkf_done, 1)
                        A(parts[:, 0, n, :], pairs[pair][:, f, :], ACT.Copy).then_inc(s_part1, 1)
                elif name == "weights1":
                    if i is not None:
                        act.wait_ge(s_acc_ps, at(i, "acc_ps", 1))
                    act.wait_ge(s_wt_ps, at(c, "wt_ps", 1))
                    A(wt[:, :], bank[4][0:E1, :], ACT.Copy).then_inc(s_wt_sb, 1)

            def steps(names, c, i):
                taken = 0
                for step in names:
                    name = step[1] if step[0] == "front" else step[0]
                    pair = taken % 2
                    if step[0] == "front":
                        front(name, c, i, pair)
                    elif step[0] == "begin":
                        A(xnt1[:, :], xnt1n[:, :], ACT.Copy).then_inc(s_cur_done, 1)
                    elif step[0] == "moe":
                        j = step[1]
                        if j <= PAIRS:
                            rows = INNER if j == PAIRS else P
                            act.wait_ge(s_gate_ps, at(i, "gate_ps", j + 1))
                            if j >= 2:
                                act.wait_ge(s_h_done, at(i, "h_done", j - 1))
                            A(gt[0:rows, j % 2, :], bank[5][0:rows, :], ACT.Tanh, bias=bgh[0:rows, j:j + 1], scale=0.5).then_inc(s_gate_act, 1)
                            A(gb[0:rows, j % 2, :], bank[5][0:rows, :], ACT.Identity, bias=bg[0:rows, j:j + 1]).then_inc(s_gate_act, 1)
                    elif step[0] == "minus":
                        b = step[1]
                        act.wait_ge(s_mrow_ps, at(i, "mrow_ps", b + 1))
                        A(mrows[:, b * SEQ:(b + 1) * SEQ], bank[4][0:3 * HC, 0:SEQ], ACT.Copy).then_inc(s_mrow_sb, 1)
                        act.wait_ge(s_mrow_sb, at(i, "mrow_sb", b + 1))
                        for a in range(3):
                            act.dma_start(qa[NEG_ROW + a:NEG_ROW + a + 1, :, :],
                                          mrows[a * HC:(a + 1) * HC, b * SEQ:(b + 1) * SEQ]).then_inc(s_mrow_in, 16)
                    elif step[0] == "score":
                        _, b, g = step
                        n = b * GROUPS + g
                        if n >= 2:
                            act.wait_ge(s_pv_ps, at(i, "pv_ps", n - 1))
                        for u in range(3):
                            act.wait_ge(s_sc_ps, at(i, "sc_ps", 3 * n + u + 1))
                            src = pairs[(taken + u) % 2][:, :, :]
                            if u < 2:
                                dst = pk0[g % 2][:, 4 * u:4 * u + 4, :]
                                src = src.rearrange("p n (h c) -> p (n h) c", c=SEQ)
                            else:
                                dst = pk1[g % 2]
                                src = src.rearrange("p n (h c) -> p (n h) c", c=P)
                            A(dst, src, ACT.Exp, scale=SCALE1).then_inc(s_pk_done, 1)
                    elif step[0] == "values":
                        n = step[1] * GROUPS + step[2]
                        act.wait_ge(s_pv_ps, at(i, "pv_ps", n + 1))
                        if n:
                            act.wait_ge(s_ot_ps, at(i, "ot_ps", n))
                        A(ot[:, :, :], bank[4].rearrange("p (c q) -> p c q", c=2), ACT.Copy).then_inc(s_ot_sb, 1)
                    elif step[0] == "turn":
                        b = step[1]
                        act.wait_ge(s_oct_ps, at(i, "oct_ps", b + 1))
                        A(oct_[:, :, b * SEQ:(b + 1) * SEQ], bank[4].rearrange("p (f q) -> p f q", f=2), ACT.Copy).then_inc(s_oct_sb, 1)
                    elif step[0] == "end":
                        act.wait_ge(s_acc_ps, at(i, "acc_ps", PAIRS + 1))
                        A(fth[:, :], bank[7], ACT.Tanh, bias=bdsh[:, :], scale=0.5).then_inc(s_fth_done, 1)
                        A(fvh[:, :], bank[7], ACT.Identity, bias=bdsh[:, :], scale=0.5).then_inc(s_fth_done, 1)
                    taken += RING.get(name, 0)

            steps(OPENING, 0, None)
            with act.Fori(0, CHUNKS - 1) as i:
                steps(ROUND, i + 1, i)
            steps(LAST, None, CHUNKS - 1)

        @block.gpsimd
        def _(pool):
            def const(ins):
                ins.then_inc(s_consts_ready, 1)

            const(pool.memset(ident[:, :], 0.0))
            const(pool.memset(identb[:, :], 0.0))
            const(pool.memset(mask_q[:, :, :], 0.0))
            const(pool.memset(mask_k[:, :, :], 0.0))
            const(pool.memset(minus_half[:, :], -0.5))
            const(pool.memset(zero[:, :], 0.0))
            const(pool.iota(iota8[:, :], pattern=[[1, E0]], base=0, channel_multiplier=0, allow_small_or_imprecise_dtypes=True))
            pool.wait_ge(s_consts_ready, 7)
            for m in (ident, identb):
                const(pool.affine_select(out=m[:, :], in_=m[:, :], compare_op=ALU.not_equal, fill=1.0, base=0,
                                         pattern=[[-1, P]], channel_multiplier=1))
            const(pool.affine_select(out=mask_q[:, :, :], in_=mask_q[:, :, :], compare_op=ALU.is_ge, fill=MASKED, base=0,
                                     pattern=[[0, 4], [-1, P]], channel_multiplier=1))
            const(pool.affine_select(out=mask_k[:, :, :], in_=mask_k[:, :, :], compare_op=ALU.is_ge, fill=MASKED, base=0,
                                     pattern=[[0, 4], [1, P]], channel_multiplier=-1))
            pool.wait_ge(s_consts_ready, N_CONSTS)

            pw = nc.gpsimd.tensor_tensor
            def steps(names, c, i):
                for step in names:
                    if step == ("front", "norm0"):
                        pool.wait_ge(s_var0, at(c, "var0", 1))
                        pw(rstd[:, :], vare[:, :], minus_half[:, 0:TILES], ALU.pow).then_inc(s_rstd0, 1)
                    elif step == ("front", "norm1"):
                        pool.wait_ge(s_var1, at(c, "var1", 1))
                        pw(rstd[:, :], vare[:, :], minus_half[:, 0:TILES], ALU.pow).then_inc(s_rstd1, 1)
                    elif step[0] == "front" and step[1].startswith("hidden"):
                        f = int(step[1][6:])
                        pool.wait_ge(s_ha_done, at(c, "ha_done", f + 1))
                        pool.wait_ge(s_hb_done, at(c, "hb_done", f + 1))
                        pw(ha[:, f, :], ha[:, f, :], hb[:, f % 2, :], ALU.add).then_inc(s_hsum_done, 1)
                    elif step[0] == "front" and step[1] in ("queries1", "keys1"):
                        for n in ((0, 1) if step[1] == "queries1" else (2, 3)):
                            pool.wait_ge(s_part2, at(c, "part2", n + 1))
                            pw(parts[:, 2, n, :], qkf[:, n, :], parts[:, 1, n, :], ALU.subtract).then_inc(s_part3, 1)
                    elif step[0] == "begin":
                        pool.wait_ge(s_xn1_done, at(i, "xn1_done", TILES))
                        pw(out[:, :, :], x1[:, :, :], zero[:, 0:1].unsqueeze(2).to_broadcast([P, TILES, D]), ALU.add).then_inc(s_keep_done, 1)
                    elif step[0] == "moe" and step[1] <= PAIRS:
                        j = step[1]
                        pool.wait_ge(s_gate_act, at(i, "gate_act", 2 * j + 1))
                        pw(waited[:, 1:2], minus_half[:, 0:1], minus_half[:, 0:1], ALU.add)
                        rows = INNER if j == PAIRS else P
                        nc.gpsimd.tensor_scalar(gt[0:rows, j % 2, :], gt[0:rows, j % 2, :], 0.5, 0.5,
                                                ALU.mult, ALU.add).then_inc(s_ga_mid, 1)
                        if j < PAIRS:
                            k = j // 2
                            pool.wait_ge(s_ga_mid, at(i, "ga_mid", j + 1))
                            pool.wait_ge(s_wb_in[k % 2], i * WB_IN + 32 * (k // 2 + 1))
                            pw(gt[:, j % 2, :], gt[:, j % 2, :], wb[:, k % 2, j % 2, :], ALU.mult).then_inc(s_ga_done, 1)
                    elif step[0] == "norm":
                        b = step[1]
                        pool.wait_ge(s_ms_done, at(i, "ms_done", b + 1))
                        pw(orms[:, :, :], oms[:, :, :], minus_half[:, :].rearrange("p (a b) -> p a b", a=2), ALU.pow).then_inc(s_orms_done, 1)
                    elif step[0] == "end":
                        pool.wait_ge(s_out_stored, at(i, "out_stored", 16))

            steps(OPENING, 0, None)
            with pool.Fori(0, CHUNKS - 1) as i:
                steps(ROUND, i + 1, i)
            steps(LAST, None, CHUNKS - 1)

        @block.vector
        def _(dve):
            V = nc.vector
            count = [0]
            base_i = [None]

            def link(ins, by_copy=False):
                count[0] += 1
                ins.then_inc(s_dve_link, 1)
                if base_i[0] is None:
                    dve.wait_ge(s_dve_link, count[0])
                else:
                    dve.wait_ge(s_dve_link, base_i[0] + count[0])
                    if by_copy:
                        V.tensor_copy(waited[:, 0:1], iota8[:, 0:1])

            def setup(ins):
                ins.then_inc(s_setup_vec, 1)

            V.memset(waited[:, 1:2], 0.0).then_inc(s_out_done, 1)
            setup(V.memset(twos_row[:, :], 2.0))
            setup(V.memset(v1[:, :, :, :], 0.0))
            setup(V.memset(qa[0:NEG_ROW, :, :], 0.0))
            setup(V.memset(ka[0:NEG_ROW, :, :], 0.0))
            setup(V.memset(ka[NEG_ROW:KROWS, :, :], 1.0))
            dve.wait_ge(s_setup_vec, 2)
            setup(V.memset(v1[:, :, :, DV:DV + 1], 1.0))
            dve.wait_ge(s_weights_in, wall)
            setup(V.tensor_scalar(bgh[:, 0:PAIRS], bg[:, 0:PAIRS], 0.5, None, ALU.mult))
            setup(V.tensor_scalar(bgh[0:INNER, PAIRS:], bg[0:INNER, PAIRS:], 0.5, None, ALU.mult))
            setup(V.tensor_scalar(bdsh[:, :], bds[:, :], 0.5, None, ALU.mult))
            for f in range(2):
                setup(V.tensor_scalar(wo1s[:, f, :], wo1[:, f, :], rms_col[:, 0:1], 1.0 - LAM0, ALU.mult, ALU.mult))
            link(V.tensor_tensor(lam_in[:, 0, :], lam_in[:, 0, :], lam_in[:, 1, :], ALU.mult))
            link(V.tensor_tensor(lam_in[:, 2, :], lam_in[:, 2, :], lam_in[:, 3, :], ALU.mult))
            link(V.reduce_sum(lam_e[:, 0, :], lam_in[:, 0, :].rearrange("p (h d) -> p h d", d=DH), AX))
            V.reduce_sum(lam_e[:, 1, :], lam_in[:, 2, :].rearrange("p (h d) -> p h d", d=DH), AX).then_inc(s_lam_exp, 1)
            dve.wait_ge(s_setup_act, 1)
            link(V.scalar_tensor_tensor(out=lam[:, :], in0=lam_e[:, 0, :], scalar=LAM0, in1=lam_e[:, 1, :],
                                        op0=ALU.add, op1=ALU.subtract))
            dve.wait_ge(s_consts_ready, N_CONSTS)
            assert count[0] == SETUP_LINKS
            count[0] = 0

            def layernorm(i, src, dst, var_ready, rstd_ready, done):
                for c in range(TILES):
                    ins = V.bn_stats(stats[:, c, :], src[:, c, :])
                link(ins, True)
                for c in range(TILES):
                    ins = V.bn_aggr(mv[:, c, :], stats[:, c, :])
                link(ins)
                V.tensor_scalar(vare[:, :], mv[:, :, 1], EPS, None, ALU.add).then_inc(var_ready, 1)
                dve.wait_ge(rstd_ready, i + 1)
                for c in range(TILES):
                    V.tensor_scalar(dst[:, c, :], src[:, c, :], mv[:, c, 0:1], rstd[:, c:c + 1], ALU.subtract, ALU.mult).then_inc(done, 1)

            def wide(ap, n):
                return ap.unsqueeze(2).to_broadcast([P, ap.shape[1], n])

            def front(name, c, i, pair):
                one, two = pairs[pair][:, 0, :], pairs[pair][:, 1, :]
                if name == "norm0":
                    dve.wait_ge(s_x_in, at(c, "x_in", 16))
                    layernorm(c, x, xn, s_var0, s_rstd0, s_xn0)
                elif name == "keys0":
                    dve.wait_ge(s_logits_ps, at(c, "logits_ps", 1))
                    link(V.tensor_tensor(logit[:, :, :], two[:, 0:TILES * E0].rearrange("p (c e) -> p c e", e=E0),
                                         gate_b[:, :].unsqueeze(1).to_broadcast([P, TILES, E0]), ALU.add))
                    link(V.reduce_max(lmax[:, :], logit[:, :, :], AX))
                    V.tensor_tensor(logit[:, :, :], logit[:, :, :], wide(lmax[:, :], E0), ALU.subtract).then_inc(s_lsub, 1)
                elif name == "router0":
                    dve.wait_ge(s_lexp_done, at(c, "lexp_done", 1))
                    link(V.reduce_sum(lsum[:, :], lexp[:, :, :], AX))
                    link(V.reciprocal(lsum[:, :], lsum[:, :]))
                    link(V.tensor_tensor(lexp[:, :, :], lexp[:, :, :], wide(lsum[:, :], E0), ALU.mult), True)
                    for k in range(TILES):
                        ins = V.max(top[:, k, :], lexp[:, k, :])
                    link(ins, True)
                    for k in range(TILES):
                        ins = V.max_index(topi[:, k, :], top[:, k, :], lexp[:, k, :])
                    link(ins)
                    link(V.tensor_copy(topf[:, :, :], topi[:, :, 0:2]))
                    for j in range(2):
                        ins = V.tensor_tensor(pick[:, j, :, :], iota8[:, :].unsqueeze(1).to_broadcast([P, TILES, E0]),
                                              topf[:, :, j:j + 1].to_broadcast([P, TILES, E0]), ALU.is_equal)
                    link(ins)
                    link(V.tensor_tensor(hvs[:, :], top[:, :, 0], top[:, :, 1], ALU.add))
                    link(V.tensor_scalar(hvs[:, :], hvs[:, :], 0.5, None, ALU.mult))
                elif name == "inner0":
                    dve.wait_ge(s_u_ps, at(c, "u_ps", 1))
                    for j in range(2):
                        V.tensor_tensor(um[:, j, :, :].rearrange("p c (e r) -> p (c e) r", r=R0),
                                        one.rearrange("p (g r) -> p g r", r=R0),
                                        wide(pick[:, j, :, :].rearrange("p c e -> p (c e)"), R0), ALU.mult).then_inc(s_um_done, 1)
                elif name == "scores0":
                    for b in range(CB):
                        dve.wait_ge(s_s0_ps, at(c, "s0_ps", b + 1))
                        V.tensor_reduce(nmax0[:, 2 * b:2 * b + 1], pairs[pair][:, b, 0:P], AX, ALU.max, negate=True)
                        ins = V.tensor_reduce(nmax0[:, 2 * b + 1:2 * b + 2], pairs[pair][:, b, P:3 * P], AX, ALU.max, negate=True)
                    link(ins)
                    V.tensor_scalar(nbias0[:, :], nmax0[:, :], SCALE0, None, ALU.mult).then_inc(s_nb0, 1)
                elif name.startswith("hidden"):
                    f = int(name[6:])
                    dve.wait_ge(s_inter_ps, at(c, "inter_ps", 2 * f + 2))
                    if f >= 2:
                        dve.wait_ge(s_hsum_done, at(c, "hsum_done", f - 1))
                    V.tensor_scalar(hb[:, f % 2, :], two, bi[:, f:f + 1], 0.0, ALU.add, ALU.max).then_inc(s_hb_done, 1)
                elif name == "out0":
                    dve.wait_ge(s_p0_done, at(c, "p0_done", TILES))
                    link(V.reciprocal(rl0[:, :], l0[:, :]))
                    dve.wait_ge(s_att_ps, at(c, "att_ps", 1))
                    link(V.tensor_tensor(tmp0[:, :, :], one.rearrange("p (c d) -> p c d", d=D), wide(rl0[:, :], D), ALU.mult))
                    dve.wait_ge(s_th0_done, at(c, "th0_done", TILES))
                    V.tensor_tensor(gate0[:, :, :], two.rearrange("p (c d) -> p c d", d=D), wide(hvs[:, :], D), ALU.mult).then_inc(s_z_read, 1)
                    dve.wait_ge(s_z_read, at(c, "z_read", 1))
                    link(V.scalar_tensor_tensor(out=gate0[:, :, :], in0=th0[:, :, :], scalar=1.0, in1=gate0[:, :, :],
                                                op0=ALU.add, op1=ALU.mult))
                    link(V.tensor_tensor(gate0[:, :, :], gate0[:, :, :], tmp0[:, :, :], ALU.mult))
                    if i is not None:
                        dve.wait_ge(s_keep_done, at(i, "keep_done", 1))
                    link(V.tensor_tensor(x1[:, :, :], x[:, :, :], gate0[:, :, :], ALU.add))
                elif name == "norm1":
                    layernorm(c, x1, xn1, s_var1, s_rstd1, s_xn1_done)
                elif name == "router1":
                    dve.wait_ge(s_router_ps, at(c, "router_ps", 1))
                    V.tensor_tensor(rlog[:, :, :], one[:, 0:TILES * E1].rearrange("p (c e) -> p c e", e=E1),
                                    br[:, :].unsqueeze(1).to_broadcast([P, TILES, E1]), ALU.add).then_inc(s_rl_done, 1)
                    dve.wait_ge(s_rexp_done, at(c, "rexp_done", 1))
                    link(V.tensor_scalar(aff[:, :, :], rexp[:, :, :], 1.0, None, ALU.add))
                    link(V.reciprocal(aff[:, :, :], aff[:, :, :]), True)
                    for k in range(TILES):
                        ins = V.max(top1[:, k, :], aff[:, k, :])
                    link(ins, True)
                    for k in range(TILES):
                        ins = V.match_replace(rest1[:, k, :], top1[:, k, :], aff[:, k, :], -1.0)
                    link(ins)
                    link(V.scalar_tensor_tensor(out=wtok[:, :, :], in0=rest1[:, :, :], scalar=0.0, in1=aff[:, :, :],
                                                op0=ALU.is_lt, op1=ALU.mult))
                    link(V.reduce_sum(wsum[:, :], top1[:, :, :], AX))
                    link(V.tensor_scalar(wsum[:, :], wsum[:, :], 1e-9, None, ALU.add))
                    link(V.reciprocal(wsum[:, :], wsum[:, :]))
                    V.tensor_tensor(wtok[:, :, :], wtok[:, :, :], wide(wsum[:, :], E1), ALU.mult).then_inc(s_w_done, 1)
                elif name in ("queries1", "keys1"):
                    for n in ((0, 1) if name == "queries1" else (2, 3)):
                        dve.wait_ge(s_qkf_done, at(c, "qkf_done", n + 1))
                        dve.wait_ge(s_part1, at(c, "part1", n + 1))
                        link(V.tensor_tensor(qkf[:, n, :], qkf[:, n, :], parts[:, 0, n, :], ALU.subtract))
                        V.tensor_copy(parts[:, 1, n, :], qkf[:, n, :]).then_inc(s_part2, 1)
                elif name == "values1":
                    if i is not None:
                        dve.wait_ge(s_pv_ps, at(i, "pv_ps", CB * GROUPS))
                    for n in range(2):
                        dve.wait_ge(s_v_ps, at(c, "v_ps", n + 1))
                        V.tensor_copy(v1[:, 2 * n:2 * n + 2, :, 0:DV].rearrange("p c h d -> p (c h) d"),
                                      pairs[pair][:, n, :].rearrange("p (g d) -> p g d", d=DV)).then_inc(s_v_sb, 1)

            def experts(i, j):
                rows = INNER if j == PAIRS else P
                dve.wait_ge(s_gate_act, at(i, "gate_act", 2 * j + 2))
                if j == PAIRS:
                    dve.wait_ge(s_ga_mid, at(i, "ga_mid", j + 1))
                else:
                    dve.wait_ge(s_ga_done, at(i, "ga_done", j + 1))
                if j >= HR:
                    dve.wait_ge(s_acc_ps, at(i, "acc_ps", j - HR + 1))
                link(V.tensor_tensor(h1[0:rows, j % HR, :], gt[0:rows, j % 2, :], gb[0:rows, j % 2, :], ALU.mult))
                dve.wait_ge(s_up_ps, at(i, "up_ps", j + 1))
                V.scalar_tensor_tensor(out=h1[0:rows, j % HR, :], in0=bank[6][0:rows, :], scalar=bu[0:rows, j:j + 1],
                                       in1=h1[0:rows, j % HR, :], op0=ALU.add, op1=ALU.mult).then_inc(s_h_done, 1)

            def steps(names, c, i, links):
                base_i[0] = links
                count[0] = 0
                taken = 0
                for step in names:
                    name = step[1] if step[0] == "front" else step[0]
                    pair = taken % 2
                    taken += RING.get(name, 0)
                    if step[0] == "front":
                        front(name, c, i, pair)
                    elif step[0] == "moe":
                        if 1 <= step[1] <= PAIRS + 1:
                            experts(i, step[1] - 1)
                    elif step[0] == "max":
                        _, b, g, u = step
                        dve.wait_ge(s_max_ps, at(i, "max_ps", b * MAX_UNITS + 3 * g + u + 1))
                        if u == 0:
                            src = pairs[pair][:, :, :].rearrange("p n (h c) -> p (n h) c", c=P)
                            dst = nmax1[:, 2 * b, GHC * g:GHC * (g + 1)]
                        else:
                            src = pairs[pair][:, :, :].rearrange("p n (h c) -> p (n h) c", c=SEQ)
                            dst = nmax1[:, 2 * b + 1, GHC * g + 4 * (u - 1):GHC * g + 4 * u]
                        V.tensor_reduce(dst, src, AX, ALU.max, negate=True).then_inc(s_nmax_done, 1)
                    elif step[0] == "minus":
                        b = step[1]
                        dve.wait_ge(s_nmax_done, at(i, "nmax_done", (b + 1) * MAX_UNITS))
                        k = slice(2 * b, 2 * b + 2)
                        link(V.tensor_copy(mparts[:, k, 0, :], nmax1[:, k, :]))
                        link(V.tensor_tensor(mres[:, k, :], nmax1[:, k, :], mparts[:, k, 0, :], ALU.subtract))
                        link(V.tensor_copy(mparts[:, k, 1, :], mres[:, k, :]))
                        V.tensor_tensor(mparts[:, k, 2, :], mres[:, k, :], mparts[:, k, 1, :], ALU.subtract).then_inc(s_mp_done, 1)
                    elif step[0] == "back":
                        _, b, g = step
                        n = b * GROUPS + g
                        dve.wait_ge(s_ot_ps, at(i, "ot_ps", n + 1))
                        o = bank[4].rearrange("p (g w) -> p g w", w=VW1)
                        rl = rl1[:, :, :, :].rearrange("p q c h -> p (q c h)")
                        link(V.reciprocal(rl, o[:, :, DV]))
                        link(V.tensor_tensor(rl1[:, :, 1, :], rl1[:, :, 1, :],
                                             lam[:, g * GH:(g + 1) * GH].unsqueeze(1).to_broadcast([P, 2, GH]), ALU.mult))
                        link(V.tensor_tensor(o12[:, :, :, :, :].rearrange("p q c h d -> p (q c h) d"), o[:, :, 0:DV],
                                             wide(rl, DV), ALU.mult))
                        V.tensor_tensor(oc[:, 2 * b:2 * b + 2, g * GH * DV:(g + 1) * GH * DV],
                                        o12[:, :, 0, :, :].rearrange("p q h d -> p q (h d)"),
                                        o12[:, :, 1, :, :].rearrange("p q h d -> p q (h d)"), ALU.subtract).then_inc(s_oc_done, 1)
                    elif step[0] == "norm":
                        b = step[1]
                        dve.wait_ge(s_oc_done, at(i, "oc_done", GROUPS * (b + 1)))
                        k = slice(2 * b, 2 * b + 2)
                        link(V.tensor_tensor(osq[:, :, :], oc[:, k, :], oc[:, k, :], ALU.mult))
                        link(V.reduce_sum(oms[:, :, :].rearrange("p q h -> p (q h)"),
                                          osq[:, :, :].rearrange("p q (h d) -> p (q h) d", d=DV), AX))
                        V.tensor_scalar(oms[:, :, :], oms[:, :, :], 1.0 / DV, EPS, ALU.mult, ALU.add).then_inc(s_ms_done, 1)
                    elif step[0] == "turn":
                        b = step[1]
                        k = slice(2 * b, 2 * b + 2)
                        dve.wait_ge(s_orms_done, at(i, "orms_done", b + 1))
                        V.tensor_tensor(on[:, :, :].rearrange("p q (h d) -> p (q h) d", d=DV),
                                        oc[:, k, :].rearrange("p q (h d) -> p (q h) d", d=DV),
                                        wide(orms[:, :, :].rearrange("p q h -> p (q h)"), DV), ALU.mult).then_inc(s_on_done, 1)
                    elif step[0] == "end":
                        dve.wait_ge(s_fth_done, at(i, "fth_done", 2))
                        link(V.scalar_tensor_tensor(out=fg[:, :], in0=fth[:, :], scalar=1.0, in1=fvh[:, :], op0=ALU.add, op1=ALU.mult))
                        dve.wait_ge(s_s1_ps, at(i, "s1_ps", 1))
                        V.tensor_tensor(fg[:, :], bank[4], fg[:, :], ALU.mult).then_inc(s_fg_done, 1)
                        dve.wait_ge(s_fin_ps, at(i, "fin_ps", 1))
                        dve.wait_ge(s_keep_done, at(i, "keep_done", 1))
                        V.tensor_tensor(out[:, :, :], out[:, :, :], bank[5].rearrange("p (c d) -> p c d", d=D), ALU.add).then_inc(s_out_done, 1)
                return count[0]

            n = steps(OPENING, 0, None, SETUP_LINKS)
            assert n == OPEN_LINKS, n
            with dve.Fori(0, CHUNKS - 1) as i:
                n = steps(ROUND, i + 1, i, SETUP_LINKS + OPEN_LINKS + i * ROUND_LINKS)
            assert n == ROUND_LINKS, n
            steps(LAST, None, CHUNKS - 1, SETUP_LINKS + OPEN_LINKS + (CHUNKS - 1) * ROUND_LINKS)


def l0_and_l1_kernel(nc, a, out):
    t = dict(a)
    t["out"] = out
    t["parts_dram"] = nc.dram_tensor("parts_scratch", (2, HC, 3 * DH, CHUNK), BF16, kind="Internal").ap()
    t["wt_dram"] = nc.dram_tensor("wt_scratch", (E1, CHUNK), F32, kind="Internal").ap()
    build(nc, t)


def kernel(**inputs):
    import numpy as _np
    import concourse.bacc as _bacc
    from concourse import mybir as _mybir
    from concourse.bass_utils import run_bass_kernel_spmd as _run

    v = {k: _np.asarray(x) for k, x in inputs.items()}

    def rows(w, n):
        return w.reshape(n, -1, w.shape[1]).transpose(1, 0, 2)

    a = {
        "x": v["L0_attn_in_features"].reshape(CHUNKS, TILES, P, D).transpose(0, 2, 1, 3),
        "wkq": _np.stack([rows(v["L0_attn_w_k"], OT).reshape(P, -1), rows(v["L0_attn_w_q"], OT).reshape(P, -1)], 1),
        "wvo": _np.stack([rows(v["L0_attn_w_v"], OT).reshape(P, -1), rows(v["L0_attn_w_o"].T, OT).reshape(P, -1)], 1),
        "wi_t": v["L0_ffn_wi"].T,
        "bi": v["L0_ffn_bi"].reshape(FB, P).T,
        "wo_t": rows(v["L0_ffn_wo"].T, FB),
        "bo": v["L0_ffn_bo"].reshape(1, P),
        "la": v["L0_ffn_lora_A"].reshape(E0 * R0, D).T,
        "lb": v["L0_ffn_lora_B"].transpose(0, 2, 1).reshape(E0 * R0, 512),
        "gate_w": v["L0_ffn_gate_w"].T,
        "gate_b": v["L0_ffn_gate_b"],
        "wq1": v["L1_attn_Wq"].T, "wk1": v["L1_attn_Wk"].T, "wv1": v["L1_attn_Wv"].T,
        "wo1": rows(v["L1_attn_Wo"].T, 2),
        "lq1": v["L1_attn_lq1"].reshape(-1), "lk1": v["L1_attn_lk1"].reshape(-1),
        "lq2": v["L1_attn_lq2"].reshape(-1), "lk2": v["L1_attn_lk2"].reshape(-1),
        "rms": v["L1_attn_rms_scale"].reshape(DV, 1),
        "wr": v["L1_ffn_Wr"], "br": v["L1_ffn_br"],
        "wg": v["L1_ffn_Wg"].transpose(1, 0, 2).reshape(D, -1), "wu": v["L1_ffn_Wu"].transpose(1, 0, 2).reshape(D, -1),
        "wd": v["L1_ffn_Wd"].reshape(PAIRS, P, D).transpose(1, 0, 2),
        "bg": v["L1_ffn_bg"].reshape(PAIRS, P).T, "bu": v["L1_ffn_bu"].reshape(PAIRS, P).T,
        "bd": v["L1_ffn_bd"],
        "wgs": v["L1_ffn_Wg_s"], "wus": v["L1_ffn_Wu_s"], "wds": v["L1_ffn_Wd_s"],
        "bgs": v["L1_ffn_bg_s"].reshape(INNER, 1), "bus": v["L1_ffn_bu_s"].reshape(INNER, 1),
        "bds": v["L1_ffn_bd_s"].reshape(D, 1),
    }
    nc = _bacc.Bacc("TRN2", target_bir_lowering=False, num_devices=1)
    arrays, aps = {}, {}
    for name, x in a.items():
        x = _np.ascontiguousarray(x)
        arrays[f"in_{name}"] = x
        aps[name] = nc.dram_tensor(f"in_{name}", x.shape, _mybir.dt.from_np(x.dtype), kind="ExternalInput").ap()
    out = nc.dram_tensor("out", (CHUNKS, P, TILES, D), _mybir.dt.float32, kind="ExternalOutput").ap()
    l0_and_l1_kernel(nc, aps, out)
    r = _run(nc, [arrays], core_ids=[0])
    got = r.results[0]["out"]
    return got.transpose(0, 2, 1, 3).reshape(BATCHES, SEQ, D)
```

```python
from contextlib import ExitStack

import numpy as np

import concourse.bass as bass
from concourse import mybir

ALU = mybir.AluOpType
ACT = mybir.ActivationFunctionType
F32 = mybir.dt.float32
BF16 = mybir.dt.bfloat16
U32 = mybir.dt.uint32
AX = mybir.AxisListType.X

P = 128
D = 128
BATCHES, SEQ = 8, 256
CHUNK = 512
CB = CHUNK // SEQ
TILES = CHUNK // P
CHUNKS = BATCHES * SEQ // CHUNK
EPS = 1e-5
MASKED = -1e30

OT = 1024 // P
E0, R0 = 8, 16
FB = 512 // P
SCALE0 = 1.0 / 32.0

HEADS, DH = 16, 8
HC = 2 * HEADS
DV = 2 * DH
HR = 3
VW1 = 32
SCALE1 = 1.0 / float(np.sqrt(DH))
NEG_ROW = 96
KROWS = NEG_ROW + 3
LAM0 = 0.8
GROUPS = 4
GH = HEADS // GROUPS
GHC = 2 * GH
E1, INNER = 32, 64
PAIRS = E1 // 2
TOPK = 8

MAX_UNITS = 3 * GROUPS
RING = {"turn0": 1, "keys0": 1, "inner0": 1, "scores0": 1, "picks0": 1, "probs0": 1, "out0": 1, "turn1": 1,
        "router1": 1, "queries1": 1, "keys1": 1, "values1": 1, "max": 1, "score": 3,
        **{f"hidden{h}": 1 for h in range(FB // 2)}}
MOE_AHEAD = 5


def order(text):
    steps = [tuple(int(x) if x.isdigit() else x for x in token.split("/")) for token in text.split()]
    alone = ("begin", "keep", "end", "fin", "setup", "stored")
    return [("front", *s) if len(s) == 1 and s[0] not in alone else s for s in steps]


def units(steps):
    out = []
    for s in steps:
        name = s[1] if s[0] == "front" else s[0]
        for n in range(RING.get(name, 0)):
            out.append((*s, n) if name == "score" else s)
    return out


OPENING = order("""
    load norm0 scale0 turn0 keys0 router0 inner0 scores0 picks0 probs0 hidden0 hidden1 setup out0 norm1 scale1
    turn1 router1 choose1 queries1 keys1 values1 weights1 begin moe/0 moe/1 moe/2 moe/3 max/0/0/0 max/0/0/1
    max/0/0/2 max/0/1/0 max/0/1/1 max/0/1/2 max/0/2/0 max/0/2/1 moe/4 max/0/2/2 max/0/3/0 max/0/3/1 max/0/3/2
""")
ROUND = order("""
    keep load moe/5 minus/0 moe/6 score/0/0 score/0/1 norm0 scale0 values/0/0 moe/7 score/0/2 back/0/0 turn0
    values/0/1 score/0/3 back/0/1 keys0 router0 moe/8 values/0/2 back/0/2 max/1/0/0 inner0 moe/9 max/1/0/1
    max/1/0/2 values/0/3 max/1/1/0 scores0 max/1/1/1 back/0/3 max/1/1/2 picks0 max/1/2/0 max/1/2/1 norm/0 moe/10
    probs0 hidden0 hidden1 max/1/2/2 max/1/3/0 turn/0 max/1/3/1 max/1/3/2 moe/11 minus/1 out0 score/1/0
    score/1/1 norm1 values/1/0 score/1/2 scale1 turn1 back/1/0 moe/12 values/1/1 back/1/1 score/1/3 values/1/2
    moe/13 back/1/2 values/1/3 router1 back/1/3 norm/1 queries1 choose1 moe/14 keys1 values1 moe/15 turn/1
    moe/16 weights1 moe/17 moe/18 end fin begin max/0/0/0 max/0/0/1 max/0/0/2 max/0/1/0 max/0/1/1 moe/0
    max/0/1/2 moe/1 max/0/2/0 max/0/2/1 moe/2 max/0/2/2 moe/3 max/0/3/0 max/0/3/1 moe/4 max/0/3/2 stored
""")
LAST = order("""
    keep moe/5 minus/0 moe/6 moe/7 score/0/0 values/0/0 score/0/1 back/0/0 score/0/2 moe/8 values/0/1 score/0/3
    back/0/1 values/0/2 max/1/0/0 moe/9 max/1/0/1 max/1/0/2 max/1/1/0 back/0/2 moe/10 values/0/3 max/1/1/1
    back/0/3 max/1/1/2 norm/0 max/1/2/0 moe/11 max/1/2/1 max/1/2/2 max/1/3/0 max/1/3/1 max/1/3/2 moe/12 turn/0
    minus/1 moe/13 score/1/0 score/1/1 values/1/0 score/1/2 back/1/0 moe/14 values/1/1 score/1/3 back/1/1 moe/15
    values/1/2 back/1/2 moe/16 values/1/3 back/1/3 norm/1 moe/17 turn/1 moe/18 end fin
""")
assert len(units(OPENING)) % 2 == 0 and len(units(ROUND)) % 2 == 0
N_WEIGHTS = 13 + 4 + 1 + 4 + P // DV
N_CONSTS = 9
WB_IN = 32 * PAIRS // 4
QK_IN = 16 * 2 * 3
N_SETUP_VEC = 7
OPEN_LINKS = 42
ROUND_LINKS = 78


def build(nc, t):
    with ExitStack() as ctx:
        def sb(name, shape, dt=F32):
            return ctx.enter_context(nc.sbuf_tensor(name, shape, dt))

        def sem(name):
            return ctx.enter_context(nc.semaphore(name))

        pairs = [ctx.enter_context(nc.psum_tensor(f"scores{n}", [P, 2, 512], F32)) for n in range(2)]
        single = [ctx.enter_context(nc.psum_tensor(f"bank{n}", [P, 512], F32)) for n in range(4, 8)]
        bank = [pairs[0][:, 0, :], pairs[0][:, 1, :], pairs[1][:, 0, :], pairs[1][:, 1, :]] + [s[:, :] for s in single]

        ident = sb("ident", [P, P])
        identb = sb("identb", [P, P], BF16)
        mask_q = sb("mask_q", [P, 4, P], BF16)
        twos_row = sb("twos_row", [1, P])
        minus_half = sb("minus_half", [P, HC])
        zero = sb("zero", [P, TILES])
        waited = sb("waited", [P, 8])
        iota8 = sb("iota8", [P, E0])
        mt = sb("mt", [P, P])
        vo = sb("vo", [P, P])
        wi_t = sb("wi_t", [P, 512])
        bi = sb("bi", [P, FB])
        wo_t = sb("wo_t", [P, FB, P])
        bo = sb("bo", [1, P])
        la = sb("la", [P, E0 * R0])
        lb = sb("lb", [P, 512])
        gate_w = sb("gate_w", [P, E0])
        gate_b = sb("gate_b", [P, E0])
        wq1 = sb("wq1", [P, 2 * P])
        wk1 = sb("wk1", [P, 2 * P])
        wv1 = sb("wv1", [P, 2 * P])
        wo1 = sb("wo1", [P, 2, P])
        wo1s = sb("wo1s", [P, 2, P])
        rms_col = sb("rms_col", [P, 1])
        lam_in = sb("lam_in", [P, 4, HEADS * DH])
        lam_e = sb("lam_e", [P, 2, HEADS])
        lam = sb("lam", [P, HEADS])
        wr = sb("wr", [P, E1])
        br = sb("br", [P, E1])
        wg = sb("wg", [P, E1 * INNER])
        wu = sb("wu", [P, E1 * INNER])
        wd = sb("wd", [P, PAIRS, P])
        bd = sb("bd", [E1, P])
        bg = sb("bg", [P, PAIRS + 1])
        bgh = sb("bgh", [P, PAIRS + 1])
        bu = sb("bu", [P, PAIRS + 1])
        wgs = sb("wgs", [P, INNER])
        wus = sb("wus", [P, INNER])
        wds = sb("wds", [INNER, P])
        bds = sb("bds", [P, 1])
        bdsh = sb("bdsh", [P, 1])

        x = sb("x", [P, TILES, D])
        stats = sb("stats", [P, TILES, 6])
        mv = sb("mv", [P, TILES, 2])
        vare = sb("vare", [P, TILES])
        rstd = sb("rstd", [P, TILES])
        xn = sb("xn", [P, TILES, D])
        xnt = sb("xnt", [P, CHUNK])
        yk = sb("yk", [P, CHUNK])
        vw = sb("vw", [P, TILES, D])
        nmax0 = sb("nmax0", [P, TILES])
        nbias0 = sb("nbias0", [P, TILES])
        l0 = sb("l0", [P, TILES])
        rl0 = sb("rl0", [P, TILES])
        pt0 = sb("pt0", [P, CB, 3 * P])
        logit = sb("logit", [P, TILES, E0])
        lmax = sb("lmax", [P, TILES])
        lexp = sb("lexp", [P, TILES, E0])
        lsum = sb("lsum", [P, TILES])
        top = sb("top", [P, TILES, 8])
        topi = sb("topi", [P, TILES, 8], U32)
        topf = sb("topf", [P, TILES, 2])
        pick = sb("pick", [P, 2, TILES, E0])
        hvs = sb("hvs", [P, TILES])
        umt = sb("umt", [P, 2, CHUNK])
        ha = sb("ha", [P, FB, CHUNK])
        hb = sb("hb", [P, 2, CHUNK])
        p0 = ha[:, 0:2, :].rearrange("p f (n q) -> p (f n) q", q=SEQ)
        um = hb[:, :, :].rearrange("p j (c e) -> p j c e", c=TILES)
        th0 = xn
        tmp0 = sb("tmp0", [P, TILES, D])
        gate0 = yk[:, :].rearrange("p (c d) -> p c d", d=D)
        x1 = sb("x1", [P, TILES, D])

        xn1 = tmp0
        xnt1n = sb("xnt1n", [P, CHUNK])
        xnt1 = sb("xnt1", [P, CHUNK])
        rlog = sb("rlog", [P, TILES, E1])
        rexp = sb("rexp", [P, TILES, E1])
        aff = sb("aff", [P, TILES, E1])
        top1 = sb("top1", [P, TILES, TOPK])
        rest1 = sb("rest1", [P, TILES, E1])
        wsum = sb("wsum", [P, TILES])
        wtok = sb("wtok", [P, TILES, E1])
        wt = sb("wt", [E1, CHUNK])
        wb = sb("wb", [P, 2, 2, CHUNK])
        qkf = sb("qkf", [P, 4, CHUNK])
        parts = sb("parts", [P, 3, 4, CHUNK], BF16)
        qa = sb("qa", [KROWS, HC, SEQ], BF16)
        ka = sb("ka", [KROWS, HC, SEQ], BF16)
        v1 = sb("v1", [P, TILES, HEADS, VW1])
        nmax1 = sb("nmax1", [P, TILES, HC])
        mres = sb("mres", [P, TILES, HC])
        mparts = sb("mparts", [P, TILES, 3, HC], BF16)
        mrows = sb("mrows", [3 * HC, CHUNK], BF16)
        pkb = sb("pkb", [P, GHC * (SEQ + P)])
        pk = [parts[:, :, :, :].rearrange("p a f t -> p (a f t)").bitcast(F32), pkb[:, :]]
        pk0 = [r[:, 0:GHC * SEQ].rearrange("p (h q) -> p h q", q=SEQ) for r in pk]
        pk1 = [r[:, GHC * SEQ:GHC * (SEQ + P)].rearrange("p (h q) -> p h q", q=P) for r in pk]
        ot = sb("ot", [P, 2, SEQ])
        rl1 = sb("rl1", [P, 2, 2, GH])
        o12 = sb("o12", [P, 2, 2, GH, DV])
        oc = sb("oc", [P, TILES, HEADS * DV])
        osq = sb("osq", [P, 2, HEADS * DV])
        oms = sb("oms", [P, 2, HEADS])
        orms = sb("orms", [P, 2, HEADS])
        on = sb("on", [P, 2, HEADS * DV])
        oct_ = sb("oct", [P, 2, CHUNK])
        gt = sb("gt", [P, 2, CHUNK])
        gb = sb("gb", [P, 2, CHUNK])
        h1 = sb("h1", [P, HR, CHUNK])
        kq_room = ha[:, :, :].rearrange("p f t -> p (f t)").rearrange("p (a c) -> p a c", a=2)
        vo_room = wb[:, :, :, :].rearrange("p n j t -> p (n j t)").rearrange("p (a c) -> p a c", a=2)
        fth = sb("fth", [P, CHUNK])
        fvh = sb("fvh", [P, CHUNK])
        fg = fvh
        out = sb("out_tok", [P, TILES, D])

        s_weights_in = sem("weights_in")
        s_consts_ready = sem("consts_ready")
        s_kq_in = sem("kq_in")
        s_vo_in = sem("vo_in")
        s_early_in = sem("early_in")
        s_ffn_in = sem("ffn_in")
        s_rooms = sem("rooms")
        s_mt_done = sem("mt_done")
        s_vo_done = sem("vo_done")
        s_mt_copied = sem("mt_copied")
        s_vo_copied = sem("vo_copied")
        s_setup_vec = sem("setup_vec")
        s_setup_act = sem("setup_act")
        s_lam_exp = sem("lam_exp")
        s_x_in = sem("x_in")
        s_var0 = sem("var0")
        s_rstd0 = sem("rstd0")
        s_xn0 = sem("xn0")
        s_xnt_ps = sem("xnt_ps")
        s_xnt_sb = sem("xnt_sb")
        s_yk_ps = sem("yk_ps")
        s_yk_sb = sem("yk_sb")
        s_vw_ps = sem("vw_ps")
        s_vw_sb = sem("vw_sb")
        s_s0_ps = sem("s0_ps")
        s_nb0 = sem("nb0")
        s_p0_done = sem("p0_done")
        s_pt_ps = sem("pt_ps")
        s_pt_sb = sem("pt_sb")
        s_att_ps = sem("att_ps")
        s_logits_ps = sem("logits_ps")
        s_u_ps = sem("u_ps")
        s_lsub = sem("lsub")
        s_lexp_done = sem("lexp_done")
        s_um_done = sem("um_done")
        s_umt_ps = sem("umt_ps")
        s_umt_sb = sem("umt_sb")
        s_inter_ps = sem("inter_ps")
        s_inter2_ps = sem("inter2_ps")
        s_ha_done = sem("ha_done")
        s_hb_done = sem("hb_done")
        s_hsum_done = sem("hsum_done")
        s_z_ps = sem("z_ps")
        s_th0_done = sem("th0_done")
        s_var1 = sem("var1")
        s_rstd1 = sem("rstd1")
        s_xn1_done = sem("xn1_done")
        s_xnt1_ps = sem("xnt1_ps")
        s_xnt1_sb = sem("xnt1_sb")
        s_router_ps = sem("router_ps")
        s_rl_done = sem("rl_done")
        s_rexp_done = sem("rexp_done")
        s_w_done = sem("w_done")
        s_wt_ps = sem("wt_ps")
        s_wt_sb = sem("wt_sb")
        s_wt_stored = sem("wt_stored")
        s_wb_in0 = sem("wb_in0")
        s_wb_in1 = sem("wb_in1")
        s_qk_ps = sem("qk_ps")
        s_qkf_done = sem("qkf_done")
        s_part1 = sem("part1")
        s_part2 = sem("part2")
        s_part3 = sem("part3")
        s_parts_stored = sem("parts_stored")
        s_qk_in0 = sem("qk_in0")
        s_qk_in1 = sem("qk_in1")
        s_qk_in2 = sem("qk_in2")
        s_qk_in3 = sem("qk_in3")
        s_v_ps = sem("v_ps")
        s_v_sb = sem("v_sb")
        s_max_ps = sem("max_ps")
        s_nmax_done = sem("nmax_done")
        s_mp_done = sem("mp_done")
        s_mrow_ps = sem("mrow_ps")
        s_mrow_sb = sem("mrow_sb")
        s_mrow_in = sem("mrow_in")
        s_gate_ps = sem("gate_ps")
        s_gate_act = sem("gate_act")
        s_ga_done = sem("ga_done")
        s_up_ps = sem("up_ps")
        s_h_done = sem("h_done")
        s_acc_ps = sem("acc_ps")
        s_sc_ps = sem("sc_ps")
        s_pk_done = sem("pk_done")
        s_pk_masked = sem("pk_masked")
        s_pv_ps = sem("pv_ps")
        s_ot_sb = sem("ot_sb")
        s_ot_ps = sem("ot_ps")
        s_o_read = sem("o_read")
        s_oc_done = sem("oc_done")
        s_ms_done = sem("ms_done")
        s_orms_done = sem("orms_done")
        s_on_done = sem("on_done")
        s_oct_ps = sem("oct_ps")
        s_oct_sb = sem("oct_sb")
        s_s1_ps = sem("s1_ps")
        s_fth_done = sem("fth_done")
        s_fg_done = sem("fg_done")
        s_fin_ps = sem("fin_ps")
        s_keep_done = sem("keep_done")
        s_cur_done = sem("cur_done")
        s_z_read = sem("z_read")
        s_out_done = sem("out_done")
        s_out_stored = sem("out_stored")
        s_dve_link = sem("dve_link")
        s_qk_first = sem("qk_first")
        s_qk_in = [s_qk_in0, s_qk_in1, s_qk_in2, s_qk_in3]
        s_wb_in = [s_wb_in0, s_wb_in1]

        PER = dict(x_in=16, var0=1, rstd0=1, xn0=TILES, xnt_ps=1, xnt_sb=1, yk_ps=1, yk_sb=1, vw_ps=1, vw_sb=1,
                   s0_ps=CB, nb0=1, p0_done=TILES, pt_ps=CB, pt_sb=CB, att_ps=1, logits_ps=1, u_ps=1, lsub=1,
                   lexp_done=1, um_done=2, umt_ps=2, umt_sb=2, inter_ps=FB, inter2_ps=FB, ha_done=FB, hb_done=FB,
                   hsum_done=FB, z_ps=1, th0_done=TILES, var1=1, rstd1=1, xn1_done=TILES, xnt1_ps=1,
                   xnt1_sb=1, router_ps=1, rl_done=1, rexp_done=1, w_done=1, wt_ps=1, wt_sb=1, wt_stored=16,
                   qk_ps=4, qkf_done=4, part1=4, part2=4, part3=4, parts_stored=16 * 12,
                   v_ps=2, v_sb=2, max_ps=CB * MAX_UNITS, nmax_done=CB * MAX_UNITS,
                   mp_done=CB, mrow_ps=CB, mrow_sb=CB, mrow_in=16 * 3 * CB,
                   gate_ps=PAIRS + 1, gate_act=2 * (PAIRS + 1), ga_done=PAIRS,
                   up_ps=PAIRS + 1, h_done=PAIRS + 1, acc_ps=PAIRS + 1, sc_ps=CB * GROUPS * 3, pk_done=CB * GROUPS * 3, pk_masked=CB * GROUPS * 3,
                   pv_ps=CB * GROUPS, ot_sb=CB * GROUPS, ot_ps=CB * GROUPS, oc_done=CB * GROUPS, o_read=CB * GROUPS, ms_done=CB,
                   orms_done=CB, on_done=CB, oct_ps=CB, oct_sb=CB, s1_ps=1, fth_done=2, fg_done=1,
                   fin_ps=1, out_done=1, out_stored=16, keep_done=1, cur_done=1, z_read=1)

        def at(i, name, k):
            return i * PER[name] + k

        def ring_free(pe, i, c, before):
            kind = before[1] if before[0] == "front" else before[0]
            if kind == "max":
                _, b, g, u = before
                pe.wait_ge(s_nmax_done, at(i if b else c, "nmax_done", b * MAX_UNITS + 3 * g + u + 1))
            elif kind == "score":
                _, b, g, u = before
                pe.wait_ge(s_pk_done, at(i, "pk_done", 3 * (b * GROUPS + g) + u + 1))
            elif kind == "turn0":
                pe.wait_ge(s_xnt_sb, at(c, "xnt_sb", 1))
            elif kind == "keys0":
                pe.wait_ge(s_yk_sb, at(c, "yk_sb", 1))
                pe.wait_ge(s_lsub, at(c, "lsub", 1))
            elif kind == "inner0":
                pe.wait_ge(s_vw_sb, at(c, "vw_sb", 1))
                pe.wait_ge(s_um_done, at(c, "um_done", 2))
            elif kind == "scores0":
                pe.wait_ge(s_p0_done, at(c, "p0_done", TILES))
            elif kind == "picks0":
                pe.wait_ge(s_umt_sb, at(c, "umt_sb", 2))
            elif kind == "probs0":
                pe.wait_ge(s_pt_sb, at(c, "pt_sb", CB))
            elif kind.startswith("hidden"):
                pe.wait_ge(s_hb_done, at(c, "hb_done", 2 * int(kind[6:]) + 2))
            elif kind == "out0":
                pe.wait_ge(s_z_read, at(c, "z_read", 1))
            elif kind == "turn1":
                pe.wait_ge(s_xnt1_sb, at(c, "xnt1_sb", 1))
            elif kind == "router1":
                pe.wait_ge(s_rl_done, at(c, "rl_done", 1))
            elif kind == "queries1":
                pe.wait_ge(s_part1, at(c, "part1", 2))
            elif kind == "keys1":
                pe.wait_ge(s_part1, at(c, "part1", 4))
            elif kind == "values1":
                pe.wait_ge(s_v_sb, at(c, "v_sb", 2))

        def load_wb(queue, k):
            src = t["wt_dram"].rearrange("(j e) t -> e j t", e=2)
            for e in range(2):
                queue.dma_start(wb[e * INNER:(e + 1) * INNER, k % 2, :, :],
                             src[e, 2 * k:2 * k + 2, :].partition_broadcast(INNER)).then_inc(s_wb_in[k % 2], 16)

        block = ctx.enter_context(nc.Block())

        n_weights = [0]

        @block.sync
        def _(sp):
            def load_qk(b, g0, groups, signal):
                for n, dst in enumerate((qa, ka)):
                    row = 0
                    for width in (3, 2, 1):
                        first = 0 if n == 0 else 3 - width
                        src = t["parts_dram"][n, g0 * GHC:(g0 + groups) * GHC, first * DH:(first + width) * DH, b * SEQ:(b + 1) * SEQ]
                        sp.dma_start(dst[row:row + width * DH, g0 * GHC:(g0 + groups) * GHC, :],
                                     src.rearrange("h r t -> r h t")).then_inc(signal, 16)
                        row += width * DH

            def steps(names, c, i):
                for step in names:
                    if step == ("front", "load"):
                        sp.dma_start(x[:, :, :], t["x"][bass.ds(c, 1)].rearrange("c p t d -> (c p) t d")).then_inc(s_x_in, 16)
                    elif step == ("front", "values1"):
                        sp.wait_ge(s_part1, at(c, "part1", 4))
                        sp.wait_ge(s_part2, at(c, "part2", 4))
                        sp.wait_ge(s_part3, at(c, "part3", 4))
                        for n in range(2):
                            for a in range(3):
                                for f in range(2):
                                    r = a if n == 0 else 2 - a
                                    dst = t["parts_dram"][n, f * 2 * GHC:(f + 1) * 2 * GHC, r * DH:(r + 1) * DH, :]
                                    sp.dma_start(dst, parts[:, a, 2 * n + f, :]).then_inc(s_parts_stored, 16)
                        if i is not None:
                            sp.wait_ge(s_sc_ps, at(i, "sc_ps", 3 * CB * GROUPS))
                        sp.wait_ge(s_parts_stored, at(c, "parts_stored", 16 * 12))
                        if i is None:
                            sp.wait_ge(s_rooms, 5)
                        load_qk(0, 0, GROUPS, s_qk_first)
                    elif c is not None and step[0] == "end":
                        sp.wait_ge(s_wt_sb, at(c, "wt_sb", 1))
                        sp.wait_ge(s_wb_in0, i * WB_IN + WB_IN)
                        sp.wait_ge(s_wb_in1, i * WB_IN + WB_IN)
                        sp.dma_start(t["wt_dram"], wt[:, :]).then_inc(s_wt_stored, 16)
                    elif step[0] == "begin" and i is not None:
                        sp.wait_ge(s_wt_stored, at(c, "wt_stored", 16))
                        load_wb(sp, 0)
                        load_wb(sp, 1)
                    elif step[0] == "moe" and step[1] % 2 == 0 and 4 <= step[1] + 2 < PAIRS:
                        sp.wait_ge(s_ga_done, at(c if step[1] < MOE_AHEAD else i, "ga_done", step[1]))
                        load_wb(sp, step[1] // 2 + 1)
                    elif step[0] == "score" and step[1] == 0:
                        g = step[2]
                        sp.wait_ge(s_sc_ps, at(i, "sc_ps", 3 * (g + 1)))
                        load_qk(1, g, 1, s_qk_in[g])
                    elif step[0] == "fin":
                        sp.wait_ge(s_out_done, i + 2)
                        sp.dma_start(t["out"][bass.ds(i, 1)].rearrange("c p t d -> (c p) t d"), out[:, :, :]).then_inc(s_out_stored, 16)

            def load(dst, src):
                sp.dma_start(dst, src).then_inc(s_weights_in, 16)
                n_weights[0] += 1

            steps(OPENING[:1], 0, None)
            sp.dma_start(kq_room, t["wkq"]).then_inc(s_kq_in, 16)
            sp.dma_start(gate_w[:, :], t["gate_w"]).then_inc(s_early_in, 16)
            sp.dma_start(gate_b[:, :], t["gate_b"].partition_broadcast(P)).then_inc(s_early_in, 16)
            sp.dma_start(la[:, :], t["la"]).then_inc(s_early_in, 16)
            sp.dma_start(vo_room, t["wvo"]).then_inc(s_vo_in, 16)
            for dst, name in ((wi_t, "wi_t"), (bi, "bi"), (lb, "lb"), (bo, "bo"), (wo_t, "wo_t")):
                sp.dma_start(dst[tuple(slice(None) for _ in dst.shape)], t[name]).then_inc(s_ffn_in, 16)
            for dst, name in ((wr, "wr"), (wq1, "wq1"), (wk1, "wk1"), (wv1, "wv1"),
                              (wo1, "wo1"), (wg, "wg"), (wu, "wu"), (wd, "wd"), (bd, "bd"),
                              (wgs, "wgs"), (wus, "wus"), (wds, "wds"), (bds, "bds")):
                load(dst[tuple(slice(None) for _ in dst.shape)], t[name])
            load(bg[:, 0:PAIRS], t["bg"])
            load(bu[:, 0:PAIRS], t["bu"])
            load(bg[0:INNER, PAIRS:], t["bgs"])
            load(bu[0:INNER, PAIRS:], t["bus"])
            load(br[:, :], t["br"].partition_broadcast(P))
            for n, name in enumerate(("lq1", "lk1", "lq2", "lk2")):
                load(lam_in[:, n, :], t[name].partition_broadcast(P))
            for g in range(P // DV):
                load(rms_col[g * DV:(g + 1) * DV, :], t["rms"])
            assert n_weights[0] == N_WEIGHTS

            steps(OPENING[1:], 0, None)
            with sp.Fori(0, CHUNKS - 1) as i:
                steps(ROUND, i + 1, i)
            steps(LAST, None, CHUNKS - 1)
            sp.wait_ge(s_out_stored, at(CHUNKS - 1, "out_stored", 16))

        wall = 16 * N_WEIGHTS

        @block.tensor
        def _(pe):
            mm = nc.tensor.matmul

            def fold(b, room, done):
                for o in range(OT):
                    last = mm(bank[b][:, 0:P], room[:, 0, o * P:(o + 1) * P], room[:, 1, o * P:(o + 1) * P],
                              start=(o == 0), stop=(o == OT - 1))
                last.then_inc(done, 1)

            pe.wait_ge(s_consts_ready, N_CONSTS)

            def front(name, c, i, pair):
                one, two = pairs[pair][:, 0, :], pairs[pair][:, 1, :]
                if name == "turn0":
                    pe.wait_ge(s_xn0, at(c, "xn0", TILES))
                    for k in range(TILES):
                        last = nc.tensor.transpose(one[:, k * P:(k + 1) * P], xn[:, k, :], ident[:, :])
                    last.then_inc(s_xnt_ps, 1)
                    if i is None:
                        pe.wait_ge(s_kq_in, 16)
                        fold(4, kq_room, s_mt_done)
                        pe.wait_ge(s_early_in, 16 * 3)
                elif name == "keys0":
                    pe.wait_ge(s_xnt_sb, at(c, "xnt_sb", 1))
                    for k in range(TILES):
                        last = mm(two[:, k * E0:(k + 1) * E0], xnt[:, k * P:(k + 1) * P], gate_w[:, :], start=(k == 0), stop=True, skip_group_check=True)
                    last.then_inc(s_logits_ps, 1)
                    if i is None:
                        pe.wait_ge(s_mt_copied, 1)
                    mm(one, mt[:, :], xnt[:, :], start=True, stop=True).then_inc(s_yk_ps, 1)
                elif name == "inner0":
                    for k in range(TILES):
                        last = mm(one[:, k * P:(k + 1) * P], xnt[:, k * P:(k + 1) * P], la[:, :], start=(k == 0), stop=True, skip_group_check=True)
                    last.then_inc(s_u_ps, 1)
                    if i is None:
                        pe.wait_ge(s_vo_in, 16)
                        fold(5, vo_room, s_vo_done)
                        pe.wait_ge(s_vo_copied, 1)
                    for k in range(TILES):
                        last = mm(two[:, k * P:(k + 1) * P], xnt[:, k * P:(k + 1) * P], vo[:, :], start=(k == 0), stop=True, skip_group_check=True)
                    last.then_inc(s_vw_ps, 1)
                elif name == "scores0":
                    pe.wait_ge(s_yk_sb, at(c, "yk_sb", 1))
                    for b in range(CB):
                        s = pairs[pair][:, b, :]
                        base = b * SEQ
                        mm(s[:, 0:P], identb[:, :], mask_q[:, 0, :], start=True, stop=False, skip_group_check=True)
                        mm(s[:, 2 * P:3 * P], identb[:, :], mask_q[:, 0, :], start=False, stop=False, skip_group_check=True)
                        mm(s[:, 0:P], xnt[:, base:base + P], yk[:, base:base + P], start=False, stop=True, skip_group_check=True)
                        mm(s[:, P:3 * P], xnt[:, base + P:base + SEQ], yk[:, base:base + SEQ], start=False, stop=True,
                           skip_group_check=True).then_inc(s_s0_ps, 1)
                elif name == "picks0":
                    for j in range(2):
                        pe.wait_ge(s_um_done, at(c, "um_done", j + 1))
                        for k in range(TILES):
                            last = nc.tensor.transpose(pairs[pair][:, j, k * P:(k + 1) * P], um[:, j, k, :], ident[:, :])
                        last.then_inc(s_umt_ps, 1)
                elif name == "probs0":
                    for b in range(CB):
                        pe.wait_ge(s_p0_done, at(c, "p0_done", 2 * b + 2))
                        s = pairs[pair][:, b, :]
                        nc.tensor.transpose(s[:, 0:P], p0[:, 2 * b, 0:P], ident[:, :])
                        nc.tensor.transpose(s[:, P:2 * P], p0[:, 2 * b + 1, 0:P], ident[:, :])
                        nc.tensor.transpose(s[:, 2 * P:3 * P], p0[:, 2 * b + 1, P:SEQ], ident[:, :]).then_inc(s_pt_ps, 1)
                elif name.startswith("hidden"):
                    blocks = [2 * int(name[6:]) + n for n in range(2)]
                    if i is None and blocks[0] == 0:
                        pe.wait_ge(s_ffn_in, 16 * 5)
                    for n, f in enumerate(blocks):
                        mm(pairs[pair][:, n, :], wi_t[:, f * P:(f + 1) * P], xnt[:, :], start=True, stop=False, skip_group_check=True)
                        if f == 0:
                            pe.wait_ge(s_umt_sb, at(c, "umt_sb", 1))
                        mm(pairs[pair][:, n, :], lb[:, f * P:(f + 1) * P], umt[:, 0, :], start=False, stop=True,
                           skip_group_check=True).then_inc(s_inter_ps, 1)
                    for n, f in enumerate(blocks):
                        if f == 0:
                            pe.wait_ge(s_umt_sb, at(c, "umt_sb", 2))
                        pe.wait_ge(s_ha_done, at(c, "ha_done", f + 1))
                        mm(pairs[pair][:, n, :], lb[:, f * P:(f + 1) * P], umt[:, 1, :], start=False, stop=True,
                           skip_group_check=True).then_inc(s_inter2_ps, 1)
                elif name == "out0":
                    pe.wait_ge(s_vw_sb, at(c, "vw_sb", 1))
                    for b in range(CB):
                        pe.wait_ge(s_pt_sb, at(c, "pt_sb", b + 1))
                        k = 2 * b
                        mm(one[:, k * P:(k + 1) * P], pt0[:, b, 0:P], vw[:, k, :], start=(b == 0), stop=True, skip_group_check=True)
                        mm(one[:, (k + 1) * P:(k + 2) * P], pt0[:, b, P:2 * P], vw[:, k, :], start=False, stop=False, skip_group_check=True)
                        last = mm(one[:, (k + 1) * P:(k + 2) * P], pt0[:, b, 2 * P:3 * P], vw[:, k + 1, :], start=False, stop=True, skip_group_check=True)
                    last.then_inc(s_att_ps, 1)
                    pe.wait_ge(s_hsum_done, at(c, "hsum_done", FB))
                    if i is None:
                        pe.wait_ge(s_setup_vec, 1)
                    for k in range(TILES):
                        z = two[:, k * P:(k + 1) * P]
                        mm(z, twos_row[:, :], bo[:, :], start=(k == 0), stop=False, skip_group_check=True)
                        for f in range(FB):
                            last = mm(z, ha[:, f, k * P:(k + 1) * P], wo_t[:, f, :], start=False, stop=(f == FB - 1), skip_group_check=True)
                    last.then_inc(s_z_ps, 1)
                elif name == "turn1":
                    pe.wait_ge(s_xn1_done, at(c, "xn1_done", TILES))
                    for k in range(TILES):
                        last = nc.tensor.transpose(one[:, k * P:(k + 1) * P], xn1[:, k, :], ident[:, :])
                    last.then_inc(s_xnt1_ps, 1)
                elif name == "router1":
                    pe.wait_ge(s_xnt1_sb, at(c, "xnt1_sb", 1))
                    if i is None:
                        pe.wait_ge(s_weights_in, wall)
                    for k in range(TILES):
                        last = mm(one[:, k * E1:(k + 1) * E1], xnt1n[:, k * P:(k + 1) * P], wr[:, :], start=(k == 0), stop=True, skip_group_check=True)
                    last.then_inc(s_router_ps, 1)
                elif name in ("queries1", "keys1"):
                    w = wq1 if name == "queries1" else wk1
                    for f in range(2):
                        mm(pairs[pair][:, f, :], w[:, f * P:(f + 1) * P], xnt1n[:, :], start=True, stop=True).then_inc(s_qk_ps, 1)
                elif name == "values1":
                    for k in range(TILES):
                        last = mm(pairs[pair][:, k // 2, (k % 2) * 2 * P:(k % 2 + 1) * 2 * P], xnt1n[:, k * P:(k + 1) * P], wv1[:, :],
                                  start=(k % 2 == 0), stop=True, skip_group_check=True)
                        if k % 2:
                            last.then_inc(s_v_ps, 1)
                elif name == "weights1":
                    pe.wait_ge(s_w_done, at(c, "w_done", 1))
                    if i is not None:
                        pe.wait_ge(s_oct_sb, at(i, "oct_sb", CB))
                    for k in range(TILES):
                        last = nc.tensor.transpose(bank[4][0:E1, k * P:(k + 1) * P], wtok[:, k, :], ident[:, :])
                    last.then_inc(s_wt_ps, 1)

            def up(i, j):
                if j:
                    pe.wait_ge(s_h_done, at(i, "h_done", j))
                if j == PAIRS:
                    m = mm(bank[6][0:INNER, :], wus[:, :], xnt1[:, :], start=True, stop=True)
                else:
                    m = mm(bank[6], wu[:, j * P:(j + 1) * P], xnt1[:, :], start=True, stop=True)
                m.then_inc(s_up_ps, 1)

            def gate(i, j):
                if j:
                    pe.wait_ge(s_gate_act, at(i, "gate_act", 2 * j))
                else:
                    pe.wait_ge(s_out_done, i + 1)
                    pe.wait_ge(s_cur_done, at(i, "cur_done", 1))
                if j == PAIRS:
                    m = mm(bank[5][0:INNER, :], wgs[:, :], xnt1[:, :], start=True, stop=True)
                else:
                    m = mm(bank[5], wg[:, j * P:(j + 1) * P], xnt1[:, :], start=True, stop=True)
                m.then_inc(s_gate_ps, 1)

            def down(i, j):
                pe.wait_ge(s_h_done, at(i, "h_done", j + 1))
                if j == 0:
                    mm(bank[7], bd[:, :], wt[:, :], start=True, stop=False)
                if j == PAIRS:
                    m = mm(bank[7], wds[:, :], h1[0:INNER, j % HR, :], start=False, stop=True)
                else:
                    m = mm(bank[7], wd[:, j, :], h1[:, j % HR, :], start=False, stop=False)
                m.then_inc(s_acc_ps, 1)

            def scores(pair, row, cols, stat, move, rows, hc0, tile0, width):
                per = 512 // cols
                masked = stat is qa
                for n in range(2):
                    s = pairs[pair][:, n, :].rearrange("p (h c) -> p h c", c=cols)
                    if masked:
                        mm(s[:, :, cols - P:cols], identb[:, :], mask_q[:, 0:per, :], start=True, stop=False, skip_group_check=True)
                    for h in range(per):
                        hc = hc0 + n * per + h
                        last = mm(s[:, h, :], stat[0:rows, hc, row:row + P], move[0:rows, hc, tile0:tile0 + width],
                                  start=(h == 0 and not masked), stop=True, skip_group_check=True)
                return last

            def steps(names, c, i, ring):
                taken = 0
                order = ring + units(names)
                first_c = c if i is None else i

                def take():
                    nonlocal taken
                    if order[taken] is not None:
                        ring_free(pe, i, first_c if taken < 2 else c, order[taken])
                    taken += 1
                    return (taken - 1) % 2

                for step in names:
                    if step[0] == "front":
                        if step[1] in ("load", "norm0", "scale0", "router0", "norm1", "scale1", "choose1"):
                            continue
                        front(step[1], c, i, take() if step[1] in RING else 0)
                    elif step[0] == "setup":
                        pe.wait_ge(s_setup_vec, N_SETUP_VEC)
                    elif step[0] == "moe":
                        j = step[1]
                        n = c if j < MOE_AHEAD else i
                        if j <= PAIRS:
                            gate(n, j)
                        if j >= 2:
                            down(n, j - 2)
                        if 1 <= j <= PAIRS + 1:
                            up(n, j - 1)
                    elif step[0] == "max":
                        _, b, g, u = step
                        if u == 0:
                            if b == 0:
                                pe.wait_ge(s_qk_first, c * QK_IN + QK_IN)
                            else:
                                pe.wait_ge(s_qk_in[g], i * QK_IN + QK_IN)
                        pair = take()
                        if u == 0:
                            last = scores(pair, 0, P, qa, ka, NEG_ROW, GHC * g, 0, P)
                        else:
                            last = scores(pair, P, SEQ, qa, ka, NEG_ROW, GHC * g + 4 * (u - 1), 0, SEQ)
                        last.then_inc(s_max_ps, 1)
                    elif step[0] == "minus":
                        b = step[1]
                        pe.wait_ge(s_mp_done, at(i, "mp_done", b + 1))
                        if b:
                            pe.wait_ge(s_oct_sb, at(i, "oct_sb", b))
                        else:
                            pe.wait_ge(s_wt_sb, at(i, "wt_sb", 1))
                            pe.wait_ge(s_out_done, i + 1)
                        for q in range(2):
                            last = mm(bank[4][0:3 * HC, q * P:(q + 1) * P],
                                      mparts[:, 2 * b + q, :, :].rearrange("p a h -> p (a h)"), identb[:, :],
                                      start=(q == 0), stop=True, skip_group_check=True)
                        last.then_inc(s_mrow_ps, 1)
                    elif step[0] == "score":
                        _, b, g = step
                        if g == 0:
                            pe.wait_ge(s_mrow_in, at(i, "mrow_in", 16 * 3 * (b + 1)))
                        for u in range(3):
                            pair = take()
                            if u < 2:
                                last = scores(pair, 0, SEQ, ka, qa, KROWS, g * GHC + 4 * u, 0, SEQ)
                            else:
                                last = scores(pair, P, P, ka, qa, KROWS, g * GHC, P, P)
                            last.then_inc(s_sc_ps, 1)
                    elif step[0] == "values":
                        _, b, g = step
                        n = b * GROUPS + g
                        if g == 0:
                            pe.wait_ge(s_mrow_sb, at(i, "mrow_sb", b + 1))
                        else:
                            pe.wait_ge(s_o_read, at(i, "o_read", n))
                        pe.wait_ge(s_pk_masked, at(i, "pk_masked", 3 * n + 2))
                        o = bank[4].rearrange("p (c q) -> p c q", c=2)
                        for hh in range(GH):
                            head = g * GH + hh
                            mm(o[32 * hh:32 * hh + 32, :, :], v1[:, 2 * b, head, :], pk0[g % 2][:, 2 * hh:2 * hh + 2, :],
                               start=True, stop=False, skip_group_check=True)
                        pe.wait_ge(s_pk_masked, at(i, "pk_masked", 3 * n + 3))
                        for hh in range(GH):
                            head = g * GH + hh
                            last = mm(o[32 * hh:32 * hh + 32, :, P:SEQ], v1[:, 2 * b + 1, head, :], pk1[g % 2][:, 2 * hh:2 * hh + 2, :],
                                      start=False, stop=True, skip_group_check=True)
                        last.then_inc(s_pv_ps, 1)
                    elif step[0] == "back":
                        _, b, g = step
                        pe.wait_ge(s_ot_sb, at(i, "ot_sb", b * GROUPS + g + 1))
                        for q in range(2):
                            for k in range(2):
                                n = 2 * q + k
                                last = nc.tensor.transpose(bank[4][:, n * P:(n + 1) * P], ot[:, k, q * P:(q + 1) * P], ident[:, :])
                        last.then_inc(s_ot_ps, 1)
                    elif step[0] == "turn":
                        b = step[1]
                        pe.wait_ge(s_on_done, at(i, "on_done", b + 1))
                        for q in range(2):
                            for f in range(2):
                                n = 2 * f + q
                                last = nc.tensor.transpose(bank[4][:, n * P:(n + 1) * P], on[:, q, f * P:(f + 1) * P], ident[:, :])
                        last.then_inc(s_oct_ps, 1)
                    elif step[0] == "end":
                        pe.wait_ge(s_oct_sb, at(i, "oct_sb", CB))
                        if c is not None:
                            pe.wait_ge(s_wt_sb, at(c, "wt_sb", 1))
                        for f in range(2):
                            last = mm(bank[4], wo1s[:, f, :], oct_[:, f, :], start=(f == 0), stop=(f == 1))
                        last.then_inc(s_s1_ps, 1)
                    elif step[0] == "fin":
                        pe.wait_ge(s_fg_done, at(i, "fg_done", 1))
                        for k in range(TILES):
                            last = nc.tensor.transpose(bank[5][:, k * P:(k + 1) * P], fg[:, k * P:(k + 1) * P], ident[:, :])
                        last.then_inc(s_fin_ps, 1)

            steps(OPENING, 0, None, [None, None])
            with pe.Fori(0, CHUNKS - 1) as i:
                steps(ROUND, i + 1, i, units(OPENING)[-2:])
            assert units(OPENING)[-2:] == units(ROUND)[-2:]
            steps(LAST, None, CHUNKS - 1, units(ROUND)[-2:])

        @block.scalar
        def _(act):
            A = nc.scalar.activation

            def front(name, c, i, pair):
                if name == "turn0":
                    act.wait_ge(s_xnt_ps, at(c, "xnt_ps", 1))
                    A(xnt[:, :], pairs[pair][:, 0, :], ACT.Copy).then_inc(s_xnt_sb, 1)
                    if i is None:
                        act.wait_ge(s_mt_done, 1)
                        A(mt[:, :], bank[4][:, 0:P], ACT.Copy).then_inc(s_mt_copied, 1)
                elif name == "keys0":
                    act.wait_ge(s_yk_ps, at(c, "yk_ps", 1))
                    A(yk[:, :], pairs[pair][:, 0, :], ACT.Copy).then_inc(s_yk_sb, 1)
                elif name == "router0":
                    act.wait_ge(s_lsub, at(c, "lsub", 1))
                    A(lexp[:, :, :], logit[:, :, :], ACT.Exp).then_inc(s_lexp_done, 1)
                elif name == "inner0":
                    if i is None:
                        act.wait_ge(s_vo_done, 1)
                        A(vo[:, :], bank[5][:, 0:P], ACT.Copy).then_inc(s_vo_copied, 1)
                    act.wait_ge(s_vw_ps, at(c, "vw_ps", 1))
                    A(vw[:, :, :], pairs[pair][:, 1, :].rearrange("p (c d) -> p c d", d=D), ACT.Copy).then_inc(s_vw_sb, 1)
                elif name == "scores0":
                    act.wait_ge(s_nb0, at(c, "nb0", 1))
                    for k in range(TILES):
                        w = P if k % 2 == 0 else SEQ
                        o = 0 if k % 2 == 0 else P
                        A(p0[:, k, 0:w], pairs[pair][:, k // 2, o:o + w], ACT.Exp, bias=nbias0[:, k:k + 1], scale=SCALE0,
                          accum_out=l0[:, k:k + 1]).then_inc(s_p0_done, 1)
                elif name == "picks0":
                    for j in range(2):
                        act.wait_ge(s_umt_ps, at(c, "umt_ps", j + 1))
                        A(umt[:, j, :], pairs[pair][:, j, :], ACT.Copy).then_inc(s_umt_sb, 1)
                elif name == "probs0":
                    for b in range(CB):
                        act.wait_ge(s_pt_ps, at(c, "pt_ps", b + 1))
                        A(pt0[:, b, :], pairs[pair][:, b, 0:3 * P], ACT.Copy).then_inc(s_pt_sb, 1)
                elif name.startswith("hidden"):
                    if i is None and name == "hidden0":
                        act.wait_ge(s_ffn_in, 16 * 5)
                    for n in range(2):
                        f = 2 * int(name[6:]) + n
                        act.wait_ge(s_inter_ps, at(c, "inter_ps", f + 1))
                        A(ha[:, f, :], pairs[pair][:, n, :], ACT.Relu, bias=bi[:, f:f + 1]).then_inc(s_ha_done, 1)
                elif name == "out0":
                    act.wait_ge(s_z_ps, at(c, "z_ps", 1))
                    for k in range(TILES):
                        A(th0[:, k, :], pairs[pair][:, 1, k * P:(k + 1) * P], ACT.Tanh, scale=hvs[:, k:k + 1]).then_inc(s_th0_done, 1)
                elif name == "turn1":
                    act.wait_ge(s_xnt1_ps, at(c, "xnt1_ps", 1))
                    A(xnt1n[:, :], pairs[pair][:, 0, :], ACT.Copy).then_inc(s_xnt1_sb, 1)
                elif name == "router1":
                    act.wait_ge(s_rl_done, at(c, "rl_done", 1))
                    A(rexp[:, :, :], rlog[:, :, :], ACT.Exp, scale=-1.0).then_inc(s_rexp_done, 1)
                elif name in ("queries1", "keys1"):
                    if i is not None and name == "queries1":
                        act.wait_ge(s_pv_ps, at(i, "pv_ps", CB * GROUPS))
                    for f in range(2):
                        n = f if name == "queries1" else 2 + f
                        act.wait_ge(s_qk_ps, at(c, "qk_ps", n + 1))
                        A(qkf[:, n, :], pairs[pair][:, f, :], ACT.Copy).then_inc(s_qkf_done, 1)
                        A(parts[:, 0, n, :], pairs[pair][:, f, :], ACT.Copy).then_inc(s_part1, 1)
                elif name == "weights1":
                    if i is not None:
                        act.wait_ge(s_acc_ps, at(i, "acc_ps", 1))
                    act.wait_ge(s_wt_ps, at(c, "wt_ps", 1))
                    A(wt[:, :], bank[4][0:E1, :], ACT.Copy).then_inc(s_wt_sb, 1)
                    if i is None:
                        act.wait_ge(s_wt_sb, 1)
                        act.dma_start(t["wt_dram"], wt[:, :]).then_inc(s_wt_stored, 16)

            def steps(names, c, i):
                taken = 0
                for step in names:
                    name = step[1] if step[0] == "front" else step[0]
                    pair = taken % 2
                    if step[0] == "front":
                        front(name, c, i, pair)
                    elif step[0] == "begin":
                        A(xnt1[:, :], xnt1n[:, :], ACT.Copy).then_inc(s_cur_done, 1)
                        if i is None:
                            act.wait_ge(s_wt_stored, 16)
                            load_wb(act, 0)
                            load_wb(act, 1)
                    elif step[0] == "setup":
                        act.wait_ge(s_lam_exp, 1)
                        A(lam_e[:, :, :], lam_e[:, :, :], ACT.Exp).then_inc(s_setup_act, 1)
                        act.wait_ge(s_setup_vec, N_SETUP_VEC)
                        act.wait_ge(s_weights_in, wall)
                    elif step[0] == "moe":
                        j = step[1]
                        m = c if j < MOE_AHEAD else i
                        if j <= PAIRS:
                            rows = INNER if j == PAIRS else P
                            act.wait_ge(s_gate_ps, at(m, "gate_ps", j + 1))
                            if j >= 2:
                                act.wait_ge(s_h_done, at(m, "h_done", j - 1))
                            A(gt[0:rows, j % 2, :], bank[5][0:rows, :], ACT.Tanh, bias=bgh[0:rows, j:j + 1], scale=0.5).then_inc(s_gate_act, 1)
                            half, b = (0.5, bgh) if j == PAIRS else (1.0, bg)
                            A(gb[0:rows, j % 2, :], bank[5][0:rows, :], ACT.Identity, bias=b[0:rows, j:j + 1], scale=half).then_inc(s_gate_act, 1)
                    elif step[0] == "minus":
                        b = step[1]
                        act.wait_ge(s_mrow_ps, at(i, "mrow_ps", b + 1))
                        A(mrows[:, b * SEQ:(b + 1) * SEQ], bank[4][0:3 * HC, 0:SEQ], ACT.Copy).then_inc(s_mrow_sb, 1)
                        act.wait_ge(s_mrow_sb, at(i, "mrow_sb", b + 1))
                        for a in range(3):
                            act.dma_start(qa[NEG_ROW + a:NEG_ROW + a + 1, :, :],
                                          mrows[a * HC:(a + 1) * HC, b * SEQ:(b + 1) * SEQ]).then_inc(s_mrow_in, 16)
                    elif step[0] == "score":
                        _, b, g = step
                        n = b * GROUPS + g
                        if n >= 2:
                            act.wait_ge(s_pv_ps, at(i, "pv_ps", n - 1))
                        for u in range(3):
                            act.wait_ge(s_sc_ps, at(i, "sc_ps", 3 * n + u + 1))
                            src = pairs[(taken + u) % 2][:, :, :]
                            if u < 2:
                                dst = pk0[g % 2][:, 4 * u:4 * u + 4, :]
                                src = src.rearrange("p n (h c) -> p (n h) c", c=SEQ)
                            else:
                                dst = pk1[g % 2]
                                src = src.rearrange("p n (h c) -> p (n h) c", c=P)
                            A(dst, src, ACT.Exp, scale=SCALE1).then_inc(s_pk_done, 1)
                    elif step[0] == "values":
                        n = step[1] * GROUPS + step[2]
                        act.wait_ge(s_pv_ps, at(i, "pv_ps", n + 1))
                        if n:
                            act.wait_ge(s_ot_ps, at(i, "ot_ps", n))
                        A(ot[:, :, :], bank[4].rearrange("p (c q) -> p c q", c=2), ACT.Copy).then_inc(s_ot_sb, 1)
                    elif step[0] == "turn":
                        b = step[1]
                        act.wait_ge(s_oct_ps, at(i, "oct_ps", b + 1))
                        A(oct_[:, :, b * SEQ:(b + 1) * SEQ], bank[4].rearrange("p (f q) -> p f q", f=2), ACT.Copy).then_inc(s_oct_sb, 1)
                    elif step[0] == "end":
                        act.wait_ge(s_acc_ps, at(i, "acc_ps", PAIRS + 1))
                        A(fth[:, :], bank[7], ACT.Tanh, bias=bdsh[:, :], scale=0.5).then_inc(s_fth_done, 1)
                        A(fvh[:, :], bank[7], ACT.Identity, bias=bdsh[:, :], scale=0.5).then_inc(s_fth_done, 1)
                    taken += RING.get(name, 0)

            steps(OPENING, 0, None)
            with act.Fori(0, CHUNKS - 1) as i:
                steps(ROUND, i + 1, i)
            steps(LAST, None, CHUNKS - 1)

        @block.gpsimd
        def _(pool):
            def const(ins):
                ins.then_inc(s_consts_ready, 1)

            const(pool.iota(iota8[:, :], pattern=[[1, E0]], base=0, channel_multiplier=0, allow_small_or_imprecise_dtypes=True))
            const(pool.memset(minus_half[:, :], -0.5))
            const(pool.memset(ident[:, :], 0.0))
            const(pool.memset(identb[:, :], 0.0))
            const(pool.memset(mask_q[:, :, :], 0.0))
            const(pool.memset(zero[:, :], 0.0))
            pool.wait_ge(s_consts_ready, 6)
            for m in (ident, identb):
                const(pool.affine_select(out=m[:, :], in_=m[:, :], compare_op=ALU.not_equal, fill=1.0, base=0,
                                         pattern=[[-1, P]], channel_multiplier=1))
            const(pool.affine_select(out=mask_q[:, :, :], in_=mask_q[:, :, :], compare_op=ALU.is_ge, fill=MASKED, base=0,
                                     pattern=[[0, 4], [-1, P]], channel_multiplier=1))
            pool.wait_ge(s_consts_ready, N_CONSTS)

            pw = nc.gpsimd.tensor_tensor
            def steps(names, c, i):
                for step in names:
                    if step == ("front", "norm0"):
                        pool.wait_ge(s_var0, at(c, "var0", 1))
                        pw(rstd[:, :], vare[:, :], minus_half[:, 0:TILES], ALU.pow).then_inc(s_rstd0, 1)
                        if i is None:
                            pool.memset(qa[0:NEG_ROW, :, :], 0.0).then_inc(s_rooms, 1)
                            pool.memset(ka[0:NEG_ROW, :, :], 0.0).then_inc(s_rooms, 1)
                            pool.wait_ge(s_rooms, 2)
                            pool.memset(ka[NEG_ROW:KROWS, :, :], 1.0).then_inc(s_rooms, 1)
                            pool.wait_ge(s_rooms, 3)
                            pool.memset(v1[:, :, :, :], 0.0).then_inc(s_rooms, 1)
                            pool.wait_ge(s_rooms, 4)
                            pool.memset(v1[:, :, :, DV:DV + 1], 1.0).then_inc(s_rooms, 1)
                    elif step == ("front", "norm1"):
                        pool.wait_ge(s_var1, at(c, "var1", 1))
                        pw(rstd[:, :], vare[:, :], minus_half[:, 0:TILES], ALU.pow).then_inc(s_rstd1, 1)
                    elif step[0] == "front" and step[1].startswith("hidden"):
                        for n in range(2):
                            f = 2 * int(step[1][6:]) + n
                            pool.wait_ge(s_ha_done, at(c, "ha_done", f + 1))
                            pool.wait_ge(s_hb_done, at(c, "hb_done", f + 1))
                            pw(ha[:, f, :], ha[:, f, :], hb[:, f % 2, :], ALU.add).then_inc(s_hsum_done, 1)
                    elif step[0] == "front" and step[1] in ("queries1", "keys1"):
                        for n in ((0, 1) if step[1] == "queries1" else (2, 3)):
                            pool.wait_ge(s_part2, at(c, "part2", n + 1))
                            pw(parts[:, 2, n, :], qkf[:, n, :], parts[:, 1, n, :], ALU.subtract).then_inc(s_part3, 1)
                    elif step[0] == "keep":
                        pool.wait_ge(s_xn1_done, at(i, "xn1_done", TILES))
                        pw(out[:, :, :], x1[:, :, :], zero[:, 0:1].unsqueeze(2).to_broadcast([P, TILES, D]), ALU.add).then_inc(s_keep_done, 1)
                    elif step[0] == "score":
                        _, b, g = step
                        for u, (dst, n) in enumerate(((pk0[g % 2][:, 0:4, 0:P], 4), (pk0[g % 2][:, 4:8, 0:P], 4), (pk1[g % 2], 8))):
                            pool.wait_ge(s_pk_done, at(i, "pk_done", 3 * (b * GROUPS + g) + u + 1))
                            w = 2 + 3 * (g % 2) + u
                            pw(waited[:, w:w + 1], minus_half[:, 0:1], minus_half[:, 0:1], ALU.add)
                            pool.affine_select(out=dst, in_=dst, compare_op=ALU.is_ge, fill=0.0, base=0,
                                               pattern=[[0, n], [1, P]], channel_multiplier=-1).then_inc(s_pk_masked, 1)
                    elif step[0] == "moe" and step[1] <= PAIRS:
                        j = step[1]
                        m = c if j < MOE_AHEAD else i
                        if j < PAIRS:
                            k = j // 2
                            pool.wait_ge(s_gate_act, at(m, "gate_act", 2 * j + 2))
                            pool.wait_ge(s_wb_in[k % 2], m * WB_IN + 32 * (k // 2 + 1))
                            pw(gb[:, j % 2, :], gb[:, j % 2, :], wb[:, k % 2, j % 2, :], ALU.mult).then_inc(s_ga_done, 1)
                    elif step[0] == "norm":
                        b = step[1]
                        pool.wait_ge(s_ms_done, at(i, "ms_done", b + 1))
                        pw(orms[:, :, :], oms[:, :, :], minus_half[:, :].rearrange("p (a b) -> p a b", a=2), ALU.pow).then_inc(s_orms_done, 1)
                    elif step[0] == "stored":
                        pool.wait_ge(s_out_stored, at(i, "out_stored", 16))

            steps(OPENING, 0, None)
            with pool.Fori(0, CHUNKS - 1) as i:
                steps(ROUND, i + 1, i)
            steps(LAST, None, CHUNKS - 1)

        @block.vector
        def _(dve):
            V = nc.vector
            count = [0]
            base_i = [None]

            def link(ins, by_copy=False):
                count[0] += 1
                ins.then_inc(s_dve_link, 1)
                if base_i[0] is None:
                    dve.wait_ge(s_dve_link, count[0])
                else:
                    dve.wait_ge(s_dve_link, base_i[0] + count[0])
                    if by_copy:
                        V.tensor_copy(waited[:, 0:1], iota8[:, 0:1])

            def setup(ins):
                ins.then_inc(s_setup_vec, 1)

            V.memset(waited[:, 1:2], 0.0).then_inc(s_out_done, 1)
            setup(V.memset(twos_row[:, :], 2.0))
            dve.wait_ge(s_consts_ready, N_CONSTS)

            def setup_late():
                dve.wait_ge(s_weights_in, wall)
                setup(V.tensor_scalar(bgh[:, 0:PAIRS], bg[:, 0:PAIRS], 0.5, None, ALU.mult))
                setup(V.tensor_scalar(bgh[0:INNER, PAIRS:], bg[0:INNER, PAIRS:], 0.5, None, ALU.mult))
                setup(V.tensor_scalar(bd[:, :], bd[:, :], 2.0, None, ALU.mult))
                setup(V.tensor_scalar(bdsh[:, :], bds[:, :], 0.5, None, ALU.mult))
                for f in range(2):
                    setup(V.tensor_scalar(wo1s[:, f, :], wo1[:, f, :], rms_col[:, 0:1], 1.0 - LAM0, ALU.mult, ALU.mult))
                link(V.tensor_tensor(lam_in[:, 0, :], lam_in[:, 0, :], lam_in[:, 1, :], ALU.mult))
                link(V.tensor_tensor(lam_in[:, 2, :], lam_in[:, 2, :], lam_in[:, 3, :], ALU.mult))
                link(V.reduce_sum(lam_e[:, 0, :], lam_in[:, 0, :].rearrange("p (h d) -> p h d", d=DH), AX))
                V.reduce_sum(lam_e[:, 1, :], lam_in[:, 2, :].rearrange("p (h d) -> p h d", d=DH), AX).then_inc(s_lam_exp, 1)
                dve.wait_ge(s_setup_act, 1)
                link(V.scalar_tensor_tensor(out=lam[:, :], in0=lam_e[:, 0, :], scalar=LAM0, in1=lam_e[:, 1, :],
                                            op0=ALU.add, op1=ALU.subtract))

            def statistics(src, var_ready):
                for c in range(TILES):
                    ins = V.bn_stats(stats[:, c, :], src[:, c, :])
                link(ins, True)
                for c in range(TILES):
                    ins = V.bn_aggr(mv[:, c, :], stats[:, c, :])
                link(ins)
                V.tensor_scalar(vare[:, :], mv[:, :, 1], EPS, None, ALU.add).then_inc(var_ready, 1)

            def scale(src, dst, done):
                for c in range(TILES):
                    V.tensor_scalar(dst[:, c, :], src[:, c, :], mv[:, c, 0:1], rstd[:, c:c + 1], ALU.subtract, ALU.mult).then_inc(done, 1)

            def wide(ap, n):
                return ap.unsqueeze(2).to_broadcast([P, ap.shape[1], n])

            def front(name, c, i, pair):
                one, two = pairs[pair][:, 0, :], pairs[pair][:, 1, :]
                if name == "norm0":
                    dve.wait_ge(s_x_in, at(c, "x_in", 16))
                    statistics(x, s_var0)
                elif name == "scale0":
                    dve.wait_ge(s_rstd0, at(c, "rstd0", 1))
                    scale(x, xn, s_xn0)
                elif name == "keys0":
                    if i is None:
                        dve.wait_ge(s_early_in, 16 * 3)
                    dve.wait_ge(s_logits_ps, at(c, "logits_ps", 1))
                    link(V.tensor_tensor(logit[:, :, :], two[:, 0:TILES * E0].rearrange("p (c e) -> p c e", e=E0),
                                         gate_b[:, :].unsqueeze(1).to_broadcast([P, TILES, E0]), ALU.add))
                    link(V.reduce_max(lmax[:, :], logit[:, :, :], AX))
                    V.tensor_tensor(logit[:, :, :], logit[:, :, :], wide(lmax[:, :], E0), ALU.subtract).then_inc(s_lsub, 1)
                elif name == "router0":
                    dve.wait_ge(s_lexp_done, at(c, "lexp_done", 1))
                    link(V.reduce_sum(lsum[:, :], lexp[:, :, :], AX))
                    link(V.reciprocal(lsum[:, :], lsum[:, :]))
                    link(V.tensor_tensor(lexp[:, :, :], lexp[:, :, :], wide(lsum[:, :], E0), ALU.mult), True)
                    for k in range(TILES):
                        ins = V.max(top[:, k, :], lexp[:, k, :])
                    link(ins, True)
                    for k in range(TILES):
                        ins = V.max_index(topi[:, k, :], top[:, k, :], lexp[:, k, :])
                    link(ins)
                    link(V.tensor_copy(topf[:, :, :], topi[:, :, 0:2]))
                    for j in range(2):
                        ins = V.tensor_tensor(pick[:, j, :, :], iota8[:, :].unsqueeze(1).to_broadcast([P, TILES, E0]),
                                              topf[:, :, j:j + 1].to_broadcast([P, TILES, E0]), ALU.is_equal)
                    link(ins)
                    link(V.tensor_tensor(pick[:, 1, :, :], pick[:, 1, :, :], pick[:, 0, :, :], ALU.subtract))
                    link(V.tensor_tensor(hvs[:, :], top[:, :, 0], top[:, :, 1], ALU.add))
                    link(V.tensor_scalar(hvs[:, :], hvs[:, :], 0.5, None, ALU.mult))
                elif name == "inner0":
                    dve.wait_ge(s_u_ps, at(c, "u_ps", 1))
                    for j in range(2):
                        V.tensor_tensor(um[:, j, :, :].rearrange("p c (e r) -> p (c e) r", r=R0),
                                        one.rearrange("p (g r) -> p g r", r=R0),
                                        wide(pick[:, j, :, :].rearrange("p c e -> p (c e)"), R0), ALU.mult).then_inc(s_um_done, 1)
                elif name == "scores0":
                    for b in range(CB):
                        dve.wait_ge(s_s0_ps, at(c, "s0_ps", b + 1))
                        V.tensor_reduce(nmax0[:, 2 * b:2 * b + 1], pairs[pair][:, b, 0:P], AX, ALU.max, negate=True)
                        ins = V.tensor_reduce(nmax0[:, 2 * b + 1:2 * b + 2], pairs[pair][:, b, P:3 * P], AX, ALU.max, negate=True)
                    link(ins)
                    V.tensor_scalar(nbias0[:, :], nmax0[:, :], SCALE0, None, ALU.mult).then_inc(s_nb0, 1)
                elif name.startswith("hidden"):
                    if i is None and name == "hidden0":
                        dve.wait_ge(s_ffn_in, 16 * 5)
                    for n in range(2):
                        f = 2 * int(name[6:]) + n
                        dve.wait_ge(s_inter2_ps, at(c, "inter2_ps", f + 1))
                        if f >= 2:
                            dve.wait_ge(s_hsum_done, at(c, "hsum_done", f - 1))
                        V.tensor_scalar(hb[:, f % 2, :], pairs[pair][:, n, :], bi[:, f:f + 1], 0.0, ALU.add, ALU.max).then_inc(s_hb_done, 1)
                elif name == "out0":
                    dve.wait_ge(s_p0_done, at(c, "p0_done", TILES))
                    link(V.reciprocal(rl0[:, :], l0[:, :]))
                    dve.wait_ge(s_att_ps, at(c, "att_ps", 1))
                    link(V.tensor_tensor(tmp0[:, :, :], one.rearrange("p (c d) -> p c d", d=D), wide(rl0[:, :], D), ALU.mult))
                    dve.wait_ge(s_th0_done, at(c, "th0_done", TILES))
                    V.tensor_tensor(gate0[:, :, :], two.rearrange("p (c d) -> p c d", d=D), wide(hvs[:, :], D), ALU.mult).then_inc(s_z_read, 1)
                    dve.wait_ge(s_z_read, at(c, "z_read", 1))
                    link(V.scalar_tensor_tensor(out=gate0[:, :, :], in0=th0[:, :, :], scalar=1.0, in1=gate0[:, :, :],
                                                op0=ALU.add, op1=ALU.mult))
                    link(V.tensor_tensor(gate0[:, :, :], gate0[:, :, :], tmp0[:, :, :], ALU.mult))
                    if i is not None:
                        dve.wait_ge(s_keep_done, at(i, "keep_done", 1))
                    link(V.tensor_tensor(x1[:, :, :], x[:, :, :], gate0[:, :, :], ALU.add))
                elif name == "norm1":
                    statistics(x1, s_var1)
                elif name == "scale1":
                    dve.wait_ge(s_rstd1, at(c, "rstd1", 1))
                    scale(x1, xn1, s_xn1_done)
                elif name == "router1":
                    if i is None:
                        dve.wait_ge(s_weights_in, wall)
                    dve.wait_ge(s_router_ps, at(c, "router_ps", 1))
                    V.tensor_tensor(rlog[:, :, :], one[:, 0:TILES * E1].rearrange("p (c e) -> p c e", e=E1),
                                    br[:, :].unsqueeze(1).to_broadcast([P, TILES, E1]), ALU.add).then_inc(s_rl_done, 1)
                elif name == "choose1":
                    dve.wait_ge(s_rexp_done, at(c, "rexp_done", 1))
                    link(V.tensor_scalar(aff[:, :, :], rexp[:, :, :], 1.0, None, ALU.add))
                    link(V.reciprocal(aff[:, :, :], aff[:, :, :]), True)
                    for k in range(TILES):
                        ins = V.max(top1[:, k, :], aff[:, k, :])
                    link(ins, True)
                    for k in range(TILES):
                        ins = V.match_replace(rest1[:, k, :], top1[:, k, :], aff[:, k, :], -1.0)
                    link(ins)
                    link(V.scalar_tensor_tensor(out=wtok[:, :, :], in0=rest1[:, :, :], scalar=0.0, in1=aff[:, :, :],
                                                op0=ALU.is_lt, op1=ALU.mult))
                    link(V.reduce_sum(wsum[:, :], top1[:, :, :], AX))
                    link(V.tensor_scalar(wsum[:, :], wsum[:, :], 1e-9, 2.0, ALU.add, ALU.mult))
                    link(V.reciprocal(wsum[:, :], wsum[:, :]))
                    V.tensor_tensor(wtok[:, :, :], wtok[:, :, :], wide(wsum[:, :], E1), ALU.mult).then_inc(s_w_done, 1)
                elif name in ("queries1", "keys1"):
                    for n in ((0, 1) if name == "queries1" else (2, 3)):
                        dve.wait_ge(s_qkf_done, at(c, "qkf_done", n + 1))
                        dve.wait_ge(s_part1, at(c, "part1", n + 1))
                        link(V.tensor_tensor(qkf[:, n, :], qkf[:, n, :], parts[:, 0, n, :], ALU.subtract))
                        V.tensor_copy(parts[:, 1, n, :], qkf[:, n, :]).then_inc(s_part2, 1)
                elif name == "values1":
                    if i is not None:
                        dve.wait_ge(s_pv_ps, at(i, "pv_ps", CB * GROUPS))
                    else:
                        dve.wait_ge(s_rooms, 5)
                    for n in range(2):
                        dve.wait_ge(s_v_ps, at(c, "v_ps", n + 1))
                        V.tensor_copy(v1[:, 2 * n:2 * n + 2, :, 0:DV].rearrange("p c h d -> p (c h) d"),
                                      pairs[pair][:, n, :].rearrange("p (g d) -> p g d", d=DV)).then_inc(s_v_sb, 1)

            def experts(i, j):
                rows = INNER if j == PAIRS else P
                dve.wait_ge(s_gate_act, at(i, "gate_act", 2 * j + 2))
                if j < PAIRS:
                    dve.wait_ge(s_ga_done, at(i, "ga_done", j + 1))
                if j >= HR:
                    dve.wait_ge(s_acc_ps, at(i, "acc_ps", j - HR + 1))
                link(V.scalar_tensor_tensor(out=h1[0:rows, j % HR, :], in0=gt[0:rows, j % 2, :], scalar=1.0,
                                            in1=gb[0:rows, j % 2, :], op0=ALU.add, op1=ALU.mult))
                dve.wait_ge(s_up_ps, at(i, "up_ps", j + 1))
                V.scalar_tensor_tensor(out=h1[0:rows, j % HR, :], in0=bank[6][0:rows, :], scalar=bu[0:rows, j:j + 1],
                                       in1=h1[0:rows, j % HR, :], op0=ALU.add, op1=ALU.mult).then_inc(s_h_done, 1)

            def steps(names, c, i, links):
                base_i[0] = links
                count[0] = 0
                taken = 0
                for step in names:
                    name = step[1] if step[0] == "front" else step[0]
                    pair = taken % 2
                    taken += RING.get(name, 0)
                    if step[0] == "front":
                        front(name, c, i, pair)
                    elif step[0] == "moe":
                        if 1 <= step[1] <= PAIRS + 1:
                            experts(c if step[1] < MOE_AHEAD else i, step[1] - 1)
                    elif step[0] == "setup":
                        setup_late()
                    elif step[0] == "max":
                        _, b, g, u = step
                        dve.wait_ge(s_max_ps, at(i if b else c, "max_ps", b * MAX_UNITS + 3 * g + u + 1))
                        if u == 0:
                            src = pairs[pair][:, :, :].rearrange("p n (h c) -> p (n h) c", c=P)
                            dst = nmax1[:, 2 * b, GHC * g:GHC * (g + 1)]
                        else:
                            src = pairs[pair][:, :, :].rearrange("p n (h c) -> p (n h) c", c=SEQ)
                            dst = nmax1[:, 2 * b + 1, GHC * g + 4 * (u - 1):GHC * g + 4 * u]
                        V.tensor_reduce(dst, src, AX, ALU.max, negate=True).then_inc(s_nmax_done, 1)
                    elif step[0] == "minus":
                        b = step[1]
                        dve.wait_ge(s_nmax_done, at(i, "nmax_done", (b + 1) * MAX_UNITS))
                        k = slice(2 * b, 2 * b + 2)
                        link(V.tensor_copy(mparts[:, k, 0, :], nmax1[:, k, :]))
                        link(V.tensor_tensor(mres[:, k, :], nmax1[:, k, :], mparts[:, k, 0, :], ALU.subtract))
                        link(V.tensor_copy(mparts[:, k, 1, :], mres[:, k, :]))
                        V.tensor_tensor(mparts[:, k, 2, :], mres[:, k, :], mparts[:, k, 1, :], ALU.subtract).then_inc(s_mp_done, 1)
                    elif step[0] == "back":
                        _, b, g = step
                        n = b * GROUPS + g
                        dve.wait_ge(s_ot_ps, at(i, "ot_ps", n + 1))
                        o = bank[4].rearrange("p (g w) -> p g w", w=VW1)
                        rl = rl1[:, :, :, :].rearrange("p q c h -> p (q c h)")
                        link(V.reciprocal(rl, o[:, :, DV]))
                        V.tensor_tensor(o12[:, :, :, :, :].rearrange("p q c h d -> p (q c h) d"), o[:, :, 0:DV],
                                        wide(rl, DV), ALU.mult).then_inc(s_o_read, 1)
                        dve.wait_ge(s_o_read, at(i, "o_read", n + 1))
                        link(V.tensor_tensor(o12[:, :, 1, :, :], o12[:, :, 1, :, :],
                                             lam[:, g * GH:(g + 1) * GH].unsqueeze(1).unsqueeze(3).to_broadcast([P, 2, GH, DV]), ALU.mult))
                        V.tensor_tensor(oc[:, 2 * b:2 * b + 2, g * GH * DV:(g + 1) * GH * DV],
                                        o12[:, :, 0, :, :].rearrange("p q h d -> p q (h d)"),
                                        o12[:, :, 1, :, :].rearrange("p q h d -> p q (h d)"), ALU.subtract).then_inc(s_oc_done, 1)
                    elif step[0] == "norm":
                        b = step[1]
                        dve.wait_ge(s_oc_done, at(i, "oc_done", GROUPS * (b + 1)))
                        k = slice(2 * b, 2 * b + 2)
                        link(V.tensor_tensor(osq[:, :, :], oc[:, k, :], oc[:, k, :], ALU.mult))
                        link(V.reduce_sum(oms[:, :, :].rearrange("p q h -> p (q h)"),
                                          osq[:, :, :].rearrange("p q (h d) -> p (q h) d", d=DV), AX))
                        V.tensor_scalar(oms[:, :, :], oms[:, :, :], 1.0 / DV, EPS, ALU.mult, ALU.add).then_inc(s_ms_done, 1)
                    elif step[0] == "turn":
                        b = step[1]
                        k = slice(2 * b, 2 * b + 2)
                        dve.wait_ge(s_orms_done, at(i, "orms_done", b + 1))
                        V.tensor_tensor(on[:, :, :].rearrange("p q (h d) -> p (q h) d", d=DV),
                                        oc[:, k, :].rearrange("p q (h d) -> p (q h) d", d=DV),
                                        wide(orms[:, :, :].rearrange("p q h -> p (q h)"), DV), ALU.mult).then_inc(s_on_done, 1)
                    elif step[0] == "end":
                        dve.wait_ge(s_fth_done, at(i, "fth_done", 2))
                        link(V.scalar_tensor_tensor(out=fg[:, :], in0=fth[:, :], scalar=1.0, in1=fvh[:, :], op0=ALU.add, op1=ALU.mult))
                        dve.wait_ge(s_s1_ps, at(i, "s1_ps", 1))
                        V.tensor_tensor(fg[:, :], bank[4], fg[:, :], ALU.mult).then_inc(s_fg_done, 1)
                    elif step[0] == "fin":
                        dve.wait_ge(s_fin_ps, at(i, "fin_ps", 1))
                        dve.wait_ge(s_keep_done, at(i, "keep_done", 1))
                        V.tensor_tensor(out[:, :, :], out[:, :, :], bank[5].rearrange("p (c d) -> p c d", d=D), ALU.add).then_inc(s_out_done, 1)
                return count[0]

            n = steps(OPENING, 0, None, 0)
            assert n == OPEN_LINKS, n
            with dve.Fori(0, CHUNKS - 1) as i:
                n = steps(ROUND, i + 1, i, OPEN_LINKS + i * ROUND_LINKS)
            assert n == ROUND_LINKS, n
            steps(LAST, None, CHUNKS - 1, OPEN_LINKS + (CHUNKS - 1) * ROUND_LINKS)


def l0_and_l1_kernel(nc, a, out):
    t = dict(a)
    t["out"] = out
    t["parts_dram"] = nc.dram_tensor("parts_scratch", (2, HC, 3 * DH, CHUNK), BF16, kind="Internal").ap()
    t["wt_dram"] = nc.dram_tensor("wt_scratch", (E1, CHUNK), F32, kind="Internal").ap()
    build(nc, t)


def kernel(**inputs):
    import numpy as _np
    import concourse.bacc as _bacc
    from concourse import mybir as _mybir
    from concourse.bass_utils import run_bass_kernel_spmd as _run

    v = {k: _np.asarray(x) for k, x in inputs.items()}

    def rows(w, n):
        return w.reshape(n, -1, w.shape[1]).transpose(1, 0, 2)

    a = {
        "x": v["L0_attn_in_features"].reshape(CHUNKS, TILES, P, D).transpose(0, 2, 1, 3),
        "wkq": _np.stack([rows(v["L0_attn_w_k"], OT).reshape(P, -1), rows(v["L0_attn_w_q"], OT).reshape(P, -1)], 1),
        "wvo": _np.stack([rows(v["L0_attn_w_v"], OT).reshape(P, -1), rows(v["L0_attn_w_o"].T, OT).reshape(P, -1)], 1),
        "wi_t": v["L0_ffn_wi"].T,
        "bi": v["L0_ffn_bi"].reshape(FB, P).T,
        "wo_t": rows(v["L0_ffn_wo"].T, FB),
        "bo": v["L0_ffn_bo"].reshape(1, P),
        "la": v["L0_ffn_lora_A"].reshape(E0 * R0, D).T,
        "lb": v["L0_ffn_lora_B"].transpose(0, 2, 1).reshape(E0 * R0, 512),
        "gate_w": v["L0_ffn_gate_w"].T,
        "gate_b": v["L0_ffn_gate_b"],
        "wq1": v["L1_attn_Wq"].T, "wk1": v["L1_attn_Wk"].T, "wv1": v["L1_attn_Wv"].T,
        "wo1": rows(v["L1_attn_Wo"].T, 2),
        "lq1": v["L1_attn_lq1"].reshape(-1), "lk1": v["L1_attn_lk1"].reshape(-1),
        "lq2": v["L1_attn_lq2"].reshape(-1), "lk2": v["L1_attn_lk2"].reshape(-1),
        "rms": v["L1_attn_rms_scale"].reshape(DV, 1),
        "wr": v["L1_ffn_Wr"], "br": v["L1_ffn_br"],
        "wg": v["L1_ffn_Wg"].transpose(1, 0, 2).reshape(D, -1), "wu": v["L1_ffn_Wu"].transpose(1, 0, 2).reshape(D, -1),
        "wd": v["L1_ffn_Wd"].reshape(PAIRS, P, D).transpose(1, 0, 2),
        "bg": v["L1_ffn_bg"].reshape(PAIRS, P).T, "bu": v["L1_ffn_bu"].reshape(PAIRS, P).T,
        "bd": v["L1_ffn_bd"],
        "wgs": v["L1_ffn_Wg_s"], "wus": v["L1_ffn_Wu_s"], "wds": v["L1_ffn_Wd_s"],
        "bgs": v["L1_ffn_bg_s"].reshape(INNER, 1), "bus": v["L1_ffn_bu_s"].reshape(INNER, 1),
        "bds": v["L1_ffn_bd_s"].reshape(D, 1),
    }
    nc = _bacc.Bacc("TRN2", target_bir_lowering=False, num_devices=1)
    arrays, aps = {}, {}
    for name, x in a.items():
        x = _np.ascontiguousarray(x)
        arrays[f"in_{name}"] = x
        aps[name] = nc.dram_tensor(f"in_{name}", x.shape, _mybir.dt.from_np(x.dtype), kind="ExternalInput").ap()
    out = nc.dram_tensor("out", (CHUNKS, P, TILES, D), _mybir.dt.float32, kind="ExternalOutput").ap()
    l0_and_l1_kernel(nc, aps, out)
    r = _run(nc, [arrays], core_ids=[0])
    got = r.results[0]["out"]
    return got.transpose(0, 2, 1, 3).reshape(BATCHES, SEQ, D)
```
